# Optimizing a Trainium2 kernel written in Bass

```python
import numpy as np
import jax
import jax.numpy as jnp

def _softmax(x, axis=-1):
    return jax.nn.softmax(x, axis=axis)

def _gelu(x):
    return jax.nn.gelu(x, approximate=True)

def _silu(x):
    return jax.nn.silu(x)

def _sigmoid(x):
    return jax.nn.sigmoid(x)

def _layernorm(x, axis=-1, eps=1e-05):
    m = jnp.mean(x, axis=axis, keepdims=True)
    v = jnp.var(x, axis=axis, keepdims=True)
    return (x - m) / jnp.sqrt(v + eps)

def _scatter_add(tgt, idx, src, axis=0):
    return tgt.at[idx].add(src)

def _segment_sum(src, seg, n):
    return jax.ops.segment_sum(src, seg, n)
kernel_name = 'mk_vit_tower_cls_d1_tok_img768_r4_a2165b'

def setup_inputs(seed: int=0):
    np.random.seed(seed)
    _w = jnp.asarray

    def _rec_inputs():
        import jax
        import jax.numpy as jnp
        _rk = jax.random.key(seed)
        x = -0.000147625 + 0.999875 * jax.random.normal(jax.random.fold_in(_rk, 1), (64, 3, 224, 224), jnp.float32)
        cls_tok = 0.02 * jax.random.normal(jax.random.fold_in(_rk, 5), (1, 1, 192), jnp.float32)
        return (x, cls_tok)
    x, cls_tok = _rec_inputs()

    def _L0_tok_setup():
        import jax, jax.numpy as jnp
        import numpy as np
        EPS = 1e-15
        CURV = 1.0

        def _expmap0(v, c):
            norm = jnp.linalg.norm(v, axis=-1, keepdims=True)
            sn = jnp.sqrt(c) * jnp.maximum(norm, EPS)
            return jnp.tanh(sn) * v / sn

        def _mobius_add(x, y, c):
            x2 = jnp.sum(x * x, axis=-1, keepdims=True)
            y2 = jnp.sum(y * y, axis=-1, keepdims=True)
            xy = jnp.sum(x * y, axis=-1, keepdims=True)
            num = (1.0 + 2.0 * c * xy + c * y2) * x + (1.0 - c * x2) * y
            den = 1.0 + 2.0 * c * xy + c ** 2 * x2 * y2
            return num / jnp.maximum(den, EPS)

        def _unfold_patches(x, p):
            B, C, H, W = x.shape
            Hp, Wp = (H // p, W // p)
            x = x.reshape(B, C, Hp, p, Wp, p)
            x = x.transpose(0, 2, 4, 1, 3, 5)
            return x.reshape(B, Hp * Wp, C * p * p)
        key = jax.random.key(seed)
        k1, k2, k3 = jax.random.split(key, 3)
        B, C, H, W = (64, 3, 224, 224)
        p, D = (16, 192)
        N = (H // p) ** 2
        x = jax.random.normal(k1, (B, C, H, W), dtype=jnp.float32)
        z = jax.random.normal(k2, (C * p * p, D), dtype=jnp.float32) * (C * p * p) ** (-0.5)
        pos_enc = jax.random.normal(k3, (N, D), dtype=jnp.float32) * 0.02
        return {'x': x, 'z': z, 'pos_enc': pos_enc}
    _L0_tok_all = _L0_tok_setup()
    _L0_tok_in = {k: v for k, v in _L0_tok_all.items() if k in ('z', 'pos_enc')}
    del _L0_tok_all

    def _L0_attn_setup():
        import jax, jax.numpy as jnp
        import numpy as np
        DIM = 192
        NUM_HEADS = 8
        GROUPS = 2
        key = jax.random.key(seed)
        ks = jax.random.split(key, 6)
        B, N, C = (8, 256, DIM)
        x = jax.random.normal(ks[0], (B, N, C), dtype=jnp.float32)
        w_qkv = jax.random.normal(ks[1], (3 * C, C), dtype=jnp.float32) * 0.02
        g_dim = C // GROUPS
        w_g0 = jax.random.normal(ks[2], (3 * g_dim, g_dim), dtype=jnp.float32) * 0.02
        w_g1 = jax.random.normal(ks[3], (3 * g_dim, g_dim), dtype=jnp.float32) * 0.02
        w_proj = jax.random.normal(ks[4], (C, C), dtype=jnp.float32) * 0.02
        b_proj = jax.random.normal(ks[5], (C,), dtype=jnp.float32) * 0.02
        return {'x': x, 'w_qkv': w_qkv, 'w_g0': w_g0, 'w_g1': w_g1, 'w_proj': w_proj, 'b_proj': b_proj}
    _L0_attn_all = _L0_attn_setup()
    _L0_attn_in = {k: v for k, v in _L0_attn_all.items() if k in ('w_qkv', 'w_g0', 'w_g1', 'w_proj', 'b_proj')}
    del _L0_attn_all

    def _L0_ffn_setup():
        import jax, jax.numpy as jnp
        import numpy as np
        E = 128
        I = 464
        IS = 928
        K = 6
        G = 1
        TG = 1
        SCALE = 2.5
        CAP = 192

        def moe_forward(hidden_states, Wg, e_bias, W_gate_up, W_down, Wsg, Wsu, Wsd):
            B, S, H = hidden_states.shape
            x = hidden_states.reshape(-1, H)
            T = x.shape[0]
            logits = x.astype(jnp.float32) @ Wg.T
            sig = jax.nn.sigmoid(logits)
            choice = sig + e_bias[None, :]
            grp = choice.reshape(T, G, E // G)
            group_scores = jax.lax.top_k(grp, 2)[0].sum(-1)
            gidx = jax.lax.top_k(group_scores, TG)[1]
            gmask = jnp.zeros((T, G), jnp.float32).at[jnp.arange(T)[:, None], gidx].set(1.0)
            smask = jnp.repeat(gmask, E // G, axis=1)
            scores_for_choice = jnp.where(smask > 0, choice, 0.0)
            topk_idx = jax.lax.top_k(scores_for_choice, K)[1]
            topk_w = jnp.take_along_axis(sig, topk_idx, axis=1)
            topk_w = topk_w / (topk_w.sum(-1, keepdims=True) + 1e-20)
            topk_w = topk_w * SCALE
            P = T * K
            flat_e = topk_idx.reshape(-1)
            order = jnp.argsort(flat_e)
            se = flat_e[order]
            counts = jax.ops.segment_sum(jnp.ones(P, jnp.int32), flat_e, num_segments=E)
            starts = jnp.cumsum(counts) - counts
            pos = jnp.arange(P) - starts[se]
            buf_idx = jnp.where(pos < CAP, se * CAP + pos, E * CAP)
            tok_of_pair = (order // K).astype(jnp.int32)
            w_of_pair = topk_w.reshape(-1)[order]
            token_buf = jnp.zeros((E * CAP,), jnp.int32).at[buf_idx].set(tok_of_pair, mode='drop')
            w_buf = jnp.zeros((E * CAP,), x.dtype).at[buf_idx].set(w_of_pair.astype(x.dtype), mode='drop')
            xb = x[token_buf].reshape(E, CAP, H)
            gu = jnp.einsum('ech,ehf->ecf', xb, W_gate_up)
            g, u = jnp.split(gu, 2, axis=-1)
            inter = jax.nn.silu(g) * u
            yb = jnp.einsum('eci,eih->ech', inter, W_down)
            yb = yb * w_buf.reshape(E, CAP, 1)
            routed = jnp.zeros((T, H), x.dtype).at[token_buf].add(yb.reshape(E * CAP, H))
            shared = jax.nn.silu(x @ Wsg) * (x @ Wsu) @ Wsd
            return (routed + shared).reshape(B, S, H)
        key = jax.random.key(seed)
        ks = jax.random.split(key, 8)
        B, S, H = (1, 512, 192)
        sc = 0.02
        return {'hidden_states': jax.random.normal(ks[0], (B, S, H), jnp.float32), 'Wg': jax.random.normal(ks[1], (E, H), jnp.float32) * sc, 'e_bias': jnp.zeros((E,), jnp.float32), 'W_gate_up': jax.random.normal(ks[2], (E, H, 2 * I), jnp.float32) * sc, 'W_down': jax.random.normal(ks[3], (E, I, H), jnp.float32) * sc, 'Wsg': jax.random.normal(ks[4], (H, IS), jnp.float32) * sc, 'Wsu': jax.random.normal(ks[5], (H, IS), jnp.float32) * sc, 'Wsd': jax.random.normal(ks[6], (IS, H), jnp.float32) * sc}
    _L0_ffn_all = _L0_ffn_setup()
    _L0_ffn_in = {k: v for k, v in _L0_ffn_all.items() if k in ('Wg', 'e_bias', 'W_gate_up', 'W_down', 'Wsg', 'Wsu', 'Wsd')}
    del _L0_ffn_all
    return {'x': x, 'cls_tok': cls_tok, 'L0_tok_z': _L0_tok_in['z'], 'L0_tok_pos_enc': _L0_tok_in['pos_enc'], 'L0_attn_w_qkv': _L0_attn_in['w_qkv'], 'L0_attn_w_g0': _L0_attn_in['w_g0'], 'L0_attn_w_g1': _L0_attn_in['w_g1'], 'L0_attn_w_proj': _L0_attn_in['w_proj'], 'L0_attn_b_proj': _L0_attn_in['b_proj'], 'L0_ffn_Wg': _L0_ffn_in['Wg'], 'L0_ffn_e_bias': _L0_ffn_in['e_bias'], 'L0_ffn_W_gate_up': _L0_ffn_in['W_gate_up'], 'L0_ffn_W_down': _L0_ffn_in['W_down'], 'L0_ffn_Wsg': _L0_ffn_in['Wsg'], 'L0_ffn_Wsu': _L0_ffn_in['Wsu'], 'L0_ffn_Wsd': _L0_ffn_in['Wsd']}

def reference(x, cls_tok, L0_tok_z, L0_tok_pos_enc, L0_attn_w_qkv, L0_attn_w_g0, L0_attn_w_g1, L0_attn_w_proj, L0_attn_b_proj, L0_ffn_Wg, L0_ffn_e_bias, L0_ffn_W_gate_up, L0_ffn_W_down, L0_ffn_Wsg, L0_ffn_Wsu, L0_ffn_Wsd):
    import jax
    import jax.numpy as jnp

    def _L0_tok_ref(x, z, pos_enc):
        import jax, jax.numpy as jnp
        import numpy as np
        EPS = 1e-15
        CURV = 1.0

        def _expmap0(v, c):
            norm = jnp.linalg.norm(v, axis=-1, keepdims=True)
            sn = jnp.sqrt(c) * jnp.maximum(norm, EPS)
            return jnp.tanh(sn) * v / sn

        def _mobius_add(x, y, c):
            x2 = jnp.sum(x * x, axis=-1, keepdims=True)
            y2 = jnp.sum(y * y, axis=-1, keepdims=True)
            xy = jnp.sum(x * y, axis=-1, keepdims=True)
            num = (1.0 + 2.0 * c * xy + c * y2) * x + (1.0 - c * x2) * y
            den = 1.0 + 2.0 * c * xy + c ** 2 * x2 * y2
            return num / jnp.maximum(den, EPS)

        def _unfold_patches(x, p):
            B, C, H, W = x.shape
            Hp, Wp = (H // p, W // p)
            x = x.reshape(B, C, Hp, p, Wp, p)
            x = x.transpose(0, 2, 4, 1, 3, 5)
            return x.reshape(B, Hp * Wp, C * p * p)
        p = 16
        patches = _unfold_patches(x, p)
        v = jnp.einsum('bnf,fd->bnd', patches, z)
        h = _expmap0(v, CURV)
        pos = _expmap0(pos_enc, CURV)
        out = _mobius_add(h, pos[None, :, :], CURV)
        return out

    def _L0_attn_ref(x, w_qkv, w_g0, w_g1, w_proj, b_proj):
        import jax, jax.numpy as jnp
        import numpy as np
        DIM = 192
        NUM_HEADS = 8
        GROUPS = 2
        B, N, C = x.shape
        H = NUM_HEADS
        hd = C // H
        scale = hd ** (-0.5)
        g = GROUPS
        g_dim = C // g
        qkv = (x @ w_qkv.T).reshape(B, N, 3, H, hd)
        qkv = jnp.transpose(qkv, (2, 0, 3, 1, 4))
        q, k, v = (qkv[0], qkv[1], qkv[2])
        attn = jax.nn.softmax(jnp.einsum('bhnd,bhmd->bhnm', q, k) * scale, axis=-1)
        origin = jnp.einsum('bhnm,bhmd->bhnd', attn, v)
        origin = origin.swapaxes(1, 2).reshape(B, N, g, g_dim)
        xg = x.reshape(B, N, g, g_dim)
        head_x = jnp.zeros((B, N, g_dim), dtype=x.dtype)
        outputs = []
        for i, w in enumerate([w_g0, w_g1]):
            cur = xg[:, :, i] + head_x
            qkv2 = (cur @ w.T).reshape(B, N, 3, g_dim)
            q2, k2, v2 = (qkv2[:, :, 0], qkv2[:, :, 1], qkv2[:, :, 2])
            a2 = jax.nn.softmax(jnp.einsum('bnd,bmd->bnm', q2, k2) * scale, axis=-1)
            head_x = jnp.einsum('bnm,bmd->bnd', a2, v2)
            outputs.append(head_x + origin[:, :, i])
        out = jnp.concatenate(outputs, axis=-1)
        return out @ w_proj.T + b_proj

    def _L0_ffn_ref(hidden_states, Wg, e_bias, W_gate_up, W_down, Wsg, Wsu, Wsd):
        import jax, jax.numpy as jnp
        import numpy as np
        E = 128
        I = 464
        IS = 928
        K = 6
        G = 1
        TG = 1
        SCALE = 2.5
        CAP = 192

        def moe_forward(hidden_states, Wg, e_bias, W_gate_up, W_down, Wsg, Wsu, Wsd):
            B, S, H = hidden_states.shape
            x = hidden_states.reshape(-1, H)
            T = x.shape[0]
            logits = x.astype(jnp.float32) @ Wg.T
            sig = jax.nn.sigmoid(logits)
            choice = sig + e_bias[None, :]
            grp = choice.reshape(T, G, E // G)
            group_scores = jax.lax.top_k(grp, 2)[0].sum(-1)
            gidx = jax.lax.top_k(group_scores, TG)[1]
            gmask = jnp.zeros((T, G), jnp.float32).at[jnp.arange(T)[:, None], gidx].set(1.0)
            smask = jnp.repeat(gmask, E // G, axis=1)
            scores_for_choice = jnp.where(smask > 0, choice, 0.0)
            topk_idx = jax.lax.top_k(scores_for_choice, K)[1]
            topk_w = jnp.take_along_axis(sig, topk_idx, axis=1)
            topk_w = topk_w / (topk_w.sum(-1, keepdims=True) + 1e-20)
            topk_w = topk_w * SCALE
            P = T * K
            flat_e = topk_idx.reshape(-1)
            order = jnp.argsort(flat_e)
            se = flat_e[order]
            counts = jax.ops.segment_sum(jnp.ones(P, jnp.int32), flat_e, num_segments=E)
            starts = jnp.cumsum(counts) - counts
            pos = jnp.arange(P) - starts[se]
            buf_idx = jnp.where(pos < CAP, se * CAP + pos, E * CAP)
            tok_of_pair = (order // K).astype(jnp.int32)
            w_of_pair = topk_w.reshape(-1)[order]
            token_buf = jnp.zeros((E * CAP,), jnp.int32).at[buf_idx].set(tok_of_pair, mode='drop')
            w_buf = jnp.zeros((E * CAP,), x.dtype).at[buf_idx].set(w_of_pair.astype(x.dtype), mode='drop')
            xb = x[token_buf].reshape(E, CAP, H)
            gu = jnp.einsum('ech,ehf->ecf', xb, W_gate_up)
            g, u = jnp.split(gu, 2, axis=-1)
            inter = jax.nn.silu(g) * u
            yb = jnp.einsum('eci,eih->ech', inter, W_down)
            yb = yb * w_buf.reshape(E, CAP, 1)
            routed = jnp.zeros((T, H), x.dtype).at[token_buf].add(yb.reshape(E * CAP, H))
            shared = jax.nn.silu(x @ Wsg) * (x @ Wsu) @ Wsd
            return (routed + shared).reshape(B, S, H)
        return moe_forward(hidden_states, Wg, e_bias, W_gate_up, W_down, Wsg, Wsu, Wsd)
    h = _L0_tok_ref(x, L0_tok_z, L0_tok_pos_enc)
    h = jnp.concatenate([jnp.broadcast_to(cls_tok, (h.shape[0], 1, h.shape[2])), h], axis=1)
    h = h + _L0_attn_ref(_layernorm(h, axis=-1), L0_attn_w_qkv, L0_attn_w_g0, L0_attn_w_g1, L0_attn_w_proj, L0_attn_b_proj)
    h = h + _L0_ffn_ref(_layernorm(h, axis=-1), L0_ffn_Wg, L0_ffn_e_bias, L0_ffn_W_gate_up, L0_ffn_W_down, L0_ffn_Wsg, L0_ffn_Wsu, L0_ffn_Wsd)
    return h

_drawn_inputs = setup_inputs


def setup_inputs(seed=0):
    import zlib

    import numpy as np

    out = dict(_drawn_inputs(seed))
    spreads = {'L0_ffn_e_bias': (0.0, 0.1)}
    factors = {}
    for name, (base, spread) in spreads.items():
        noise = np.random.default_rng([zlib.crc32(name.encode()), seed]).standard_normal(out[name].shape)
        drawn = base * np.exp(spread * noise) if base else spread * noise
        out[name] = jnp.asarray(drawn.astype(out[name].dtype))
    for name, factor in factors.items():
        out[name] = (out[name] * factor).astype(out[name].dtype)
    return out
```

```python
import concourse.bass as bass
from concourse import mybir
from contextlib import ExitStack

IMAGES, CHANNELS, SIDE, PATCH = 64, 3, 224, 16
GRID = SIDE // PATCH
PATCHES = GRID * GRID
TOKENS = PATCHES + 1
DIM = 192
HALF = DIM // 2
HEADS, HEAD_DIM, HEAD_PAD = 8, 24, 32
SCALE = float(HEAD_DIM) ** -0.5
ROWS = 99
PADDED = 2 * ROWS
FEATURES = CHANNELS * PATCH * PATCH
FCHUNKS = FEATURES // 128
TILE_IMAGES = 8
TILES = IMAGES // TILE_IMAGES
TROWS = TILE_IMAGES * GRID
EXPERTS, TOP, CAP, EHID = 128, 6, 192, 464
ECHUNK, ECHUNKS = 116, 4
SHID, SCHUNKS = 928, 8
ROUTE_SCALE = 2.5
SLOTS = EXPERTS * CAP
XCOLS = DIM + EXPERTS + 1
NTOK = IMAGES * TOKENS
SINK = NTOK
SLOT_TOP = 32768.0
UNITS = HEADS + 2
G0, G1 = 0, 5
UNIT_HEAD = {n: h for h, n in enumerate(n for n in range(UNITS) if n not in (G0, G1))}
FF_SLOT = 2

fp32 = mybir.dt.float32
bf16 = mybir.dt.bfloat16
u32 = mybir.dt.uint32
ALU = mybir.AluOpType
ACT = mybir.ActivationFunctionType
AX = mybir.AxisListType


class Steps:

    def __init__(self, engine, sem, base=0):
        self.engine, self.sem, self.base, self.n = engine, sem, base, 0

    def link(self, ins, carrier=None):
        self.n += 1
        ins.then_inc(self.sem, 1)
        self.engine.wait_ge(self.sem, self.base + self.n)
        if carrier is not None:
            self.engine.sem_inc(carrier, 1)


def need(engine, sem, value):
    if isinstance(value, int) and value <= 0:
        return
    engine.wait_ge(sem, value)


def embed(nc, PS, t, x, cls_tok, z, pos_enc, w_qkv, w_g0, w_g1, w_proj, b_proj, Wg, e_bias,
          Wsg, Wsu, Wsd, hseq, xdisp, out):
    ctx = ExitStack()

    def sb(name, shape, dt=fp32):
        return ctx.enter_context(nc.sbuf_tensor(name, shape, dt))

    def sem(name):
        return ctx.enter_context(nc.semaphore(name))

    ximg = sb("ximg", [TROWS, 2, CHANNELS, PATCH * SIDE])
    prow = sb("prow", [TROWS, 2, FEATURES])
    patchT = sb("patchT", [128, 2, FCHUNKS, TROWS])
    zw = sb("zw", [128, FCHUNKS, DIM])
    vbuf = sb("vbuf", [TROWS, 2, GRID, DIM])
    hbuf = sb("hbuf", [TROWS, GRID, DIM])
    pos = sb("pos", [TROWS, GRID, DIM])
    prods = sb("prods", [TROWS, 2, 2, 2, DIM])
    y2 = sb("y2", [TROWS, GRID])
    sums = sb("sums", [TROWS, 2, 2, GRID])
    norm = sb("norm", [TROWS, GRID])
    th = sb("th", [TROWS, GRID])
    s = sb("s", [TROWS, GRID])
    x2 = sb("x2", [TROWS, GRID])
    xy = sb("xy", [TROWS, GRID])
    num = sb("num", [TROWS, GRID])
    den = sb("den", [TROWS, GRID])
    alpha = sb("alpha", [TROWS, GRID])
    beta = sb("beta", [TROWS, GRID])
    halfp = sb("halfp", [TROWS, GRID])
    minus1 = sb("minus1", [TROWS, GRID])
    empty = sb("empty", [HALF, 2, XCOLS])
    n_qkv = sb("n_qkv", [HALF, 6, DIM])
    n_g = sb("n_g", [HALF, 2, 3, HALF])
    n_p = sb("n_p", [HALF, 2, DIM])
    n_gate = sb("n_gate", [EXPERTS, DIM])

    zero_set = sem("zero_set")
    ident_set = sem("ident_set")
    empty_set = sem("empty_set")
    w_loaded = sem("w_loaded")
    z_loaded = sem("z_loaded")
    w_kept = sem("w_kept")
    pos_loaded = sem("pos_loaded")
    w_turned = sem("w_turned")
    w_copied = sem("w_copied")
    x_loaded = [sem(f"x_loaded{p}") for p in range(2)]
    rows_sb = sem("rows_sb")
    left_ps = sem("left_ps")
    right_ps = sem("right_ps")
    left_sb = sem("left_sb")
    right_sb = sem("right_sb")
    v_ps = sem("v_ps")
    v_sb = sem("v_sb")
    v_prod = sem("v_prod")
    v_dot = sem("v_dot")
    tanh_in = sem("tanh_in")
    tanh_out = sem("tanh_out")
    h_sb = sem("h_sb")
    h_stored = sem("h_stored")
    filled = sem("filled")
    pchain = sem("a_pchain")
    carrier = sem("a_carrier")
    pos_ready = sem("pos_ready")

    xsrc = x.rearrange("b c (g p) w -> b g c (p w)", p=PATCH)
    hdst = hseq.rearrange("(i r g) d -> i r (g d)", g=GRID, r=TROWS)
    UNIT = GRID
    turn = []
    for k in range(6):
        src = [n_qkv[:, k, c * HALF:(c + 1) * HALF] for c in range(2)]
        if k < 4:
            w = t["wq"] if k < 2 else t["wk"]
            dst = [w[:, c, k % 2, :, 0:HEAD_DIM] for c in range(2)]
        else:
            dst = [t["wv"][:, c, (k - 4) * HALF:(k - 3) * HALF] for c in range(2)]
        turn.append((src, dst, SCALE if k < 2 else 1.0, HALF))
    for g in range(2):
        for part in range(3):
            turn.append(([n_g[:, g, part, :]], [t["wg"][:, g, part, :]], SCALE if part == 0 else 1.0, HALF))
    for k in range(2):
        turn.append(([n_p[:, k, c * HALF:(c + 1) * HALF] for c in range(2)],
                     [t["wp"][:, c, k * HALF:(k + 1) * HALF] for c in range(2)], 1.0, HALF))
    turn.append(([n_gate[:, c * HALF:(c + 1) * HALF] for c in range(2)],
                 [t["wgate"][:, c, :] for c in range(2)], 1.0, EXPERTS))
    W_LOADS, W_KEPT = 5, 5

    with nc.Block() as block:

        @block.sync
        def _(sp):
            sp.dma_start(n_qkv[:], w_qkv.rearrange("(k p) c -> p k c", p=HALF)).then_inc(w_loaded, 16)
            sp.dma_start(n_g[:, 0], w_g0.rearrange("(k p) c -> p k c", p=HALF)).then_inc(w_loaded, 16)
            sp.dma_start(n_g[:, 1], w_g1.rearrange("(k p) c -> p k c", p=HALF)).then_inc(w_loaded, 16)
            sp.dma_start(n_p[:], w_proj.rearrange("(k p) c -> p k c", p=HALF)).then_inc(w_loaded, 16)
            sp.dma_start(n_gate[:], Wg).then_inc(w_loaded, 16)
            sp.dma_start(zw[:], z.rearrange("(k p) d -> p k d", p=128)).then_inc(z_loaded, 16)
            for b in range(TILE_IMAGES):
                sp.dma_start(pos[b * GRID:(b + 1) * GRID].rearrange("g w d -> g (w d)"),
                             pos_enc.rearrange("(g w) d -> g (w d)", w=GRID)).then_inc(pos_loaded, 16)

            def load(tile, par):
                for b in range(TILE_IMAGES):
                    sp.dma_start(ximg[b * GRID:(b + 1) * GRID, par],
                                 xsrc[bass.ds(tile * TILE_IMAGES + b, 1)].rearrange("b g c f -> (b g) c f")
                                 ).then_inc(x_loaded[par], 16)

            load(0, 0)
            load(1, 1)
            sp.dma_start(t["wsg"][:], Wsg.rearrange("(c p) f -> p c f", p=HALF)).then_inc(w_kept, 16)
            sp.dma_start(t["wsu"][:], Wsu.rearrange("(c p) f -> p c f", p=HALF)).then_inc(w_kept, 16)
            sp.dma_start(t["wsd"][:], Wsd.rearrange("(j p) d -> p j d", p=ECHUNK)).then_inc(w_kept, 16)
            sp.dma_start(t["bproj"][:], b_proj.rearrange("(a d) -> a d", a=1).broadcast_to([ROWS, DIM])
                         ).then_inc(w_kept, 16)
            sp.dma_start(t["ebias"][:], e_bias.rearrange("(a d) -> a d", a=1).broadcast_to([ROWS, EXPERTS])
                         ).then_inc(w_kept, 16)
            sp.wait_ge(empty_set, 1)
            for half in range(2):
                dst = xdisp.rearrange("(e t p) c -> t p e c", t=2, p=HALF)[half]
                sp.dma_start(dst, empty[:, half:half + 1, :].broadcast_to([HALF, EXPERTS, XCOLS])
                             ).then_inc(filled, 16)
            sp.dma_start(out[SINK:SINK + CAP].rearrange("(t p) d -> p t d", t=2),
                         empty[:, :, 0:DIM]).then_inc(filled, 16)
            with sp.Fori(0, TILES // 2 - 1) as k:
                for par in range(2):
                    sp.wait_ge(rows_sb, UNIT * (2 * k + par + 1))
                    load(2 * k + 2 + par, par)
            sp.wait_ge(w_kept, 16 * W_KEPT)
            sp.wait_ge(filled, 48)

        @block.gpsimd
        def _(pool):
            chain = Steps(pool, pchain)
            nc.gpsimd.memset(t["ident"][:], 0.0).then_inc(zero_set, 1)
            nc.gpsimd.memset(halfp[:], 0.5).then_inc(zero_set, 1)
            nc.gpsimd.memset(minus1[:], -1.0).then_inc(zero_set, 1)
            nc.gpsimd.memset(t["tri"][:], 1.0).then_inc(zero_set, 1)
            nc.gpsimd.memset(t["ones"][:], 1.0).then_inc(zero_set, 1)
            nc.gpsimd.memset(empty[:], 0.0).then_inc(zero_set, 1)
            nc.gpsimd.memset(t["mhalf"][:], -0.5).then_inc(zero_set, 1)
            nc.gpsimd.memset(t["wq"][:], 0.0).then_inc(zero_set, 1)
            nc.gpsimd.memset(t["wk"][:], 0.0).then_inc(zero_set, 1)
            pool.wait_ge(zero_set, 9)
            nc.gpsimd.affine_select(out=t["ident"][:], in_=t["ident"][:], compare_op=ALU.not_equal, fill=1.0,
                                    base=0, pattern=[[-1, 128]], channel_multiplier=1).then_inc(ident_set, 1)
            nc.gpsimd.affine_select(out=t["tri"][:], in_=t["tri"][:], compare_op=ALU.is_gt, fill=0.0,
                                    base=0, pattern=[[1, ROWS]], channel_multiplier=-1)
            nc.gpsimd.iota(empty[:, :, XCOLS - 1:XCOLS].rearrange("p t c -> p (t c)"), [[HALF, 2]], base=SINK,
                           channel_multiplier=1, allow_small_or_imprecise_dtypes=True).then_inc(empty_set, 1)
            nc.gpsimd.iota(t["rbase"][:], [[-CAP, EXPERTS]], base=int(SLOT_TOP), channel_multiplier=0,
                           allow_small_or_imprecise_dtypes=True)
            chain.link(nc.gpsimd.iota(t["tid"][:], [[ROWS, 2]], base=0, channel_multiplier=1,
                                      allow_small_or_imprecise_dtypes=True))

            pool.wait_ge(v_dot, 1)
            chain.link(nc.gpsimd.tensor_tensor(norm[:], y2[:], halfp[:], ALU.pow))
            nc.gpsimd.tensor_scalar(norm[:], norm[:], 1e-15, None, ALU.max).then_inc(tanh_in, 1)
            pool.wait_ge(tanh_in, 1)
            chain.link(nc.gpsimd.tensor_tensor(x2[:], norm[:], minus1[:], ALU.pow))
            pool.wait_ge(tanh_out, 1)
            chain.link(nc.gpsimd.tensor_tensor(s[:], th[:], x2[:], ALU.mult))
            for w in range(GRID):
                last = nc.gpsimd.tensor_scalar(pos[:, w], pos[:, w], s[:, w:w + 1], None, ALU.mult)
            last.then_inc(pos_ready, 1)
            first = chain.n

            def tile(tl, par, base):
                step = Steps(pool, pchain, base)
                link = step.link
                a, v = sums[:, par, 0], sums[:, par, 1]
                pool.wait_ge(v_dot, 2 + UNIT // 2 * (tl + 1))
                link(nc.gpsimd.tensor_tensor(norm[:], a, halfp[:], ALU.pow), carrier)
                nc.gpsimd.tensor_scalar(norm[:], norm[:], 1e-15, None, ALU.max).then_inc(tanh_in, 1)
                pool.wait_ge(tanh_in, tl + 2)
                link(nc.gpsimd.tensor_tensor(s[:], norm[:], minus1[:], ALU.pow))
                pool.wait_ge(tanh_out, tl + 2)
                link(nc.gpsimd.tensor_tensor(s[:], th[:], s[:], ALU.mult))
                link(nc.gpsimd.tensor_tensor(x2[:], s[:], s[:], ALU.mult))
                link(nc.gpsimd.tensor_tensor(x2[:], x2[:], a, ALU.mult))
                link(nc.gpsimd.tensor_tensor(xy[:], s[:], v, ALU.mult), carrier)
                link(nc.gpsimd.tensor_scalar(xy[:], xy[:], 2.0, 1.0, ALU.mult, ALU.add))
                link(nc.gpsimd.tensor_tensor(num[:], xy[:], y2[:], ALU.add))
                link(nc.gpsimd.tensor_tensor(den[:], x2[:], y2[:], ALU.mult))
                link(nc.gpsimd.tensor_tensor(den[:], den[:], xy[:], ALU.add), carrier)
                link(nc.gpsimd.tensor_scalar(den[:], den[:], 1e-15, None, ALU.max))
                link(nc.gpsimd.tensor_tensor(den[:], den[:], minus1[:], ALU.pow))
                link(nc.gpsimd.tensor_tensor(alpha[:], num[:], s[:], ALU.mult))
                link(nc.gpsimd.tensor_tensor(alpha[:], alpha[:], den[:], ALU.mult), carrier)
                link(nc.gpsimd.tensor_scalar(beta[:], x2[:], -1.0, 1.0, ALU.mult, ALU.add))
                link(nc.gpsimd.tensor_tensor(beta[:], beta[:], den[:], ALU.mult))
                need(pool, h_stored, 16 * tl)
                wide = [TROWS, GRID, DIM]
                nc.gpsimd.tensor_tensor(vbuf[:, par], vbuf[:, par], alpha[:].unsqueeze(2).broadcast_to(wide), ALU.mult)
                link(nc.gpsimd.tensor_tensor(hbuf[:], pos[:], beta[:].unsqueeze(2).broadcast_to(wide), ALU.mult))
                nc.gpsimd.tensor_tensor(hbuf[:], hbuf[:], vbuf[:, par], ALU.add).then_inc(h_sb, 1)
                pool.wait_ge(h_sb, tl + 1)
                pool.sem_inc(carrier, 1)
                nc.gpsimd.dma_start(hdst[bass.ds(tl, 1)].rearrange("i r f -> (i r) f"),
                                    hbuf[:].rearrange("p g d -> p (g d)")).then_inc(h_stored, 16)
                return step.n

            per = tile(0, 0, first)
            assert tile(1, 1, first + per) == per
            with pool.Fori(1, TILES // 2) as k:
                for par in range(2):
                    assert tile(2 * k + par, par, first + per * (2 * k + par)) == per
            pool.wait_ge(h_stored, 16 * TILES)

        @block.tensor
        def _(pe):
            pe.wait_ge(ident_set, 1)
            pe.wait_ge(w_loaded, 16 * W_LOADS)
            for n, (srcs, _, _, k) in enumerate(turn):
                need(pe, w_copied, n - 1)
                for m, src in enumerate(srcs):
                    last = nc.tensor.transpose(PS[0:HALF, 6 + n % 2, m * 128:m * 128 + k], src,
                                               t["ident"][0:k, 0:k])
                last.then_inc(w_turned, 1)
            pe.wait_ge(z_loaded, 16)

            def turns(u, par):
                if isinstance(u, int):
                    need(pe, left_sb, u - 1)
                    need(pe, right_sb, u - 1)
                else:
                    pe.wait_ge(left_sb, u - 1)
                    pe.wait_ge(right_sb, u - 1)
                pe.wait_ge(rows_sb, u + 1)
                w = wloc
                for k in range(FCHUNKS):
                    src = prow[:, w % 2, k * 128:(k + 1) * 128]
                    ins = nc.tensor.transpose(PS[:, 2 * (w % 2) + k // 3, (k % 3) * 128:(k % 3) * 128 + TROWS],
                                              src, t["ident"][0:TROWS, 0:TROWS])
                    if k == 2:
                        ins.then_inc(left_ps, 1)
                ins.then_inc(right_ps, 1)

            def product(u, w):
                pe.wait_ge(left_sb, u + 1)
                pe.wait_ge(right_sb, u + 1)
                if w % 2 == 0:
                    pair = (u - w) // 2 + w // 2 if isinstance(u, int) else u_pair + w // 2
                    need(pe, v_sb, pair - 1)
                bank = 4 + (par_pairs + w // 2) % 2
                for k in range(FCHUNKS):
                    ins = nc.tensor.matmul(PS[0:TROWS, bank, (w % 2) * DIM:(w % 2 + 1) * DIM],
                                           patchT[:, w % 2, k, :], zw[:, k, :], start=(k == 0), stop=(k == FCHUNKS - 1))
                ins.then_inc(v_ps, 1)

            def tile(tl, par):
                nonlocal wloc, u_pair, par_pairs
                u_pair = UNIT // 2 * tl
                par_pairs = par * (UNIT // 2)
                for w in range(GRID):
                    wloc = w
                    turns(UNIT * tl + w, par)
                    if w:
                        product(UNIT * tl + w - 1, w - 1)
                product(UNIT * tl + GRID - 1, GRID - 1)

            wloc = u_pair = par_pairs = 0
            for tl in range(2):
                tile(tl, tl)
            with pe.Fori(1, TILES // 2) as k:
                for par in range(2):
                    tile(2 * k + par, par)

        @block.scalar
        def _(act):
            act.wait_ge(tanh_in, 1)
            nc.scalar.activation(th[:], norm[:], ACT.Tanh).then_inc(tanh_out, 1)

            def pair(tl, par, m):
                act.wait_ge(v_ps, UNIT * tl + 2 * m + 2)
                if m == 0:
                    need(act, h_sb, tl - 1)
                nc.scalar.activation(
                    vbuf[:, par, 2 * m:2 * m + 2].rearrange("p w d -> p (w d)"),
                    PS[0:TROWS, 4 + (par * (UNIT // 2) + m) % 2, 0:2 * DIM], ACT.Copy).then_inc(v_sb, 1)

            def rows(tl, par, w):
                need(act, right_ps, UNIT * tl + w - 1)
                nc.scalar.activation(
                    prow[:, w % 2].rearrange("r (f q) -> r f q", q=PATCH),
                    ximg[:, par].rearrange("r c (p w q) -> r (c p) w q", p=PATCH, w=GRID)[:, :, w, :],
                    ACT.Copy).then_inc(rows_sb, 1)

            def tile(tl, par, half_of):
                act.wait_ge(x_loaded[par], 16 * TILE_IMAGES * (half_of + 1))
                rows(tl, par, 0)
                for w in range(GRID):
                    if w + 1 < GRID:
                        rows(tl, par, w + 1)
                    act.wait_ge(left_ps, UNIT * tl + w + 1)
                    nc.scalar.activation(
                        patchT[:, w % 2, 0:3, :],
                        PS[:, 2 * (w % 2), 0:384].rearrange("p (k r) -> p k r", k=3)[:, :, 0:TROWS],
                        ACT.Copy).then_inc(left_sb, 1)
                    if w and w % 2 == 0:
                        pair(tl, par, w // 2 - 1)
                pair(tl, par, GRID // 2 - 1)
                act.wait_ge(tanh_in, tl + 2)
                nc.scalar.activation(th[:], norm[:], ACT.Tanh).then_inc(tanh_out, 1)

            for tl in range(2):
                tile(tl, tl, 0)
            with act.Fori(1, TILES // 2) as k:
                for par in range(2):
                    tile(2 * k + par, par, k)

        @block.vector
        def _(dve):
            dve.wait_ge(zero_set, 9)
            for n, (_, dsts, scale, k) in enumerate(turn):
                dve.wait_ge(w_turned, n + 1)
                for m, dst in enumerate(dsts):
                    src = PS[0:HALF, 6 + n % 2, m * 128:m * 128 + k]
                    if len(dst.shape) == 3:
                        src = src.rearrange("p (h d) -> p h d", d=HEAD_DIM)
                    last = nc.vector.tensor_scalar(dst, src, scale, None, ALU.mult)
                last.then_inc(w_copied, 1)
            dve.wait_ge(pos_loaded, 16 * TILE_IMAGES)
            for turn_of in range(2):
                if turn_of:
                    dve.wait_ge(pos_ready, 1)
                nc.vector.tensor_tensor(hbuf[:], pos[:], pos[:], ALU.mult).then_inc(v_prod, 1)
                dve.wait_ge(v_prod, turn_of + 1)
                nc.vector.tensor_reduce(y2[:], hbuf[:], AX.X, ALU.add).then_inc(v_dot, 1)

            def dots(tl, par, m):
                dve.wait_ge(v_sb, UNIT // 2 * tl + m + 1)
                v = vbuf[:, par, 2 * m:2 * m + 2]
                nc.vector.tensor_tensor(prods[:, m % 2, 0], v, v, ALU.mult)
                nc.vector.tensor_tensor(prods[:, m % 2, 1], v, pos[:, 2 * m:2 * m + 2], ALU.mult).then_inc(v_prod, 1)

            def sum_up(tl, par, m):
                dve.wait_ge(v_prod, 2 + UNIT // 2 * tl + m + 1)
                nc.vector.tensor_reduce(sums[:, par, :, 2 * m:2 * m + 2], prods[:, m % 2], AX.X, ALU.add).then_inc(v_dot, 1)

            def tile(tl, par):
                for w in range(GRID):
                    dve.wait_ge(right_ps, UNIT * tl + w + 1)
                    nc.vector.tensor_copy(
                        patchT[:, w % 2, 3:6, :],
                        PS[:, 2 * (w % 2) + 1, 0:384].rearrange("p (k r) -> p k r", k=3)[:, :, 0:TROWS]
                    ).then_inc(right_sb, 1)
                    if w > 2 and w % 2 == 1:
                        dots(tl, par, w // 2 - 1)
                    if w > 2 and w % 2 == 0:
                        sum_up(tl, par, w // 2 - 2)
                sum_up(tl, par, GRID // 2 - 2)
                dots(tl, par, GRID // 2 - 1)
                sum_up(tl, par, GRID // 2 - 1)

            for tl in range(2):
                tile(tl, tl)
            with dve.Fori(1, TILES // 2) as k:
                for par in range(2):
                    tile(2 * k + par, par)

    ctx.close()


def layer(nc, PS, t, cls_tok, hseq, xdisp, out):
    ctx = ExitStack()

    def sb(name, shape, dt=fp32):
        return ctx.enter_context(nc.sbuf_tensor(name, shape, dt))

    def sem(name):
        return ctx.enter_context(nc.semaphore(name))

    hin = sb("hin", [ROWS, 2, 2, DIM])
    hb = sb("hb", [ROWS, 2, 2, DIM])
    stats1 = sb("stats1", [ROWS, 2, 6])
    mv1 = sb("mv1", [ROWS, 2, 2])
    ve1 = sb("ve1", [ROWS, 2])
    rstd1 = sb("rstd1", [ROWS, 2])
    xn = sb("xn", [ROWS, 2, DIM])
    xT = sb("xT", [HALF, 2, PADDED])
    qT = sb("qT", [128, 2, PADDED])
    kT = sb("kT", [128, 2, PADDED])
    vn = sb("vn", [ROWS, 2, DIM])
    gqk = sb("gqk", [HALF, 2, PADDED])
    gv = sb("gv", [ROWS, 2, HALF])
    cur = sb("cur", [HALF, PADDED])
    nmax = sb("nmax", [ROWS, 2, 2])
    prob = sb("prob", [ROWS, 2, 2, PADDED])
    probT = sb("probT", [ROWS, 2, 2, PADDED])
    sum_h = sb("sum_h", [ROWS, 2, HEADS])
    inv_h = sb("inv_h", [ROWS, 2, HEADS])
    sum_g = sb("sum_g", [ROWS, 2, 2])
    inv_g = sb("inv_g", [ROWS, 2, 2])
    hxT = sb("hxT", [HALF, 2, PADDED])
    heads = sb("heads", [ROWS, 2, DIM])
    yT = sb("yT", [HALF, 2, PADDED])
    h2 = sb("h2", [ROWS, 2, DIM])
    stats2 = sb("stats2", [ROWS, 2, 6])
    mv2 = sb("mv2", [ROWS, 2, 2])
    ve2 = sb("ve2", [ROWS, 2])
    rstd2 = sb("rstd2", [ROWS, 2])
    xrow = sb("xrow", [ROWS, 2, 2, XCOLS])
    x2T = sb("x2T", [HALF, 2, PADDED])
    tanh = sb("tanh", [ECHUNK, 2, PADDED])
    gated = sb("gated", [ECHUNK, 2, PADDED])
    inter = sb("inter", [ECHUNK, SCHUNKS, PADDED])
    obuf = sb("obuf", [ROWS, 2, 2, DIM])
    elog = sb("elog", [ROWS, 2, EXPERTS])
    sig = sb("sig", [ROWS, 2, EXPERTS])
    choice = sb("choice", [ROWS, 2, EXPERTS + 2])
    struck = sb("struck", [ROWS, 2, EXPERTS + 2])
    top = sb("top", [ROWS, 2, 8])
    mask = sb("mask", [ROWS, 2, EXPERTS], bf16)
    wraw = sb("wraw", [ROWS, 2, EXPERTS])
    wsum = sb("wsum", [ROWS, 2])
    winv = sb("winv", [ROWS, 2])
    place = sb("place", [ROWS, 2, EXPERTS])
    fits = sb("fits", [ROWS, 2, EXPERTS])
    code = sb("code", [ROWS, 2, EXPERTS])
    best = sb("best", [ROWS, 2, 8])
    slot = sb("slot", [ROWS, 2, 2, 8], u32)
    taken = sb("taken", [ROWS, EXPERTS])

    ready = sem("b_ready")
    h_loaded = [sem(f"h_loaded{p}") for p in range(2)]
    cls_in = sem("cls_in")
    ve1_ready = sem("ve1_ready")
    rstd1_ready = sem("rstd1_ready")
    xn_ready = sem("xn_ready")
    xt_ps, xt_ready = sem("xt_ps"), sem("xt_ready")
    q_ps, q_ready = sem("q_ps"), sem("q_ready")
    k_ps, k_ready = sem("k_ps"), sem("k_ready")
    vv_ps, vv_ready = sem("vv_ps"), sem("vv_ready")
    gqk_ps, gqk_ready = sem("gqk_ps"), sem("gqk_ready")
    gv_ps, gv_ready = sem("gv_ps"), sem("gv_ready")
    s_ps = sem("s_ps")
    max_ready = sem("max_ready")
    p_ready = sem("p_ready")
    pn_ready = sem("pn_ready")
    t_ps = sem("t_ps")
    t_ready = sem("t_ready")
    hx_ps, hx_ready = sem("hx_ps"), sem("hx_ready")
    heads_ps, heads_ready = sem("heads_ps"), sem("heads_ready")
    ot_ps, yt_ready = sem("ot_ps"), sem("yt_ready")
    proj_ps, h2_ready = sem("proj_ps"), sem("h2_ready")
    ve2_ready, rstd2_ready = sem("ve2_ready"), sem("rstd2_ready")
    xn2_ready = sem("xn2_ready")
    x2t_ps, x2t_ready = sem("x2t_ps"), sem("x2t_ready")
    logit_ps, elog_ready = sem("logit_ps"), sem("elog_ready")
    mask_ready = sem("mask_ready")
    count_ps, count_used = sem("count_ps"), sem("count_used")
    slot_ready = sem("slot_ready")
    ff_ps, tanh_ready, inter_ready = sem("ff_ps"), sem("tanh_ready"), sem("inter_ready")
    down_ps, out_ready = sem("down_ps"), sem("out_ready")
    sent = [sem(f"sent{p}") for p in range(2)]
    stored = [sem(f"stored{p}") for p in range(2)]
    c_norm, c_att, c_ffn = sem("c_norm"), sem("c_att"), sem("c_ffn")
    carrier = sem("b_carrier")
    N_NORM, N_ATT, N_FFN = 2, 3, 25

    def tiles(bank, rows, width, used=None):
        return PS[0:rows, bank, 0:2 * width].rearrange("p (t k) -> p t k", t=2)[:, :, 0:used or width]

    def both(ap):
        return ap.unsqueeze(1).broadcast_to([ap.shape[0], 2, ap.shape[1]])

    def head_at(n):
        h = UNIT_HEAD[n]
        return h, h // 4, (h % 4) * HEAD_PAD

    def steps(engine, step):
        step(0, 0, 0, True, False)
        for s in range(1, 4):
            step(s, s // 2, s % 2, True, True)
        with engine.Fori(2, IMAGES // 2 - 1) as k:
            for par in range(2):
                step(2 * k + par, k, par, True, True)
        step(IMAGES - 2, IMAGES // 2 - 1, 0, True, True)
        step(IMAGES - 1, IMAGES // 2 - 1, 1, True, True, last=True)
        step(IMAGES, IMAGES // 2, 0, False, True)

    with nc.Block() as block:

        @block.sync
        def _(sp):
            sp.wait_ge(ready, 6)
            for p in range(2):
                sp.dma_start(hin[0:1, p, 0, :], cls_tok).then_inc(cls_in, 16)

            def load(image, p):
                src = image * PATCHES
                sp.dma_start(hin[1:ROWS, p, 0, :], hseq[bass.ds(src, ROWS - 1), :]).then_inc(h_loaded[p], 16)
                sp.dma_start(hin[0:ROWS - 1, p, 1, :], hseq[bass.ds(src + ROWS - 1, ROWS - 1), :]
                             ).then_inc(h_loaded[p], 16)

            def store(f, p):
                sp.wait_ge(out_ready, f + 1)
                sp.dma_start(out[bass.ds(f * TOKENS, ROWS), :], obuf[:, p, 0, :]).then_inc(stored[p], 16)
                sp.dma_start(out[bass.ds(f * TOKENS + ROWS, ROWS - 1), :], obuf[0:ROWS - 1, p, 1, :]
                             ).then_inc(stored[p], 16)

            load(0, 0)
            load(1, 1)

            def step(s, half, par, att, ffn, last=False):
                if att and not (isinstance(s, int) and s >= IMAGES - 2):
                    sp.wait_ge(xn_ready, s + 1)
                    load(s + 2, par)
                if ffn:
                    store(s - 1, 1 - par)

            steps(sp, step)
            for p in range(2):
                sp.wait_ge(stored[p], 32 * (IMAGES // 2))

        @block.gpsimd
        def _(pool):
            nc.gpsimd.memset(hin[:], 0.0).then_inc(ready, 1)
            nc.gpsimd.memset(prob[:], 0.0).then_inc(ready, 1)
            nc.gpsimd.memset(choice[:], 1e30).then_inc(ready, 1)
            nc.gpsimd.memset(taken[:], 0.0).then_inc(ready, 1)
            nc.gpsimd.memset(xrow[:], 0.0).then_inc(ready, 1)
            nc.gpsimd.memset(obuf[:], 0.0).then_inc(ready, 1)

            def norm1(a):
                pool.wait_ge(ve1_ready, a + 1)
                nc.gpsimd.tensor_tensor(rstd1[:], ve1[:], t["mhalf"][:], ALU.pow).then_inc(rstd1_ready, 1)

            def dispatch(f, p):
                pool.wait_ge(slot_ready, f + 1)
                pool.sem_inc(carrier, 1)
                for tile in range(2):
                    rows = ROWS - tile
                    for k in range(TOP):
                        nc.gpsimd.indirect_dma_start(
                            xdisp[:, :], bass.IndirectOffsetOnAxis(slot[0:rows, p, tile, k:k + 1], 0),
                            xrow[0:rows, p, tile, :], None, bounds_check=SLOTS - 1, oob_is_err=False
                        ).then_inc(sent[p], 16)

            norm1(0)

            def step(s, half, par, att, ffn, last=False):
                if ffn:
                    pool.wait_ge(ve2_ready, s)
                    nc.gpsimd.tensor_tensor(rstd2[:], ve2[:], t["mhalf"][:], ALU.pow).then_inc(rstd2_ready, 1)
                    if not (isinstance(s, int) and s < 2):
                        dispatch(s - 2, par)
                if att and not last:
                    norm1(s + 1)

            steps(pool, step)
            dispatch(IMAGES - 1, 1)
            for p in range(2):
                pool.wait_ge(sent[p], 16 * 2 * TOP * (IMAGES // 2))

        @block.tensor
        def _(pe):
            mm, turn, ident = nc.tensor.matmul, nc.tensor.transpose, t["ident"]

            def product(dst, pairs):
                for n, (l, r) in enumerate(pairs):
                    ins = mm(dst, l, r, start=(n == 0), stop=(n == len(pairs) - 1))
                return ins

            def cols(src, tile):
                return src[:, tile * ROWS:(tile + 1) * ROWS]

            def turn_rows(bank, src):
                for c in range(2):
                    for tile in range(2):
                        ins = turn(PS[0:HALF, bank, c * PADDED + tile * ROWS:c * PADDED + (tile + 1) * ROWS],
                                   src[:, tile, c * HALF:(c + 1) * HALF], ident[0:ROWS, 0:ROWS])
                return ins

            def group_qk(bank, g, src):
                for part in range(2):
                    ins = product(PS[0:HALF, bank, part * PADDED:(part + 1) * PADDED],
                                  [(t["wg"][:, g, part, :], src)])
                ins.then_inc(gqk_ps, 1)

            def group_v(bank, g, src):
                for tile in range(2):
                    ins = product(PS[0:ROWS, bank, tile * HALF:(tile + 1) * HALF],
                                  [(cols(src, tile), t["wg"][:, g, 2, :])])
                ins.then_inc(gv_ps, 1)

            def scores(s, n):
                if n >= 2:
                    pe.wait_ge(p_ready, UNITS * s + n - 1)
                elif n == 1:
                    pe.wait_ge(k_ready, s + 1)
                if n in (G0, G1):
                    pe.wait_ge(gqk_ready, 2 * s + 1 + (n == G1))
                    if n == G0:
                        pe.wait_ge(q_ready, s + 1)
                    q, k = gqk[:, 0, :], gqk[:, 1, :]
                else:
                    _, blk, at = head_at(n)
                    q, k = qT[at:at + HEAD_PAD, blk, :], kT[at:at + HEAD_PAD, blk, :]
                for tile in range(2):
                    ins = mm(PS[0:ROWS, n % 2, tile * PADDED:(tile + 1) * PADDED], cols(q, tile), k,
                             start=True, stop=True)
                ins.then_inc(s_ps, 1)

            def turn_probs(s, n):
                if n in (G0, G1):
                    pe.wait_ge(pn_ready, 2 * s + 1 + (n == G1))
                else:
                    pe.wait_ge(p_ready, UNITS * s + n + 1)
                if n == 0:
                    pe.wait_ge(vv_ready, s + 1)
                for kt in range(2):
                    for tile in range(2):
                        ins = turn(PS[0:ROWS, 2 + n % 2, kt * PADDED + tile * ROWS:kt * PADDED + (tile + 1) * ROWS],
                                   cols(prob[:, n % 2, tile, :], kt), ident[0:ROWS, 0:ROWS])
                ins.then_inc(t_ps, 1)

            def values(s, n):
                pe.wait_ge(t_ready, UNITS * s + n + 1)
                if n in (G0, G1):
                    g = int(n == G1)
                    pe.wait_ge(gv_ready, 2 * s + 1 + g)
                    product(PS[0:HALF, 7, 0:PADDED], [(gv[:, kt, :], probT[:, n % 2, kt, :]) for kt in range(2)]
                            ).then_inc(hx_ps, 1)
                    return
                h = UNIT_HEAD[n]
                if h == 0:
                    need(pe, h2_ready, s)
                for tile in range(2):
                    ins = product(PS[0:ROWS, 4, tile * DIM + h * HEAD_DIM:tile * DIM + (h + 1) * HEAD_DIM],
                                  [(cols(probT[:, n % 2, kt, :], tile), vn[:, kt, h * HEAD_DIM:(h + 1) * HEAD_DIM])
                                   for kt in range(2)])
                if h == HEADS - 1:
                    ins.then_inc(heads_ps, 1)

            def ffn_chunk(s, j):
                if j >= 2:
                    pe.wait_ge(inter_ready, SCHUNKS * (s - 1) + j - 1)
                elif j == 1:
                    pe.wait_ge(elog_ready, s)
                for half, w in enumerate((t["wsg"], t["wsu"])):
                    ins = product(PS[0:ECHUNK, 5 + j % 2, half * PADDED:(half + 1) * PADDED],
                                  [(w[:, c, j * ECHUNK:(j + 1) * ECHUNK], x2T[:, c, :]) for c in range(2)])
                ins.then_inc(ff_ps, 1)

            def step(s, half, par, att, ffn, last=False):
                if att:
                    pe.wait_ge(xn_ready, s + 1)
                    need(pe, hx_ready, 2 * s)
                    turn_rows(7, xn).then_inc(xt_ps, 1)
                if ffn:
                    pe.wait_ge(heads_ready, s)
                    need(pe, out_ready, s - 1)
                    turn_rows(6, heads).then_inc(ot_ps, 1)
                if att:
                    pe.wait_ge(xt_ready, s + 1)
                    need(pe, p_ready, UNITS * s)
                    for blk in range(2):
                        ins = product(PS[:, 0, blk * PADDED:(blk + 1) * PADDED],
                                      [(t["wq"][:, c, blk].rearrange("p h d -> p (h d)"), xT[:, c, :]) for c in range(2)])
                    ins.then_inc(q_ps, 1)
                    for blk in range(2):
                        ins = product(PS[:, 1, blk * PADDED:(blk + 1) * PADDED],
                                      [(t["wk"][:, c, blk].rearrange("p h d -> p (h d)"), xT[:, c, :]) for c in range(2)])
                    ins.then_inc(k_ps, 1)
                if ffn:
                    pe.wait_ge(yt_ready, s)
                    for tile in range(2):
                        ins = product(PS[0:ROWS, 4, tile * DIM:(tile + 1) * DIM],
                                      [(cols(yT[:, c, :], tile), t["wp"][:, c, :]) for c in range(2)])
                    ins.then_inc(proj_ps, 1)
                if att:
                    need(pe, t_ready, UNITS * s)
                    for tile in range(2):
                        ins = product(PS[0:ROWS, 2, tile * DIM:(tile + 1) * DIM],
                                      [(cols(xT[:, c, :], tile), t["wv"][:, c, :]) for c in range(2)])
                    ins.then_inc(vv_ps, 1)
                    group_qk(3, 0, xT[:, 0, :])
                    group_v(7, 0, xT[:, 0, :])
                for n in range(UNITS + 2):
                    if att and n < UNITS:
                        scores(s, n)
                    if ffn:
                        if n == 1:
                            pe.wait_ge(xn2_ready, s)
                            need(pe, count_used, s - 1)
                            turn_rows(5, xrow[:, 1 - par]).then_inc(x2t_ps, 1)
                        if n == FF_SLOT:
                            pe.wait_ge(x2t_ready, s)
                            for tile in range(2):
                                ins = product(PS[0:ROWS, 6, tile * EXPERTS:(tile + 1) * EXPERTS],
                                              [(cols(x2T[:, c, :], tile), t["wgate"][:, c, :]) for c in range(2)])
                            ins.then_inc(logit_ps, 1)
                        if FF_SLOT <= n < FF_SLOT + SCHUNKS:
                            ffn_chunk(s, n - FF_SLOT)
                    if att and 1 <= n <= UNITS:
                        turn_probs(s, n - 1)
                    if att and n == 3:
                        pe.wait_ge(hx_ready, 2 * s + 1)
                        group_qk(7, 1, cur[:])
                    if att and n == 4:
                        pe.wait_ge(gqk_ready, 2 * s + 2)
                        group_v(7, 1, cur[:])
                    if att and n >= 2:
                        values(s, n - 2)
                    if ffn and n == UNITS:
                        pe.wait_ge(mask_ready, s)
                        pe.wait_ge(inter_ready, SCHUNKS * s - 1)
                        tri, ones = t["tri"], t["ones"]
                        first, second = mask[:, 0, :], mask[0:ROWS - 1, 1, :]
                        product(PS[0:ROWS, 5, 0:EXPERTS], [(tri[:], first)])
                        product(PS[0:ROWS, 5, EXPERTS:2 * EXPERTS], [(ones[:], first), (tri[0:ROWS - 1, :], second)])
                        product(PS[0:ROWS, 5, 2 * EXPERTS:3 * EXPERTS],
                                [(ones[:], first), (ones[0:ROWS - 1, :], second)]).then_inc(count_ps, 1)
                if ffn:
                    pe.wait_ge(inter_ready, SCHUNKS * s)
                    for tile in range(2):
                        ins = product(PS[0:ROWS, 6, tile * DIM:(tile + 1) * DIM],
                                      [(cols(inter[:, j, :], tile), t["wsd"][:, j, :]) for j in range(SCHUNKS)])
                    ins.then_inc(down_ps, 1)

            steps(pe, step)

        @block.scalar
        def _(act):
            act.wait_ge(ready, 6)

            def copy(dst, src):
                return nc.scalar.activation(dst, src, ACT.Copy)

            def step(s, half, par, att, ffn, last=False):
                if att:
                    act.wait_ge(xt_ps, s + 1)
                    copy(xT[:], tiles(7, HALF, PADDED)).then_inc(xt_ready, 1)
                    act.wait_ge(q_ps, s + 1)
                    copy(qT[:], tiles(0, 128, PADDED)).then_inc(q_ready, 1)
                    act.wait_ge(vv_ps, s + 1)
                    copy(vn[:], tiles(2, ROWS, DIM)).then_inc(vv_ready, 1)
                    act.wait_ge(gv_ps, 2 * s + 1)
                    copy(gv[:], tiles(7, ROWS, HALF)).then_inc(gv_ready, 1)
                for n in range(UNITS + 2):
                    if att and n < UNITS:
                        act.wait_ge(max_ready, UNITS * s + n + 1)
                        for tile in range(2):
                            if n in (G0, G1):
                                acc = sum_g[:, tile, int(n == G1):int(n == G1) + 1]
                            else:
                                acc = sum_h[:, tile, UNIT_HEAD[n]:UNIT_HEAD[n] + 1]
                            ins = nc.scalar.activation(prob[:, n % 2, tile, 0:TOKENS],
                                                       tiles(n % 2, ROWS, PADDED, TOKENS)[:, tile, :], ACT.Exp,
                                                       bias=nmax[:, n % 2, tile:tile + 1], accum_out=acc)
                        ins.then_inc(p_ready, 1)
                    if ffn and n == FF_SLOT:
                        act.wait_ge(logit_ps, s)
                        nc.scalar.activation(elog[:], tiles(6, ROWS, EXPERTS), ACT.Exp, scale=-1.0
                                             ).then_inc(elog_ready, 1)
                    if ffn and FF_SLOT <= n < FF_SLOT + SCHUNKS:
                        j = n - FF_SLOT
                        act.wait_ge(ff_ps, SCHUNKS * (s - 1) + j + 1)
                        nc.scalar.activation(tanh[:, j % 2, :], PS[0:ECHUNK, 5 + j % 2, 0:PADDED], ACT.Tanh,
                                             scale=0.5).then_inc(tanh_ready, 1)
                    if att and 1 <= n <= UNITS:
                        act.wait_ge(t_ps, UNITS * s + n)
                        copy(probT[:, (n - 1) % 2], tiles(2 + (n - 1) % 2, ROWS, PADDED)).then_inc(t_ready, 1)
                    if att and n == 5:
                        act.wait_ge(gv_ps, 2 * s + 2)
                        copy(gv[:], tiles(7, ROWS, HALF)).then_inc(gv_ready, 1)

            steps(act, step)

        @block.vector
        def _(dve):
            V = nc.vector
            dve.wait_ge(ready, 6)
            dve.wait_ge(cls_in, 32)

            def stats(chain, src, st, mv, ve, done):
                for tile in range(2):
                    last = V.bn_stats(st[:, tile], src[:, tile])
                chain.link(last, carrier)
                for tile in range(2):
                    last = V.bn_aggr(mv[:, tile], st[:, tile])
                chain.link(last)
                V.tensor_scalar(ve[:], mv[:, :, 1], 1e-5, None, ALU.add).then_inc(done, 1)

            def norm1_stats(a, half, p):
                chain = Steps(dve, c_norm, N_NORM * a)
                dve.wait_ge(h_loaded[p], 32 * (half + 1))
                V.tensor_tensor(hb[:, p], hin[:, p], both(t["bproj"][:]), ALU.add)
                stats(chain, hin[:, p], stats1, mv1, ve1, ve1_ready)
                return chain

            def norm1_apply(a, p, chain):
                dve.wait_ge(rstd1_ready, a + 1)
                need(dve, xt_ps, a)
                for tile in range(2):
                    last = V.tensor_scalar(xn[:, tile], hin[:, p, tile], mv1[:, tile, 0:1], rstd1[:, tile:tile + 1],
                                           ALU.subtract, ALU.mult)
                last.then_inc(xn_ready, 1)
                assert chain.n == N_NORM

            def normalise(s, n):
                g = int(n == G1)
                dve.wait_ge(p_ready, UNITS * s + n + 1)
                chain_att.link(V.reciprocal(inv_g[:, :, g], sum_g[:, :, g]))
                p = prob[:, n % 2, :, 0:TOKENS]
                V.tensor_tensor(p, p, inv_g[:, :, g:g + 1].broadcast_to([ROWS, 2, TOKENS]), ALU.mult
                                ).then_inc(pn_ready, 1)

            def gate(s, j):
                bank = 5 + j % 2
                g, u = PS[0:ECHUNK, bank, 0:PADDED], PS[0:ECHUNK, bank, PADDED:2 * PADDED]
                dve.wait_ge(tanh_ready, SCHUNKS * (s - 1) + j + 1)
                ffn_chain.link(V.scalar_tensor_tensor(gated[:, j % 2, :], tanh[:, j % 2, :], 1.0, g, ALU.add, ALU.mult))
                V.tensor_tensor(inter[:, j, :], gated[:, j % 2, :], u, ALU.mult).then_inc(inter_ready, 1)

            def choose(s):
                link = ffn_chain.link
                dve.wait_ge(elog_ready, s)
                link(V.tensor_scalar(elog[:], elog[:], 1.0, None, ALU.add))
                link(V.reciprocal(sig[:], elog[:]))
                link(V.tensor_tensor(choice[:, :, 0:EXPERTS], sig[:], both(t["ebias"][:]), ALU.add), carrier)
                V.max(top[:, 0], choice[:, 0])
                link(V.max(top[:, 1], choice[:, 1]), carrier)
                V.match_replace(struck[:, 0], top[:, 0], choice[:, 0], -1e30)
                link(V.match_replace(struck[:, 1], top[:, 1], choice[:, 1], -1e30))
                V.tensor_scalar(mask[:], struck[:, :, 0:EXPERTS], -1e29, None, ALU.is_lt).then_inc(mask_ready, 1)

            def weigh(s, p):
                link = ffn_chain.link
                dve.wait_ge(mask_ready, s)
                link(V.tensor_tensor(wraw[:], sig[:], mask[:], ALU.mult))
                link(V.tensor_reduce(wsum[:], wraw[:], AX.X, ALU.add))
                link(V.tensor_scalar(wsum[:], wsum[:], 1e-20, None, ALU.add))
                link(V.reciprocal(winv[:], wsum[:]))
                for tile in range(2):
                    V.tensor_scalar(xrow[:, p, tile, DIM:DIM + EXPERTS], wraw[:, tile], winv[:, tile:tile + 1],
                                    ROUTE_SCALE, ALU.mult, ALU.mult)
                link(V.tensor_copy(xrow[:, p, :, XCOLS - 1], t["tid"][:]))
                link(V.tensor_scalar(t["tid"][:], t["tid"][:], float(TOKENS), None, ALU.add))

            def place_tokens(s):
                link = ffn_chain.link
                dve.wait_ge(count_ps, s)
                link(V.tensor_tensor(place[:], tiles(5, ROWS, EXPERTS), both(taken[:]), ALU.add))
                V.tensor_tensor(taken[:], taken[:], PS[0:ROWS, 5, 2 * EXPERTS:3 * EXPERTS], ALU.add
                                ).then_inc(count_used, 1)
                dve.wait_ge(count_used, s)
                V.scalar_tensor_tensor(fits[:], place[:], float(CAP), mask[:], ALU.is_lt, ALU.mult)
                link(V.tensor_tensor(code[:], both(t["rbase"][:]), place[:], ALU.subtract))
                link(V.tensor_tensor(code[:], code[:], fits[:], ALU.mult), carrier)
                V.max(best[:, 0], code[:, 0])
                link(V.max(best[:, 1], code[:, 1]))
                V.tensor_scalar(slot[:, parf], best[:], -1.0, SLOT_TOP, ALU.mult, ALU.add).then_inc(slot_ready, 1)

            ffn_chain = chain_att = parf = None

            def step(s, half, par, att, ffn, last=False):
                nonlocal ffn_chain, chain_att, parf
                parf = 1 - par
                half_f = half if par else half - 1
                ffn_chain = Steps(dve, c_ffn, N_FFN * (s - 1))
                chain_att = Steps(dve, c_att, N_ATT * s)
                if ffn:
                    dve.wait_ge(ot_ps, s)
                    V.tensor_tensor(yT[:], tiles(6, HALF, PADDED), hxT[:], ALU.add).then_inc(yt_ready, 1)
                if att:
                    dve.wait_ge(k_ps, s + 1)
                    V.tensor_copy(kT[:], tiles(1, 128, PADDED)).then_inc(k_ready, 1)
                if ffn:
                    dve.wait_ge(proj_ps, s)
                    V.tensor_tensor(h2[:], tiles(4, ROWS, DIM), hb[:, parf], ALU.add).then_inc(h2_ready, 1)
                    dve.wait_ge(h2_ready, s)
                    stats(ffn_chain, h2, stats2, mv2, ve2, ve2_ready)
                if att:
                    dve.wait_ge(gqk_ps, 2 * s + 1)
                    V.tensor_copy(gqk[:], tiles(3, HALF, PADDED)).then_inc(gqk_ready, 1)
                for n in range(UNITS + 2):
                    if ffn and FF_SLOT <= n - 1 < FF_SLOT + SCHUNKS:
                        gate(s, n - 1 - FF_SLOT)
                    if att and n < UNITS:
                        dve.wait_ge(s_ps, UNITS * s + n + 1)
                        V.tensor_reduce(nmax[:, n % 2, :], tiles(n % 2, ROWS, PADDED, TOKENS), AX.X, ALU.max,
                                        negate=True).then_inc(max_ready, 1)
                    if att and n - 1 in (G0, G1):
                        normalise(s, n - 1)
                    if ffn and n == 0:
                        dve.wait_ge(rstd2_ready, s)
                        need(dve, sent[parf], 32 * TOP * half_f)
                        for tile in range(2):
                            ins = V.tensor_scalar(xrow[:, parf, tile, 0:DIM], h2[:, tile], mv2[:, tile, 0:1],
                                                  rstd2[:, tile:tile + 1], ALU.subtract, ALU.mult)
                        ins.then_inc(xn2_ready, 1)
                    if ffn and n == 1:
                        dve.wait_ge(x2t_ps, s)
                        V.tensor_copy(x2T[:], tiles(5, HALF, PADDED)).then_inc(x2t_ready, 1)
                    if att and n == 3:
                        dve.wait_ge(hx_ps, 2 * s + 1)
                        V.tensor_copy(hxT[:, 0], PS[0:HALF, 7, 0:PADDED])
                        V.tensor_tensor(cur[:], xT[:, 1], PS[0:HALF, 7, 0:PADDED], ALU.add).then_inc(hx_ready, 1)
                    if att and n == 4:
                        dve.wait_ge(gqk_ps, 2 * s + 2)
                        V.tensor_copy(gqk[:], tiles(7, HALF, PADDED)).then_inc(gqk_ready, 1)
                    if ffn and n == 4:
                        choose(s)
                    if ffn and n == 6:
                        weigh(s, parf)
                    if att and n == 8:
                        dve.wait_ge(hx_ps, 2 * s + 2)
                        V.tensor_copy(hxT[:, 1], PS[0:HALF, 7, 0:PADDED]).then_inc(hx_ready, 1)
                    if att and not last and n == 7:
                        next_norm = norm1_stats(s + 1, half + par, 1 - par)
                    if att and not last and n == 9:
                        norm1_apply(s + 1, 1 - par, next_norm)
                    if ffn and n == UNITS + 1:
                        place_tokens(s)
                if att:
                    dve.wait_ge(p_ready, UNITS * (s + 1))
                    chain_att.link(V.reciprocal(inv_h[:], sum_h[:]))
                    dve.wait_ge(heads_ps, s + 1)
                    V.tensor_tensor(heads[:].rearrange("p t (h d) -> p t h d", d=HEAD_DIM),
                                    tiles(4, ROWS, DIM).rearrange("p t (h d) -> p t h d", d=HEAD_DIM),
                                    inv_h[:].unsqueeze(3).broadcast_to([ROWS, 2, HEADS, HEAD_DIM]), ALU.mult
                                    ).then_inc(heads_ready, 1)
                    assert chain_att.n == N_ATT
                if ffn:
                    dve.wait_ge(down_ps, s)
                    need(dve, stored[parf], 32 * half_f)
                    V.scalar_tensor_tensor(obuf[:, parf], tiles(6, ROWS, DIM), 0.5, h2[:], ALU.mult, ALU.add
                                           ).then_inc(out_ready, 1)
                    assert ffn_chain.n == N_FFN

            norm1_apply(0, 0, norm1_stats(0, 0, 0))
            steps(dve, step)

    ctx.close()


def experts(nc, PS, t, Wgu, Wd, xdisp, out):
    ctx = ExitStack()

    def sb(name, shape, dt=fp32):
        return ctx.enter_context(nc.sbuf_tensor(name, shape, dt))

    def sem(name):
        return ctx.enter_context(nc.semaphore(name))

    wgu = sb("e_wgu", [HALF, 2, 2, 2 * EHID])
    wd = sb("e_wd", [ECHUNK, 2, ECHUNKS, DIM])
    xb = sb("e_xb", [HALF, 2, 2, DIM])
    wt = sb("e_wt", [HALF, 2, 2])
    tok = sb("e_tok", [HALF, 2, 2])
    tokn = sb("e_tokn", [HALF, 2, 2], u32)
    xT = sb("e_xT", [HALF, 2, 2, CAP])
    act_g = sb("e_act", [ECHUNK, 2, 2, CAP])
    inter = sb("e_inter", [ECHUNK, 2, ECHUNKS, CAP])
    yb = sb("e_yb", [HALF, 2, 2, DIM])

    w_in = [sem(f"w_in{p}") for p in range(2)]
    d_in = [sem(f"d_in{p}") for p in range(2)]
    x_in = [sem(f"x_in{p}") for p in range(2)]
    r_in = [sem(f"r_in{p}") for p in range(2)]
    xt_ps, xt_sb = sem("e_xt_ps"), sem("e_xt_sb")
    up_ps = sem("e_up_ps")
    silu_sb, inter_sb = sem("silu_sb"), sem("e_inter_sb")
    y_ps, y_sb = sem("y_ps"), sem("y_sb")
    tok_sb = sem("tok_sb")
    added = sem("added")
    carrier = sem("e_carrier")
    HALVES = 2
    BX, BG, BU, BY = 0, 1, 3, 5

    def steps(engine, step):
        step(0, 0, 0, first=True)
        for e in range(1, 4):
            step(e, e // 2, e % 2)
        with engine.Fori(2, EXPERTS // 2 - 1) as k:
            for par in range(2):
                step(2 * k + par, k, par)
        step(EXPERTS - 2, EXPERTS // 2 - 1, 0)
        step(EXPERTS - 1, EXPERTS // 2 - 1, 1, last=True)

    with nc.Block() as block:

        @block.sync
        def _(sp):
            rows = xdisp.rearrange("(e t p) c -> e p t c", t=2, p=HALF)
            up = Wgu.rearrange("e (c p) f -> e p c f", p=HALF)
            dn = Wd.rearrange("e (j p) d -> e p j d", p=ECHUNK)

            def load_up(e, p):
                sp.dma_start(xb[:, p], rows[bass.ds(e, 1)][:, :, :, 0:DIM].rearrange("e p t c -> (e p) t c")
                             ).then_inc(x_in[p], 16)
                sp.dma_start(wgu[:, p], up[bass.ds(e, 1)].rearrange("e p c f -> (e p) c f")).then_inc(w_in[p], 16)

            def load_down(e, p):
                sp.dma_start(wd[:, p], dn[bass.ds(e, 1)].rearrange("e p j d -> (e p) j d")).then_inc(d_in[p], 16)
                sp.dma_start(wt[:, p], weight_column(e), allow_slow_non_contiguous=True).then_inc(r_in[p], 16)
                sp.dma_start(tok[:, p], rows[bass.ds(e, 1)][:, :, :, XCOLS - 1].rearrange("e p t -> (e p) t"),
                             allow_slow_non_contiguous=True).then_inc(r_in[p], 16)

            def weight_column(e):
                src = xdisp[bass.ds(e * CAP, CAP), :].rearrange("(t p) c -> p t c", p=HALF)
                return src[:, :, bass.ds(DIM + e, 1)].rearrange("p t o -> p (t o)")

            for e in range(2):
                load_up(e, e)
                load_down(e, e)

            def step(e, half, par, first=False, last=False):
                if isinstance(e, int) and e >= EXPERTS - 2:
                    return
                sp.wait_ge(up_ps, 2 * (e + 1))
                load_up(e + 2, par)
                sp.wait_ge(y_sb, e + 1)
                sp.wait_ge(tok_sb, e + 1)
                load_down(e + 2, par)

            steps(sp, step)

        @block.tensor
        def _(pe):
            mm, turn, ident = nc.tensor.matmul, nc.tensor.transpose, t["ident"]

            def turn_slots(e, half, p):
                pe.wait_ge(x_in[p], 16 * (half + 1))
                need(pe, xt_sb, e)
                for c in range(2):
                    for tile in range(2):
                        ins = turn(PS[0:HALF, BX, c * CAP + tile * HALF:c * CAP + (tile + 1) * HALF],
                                   xb[:, p, tile, c * HALF:(c + 1) * HALF], ident[0:HALF, 0:HALF])
                ins.then_inc(xt_ps, 1)

            def up(e, half, p, m):
                if m == 0:
                    pe.wait_ge(w_in[p], 16 * (half + 1))
                    pe.wait_ge(xt_sb, e + 1)
                need(pe, inter_sb, 2 * (e - 1) + m + 1)
                for kind, bank in enumerate((BG + m, BU + m)):
                    for j in range(2):
                        at = kind * EHID + (2 * m + j) * ECHUNK
                        for c in range(2):
                            ins = mm(PS[0:ECHUNK, bank, j * CAP:(j + 1) * CAP], wgu[:, p, c, at:at + ECHUNK],
                                     xT[:, p, c, :], start=(c == 0), stop=(c == 1))
                ins.then_inc(up_ps, 1)

            def down(e, half, p):
                pe.wait_ge(d_in[p], 16 * (half + 1))
                pe.wait_ge(inter_sb, 2 * (e + 1))
                need(pe, y_sb, e)
                for tile in range(2):
                    for j in range(ECHUNKS):
                        ins = mm(PS[0:HALF, BY, tile * DIM:(tile + 1) * DIM],
                                 inter[:, p, j, tile * HALF:(tile + 1) * HALF], wd[:, p, j, :],
                                 start=(j == 0), stop=(j == ECHUNKS - 1))
                ins.then_inc(y_ps, 1)

            def step(e, half, par, first=False, last=False):
                up(e, half, par, 0)
                if not first:
                    down(e - 1, half if par else half - 1, 1 - par)
                if not last:
                    turn_slots(e + 1, half + par, 1 - par)
                up(e, half, par, 1)

            turn_slots(0, 0, 0)
            steps(pe, step)
            down(EXPERTS - 1, EXPERTS // 2 - 1, 1)

        @block.scalar
        def _(act):
            def step(e, half, par, first=False, last=False):
                for m in range(2):
                    act.wait_ge(up_ps, 2 * e + m + 1)
                    nc.scalar.activation(act_g[:, m], PS[0:ECHUNK, BG + m, 0:2 * CAP].rearrange("p (j s) -> p j s", j=2),
                                         ACT.Silu).then_inc(silu_sb, 1)

            steps(act, step)

        @block.vector
        def _(dve):
            V = nc.vector

            def rows_out(e, p):
                dve.wait_ge(xt_ps, e + 1)
                V.tensor_copy(xT[:, p], PS[0:HALF, BX, 0:2 * CAP].rearrange("p (c s) -> p c s", c=2)).then_inc(xt_sb, 1)

            def result(e, half, p):
                dve.wait_ge(y_ps, e + 1)
                dve.wait_ge(r_in[p], 32 * (half + 1))
                need(dve, added, 32 * (e - 1))
                V.tensor_copy(tokn[:, p], tok[:, p]).then_inc(tok_sb, 1)
                V.tensor_tensor(yb[:, p], PS[0:HALF, BY, 0:2 * DIM].rearrange("p (t d) -> p t d", t=2),
                                wt[:, p].unsqueeze(2).broadcast_to([HALF, 2, DIM]), ALU.mult).then_inc(y_sb, 1)

            def step(e, half, par, first=False, last=False):
                def gate(m):
                    dve.wait_ge(silu_sb, 2 * e + m + 1)
                    V.tensor_tensor(inter[:, par, 2 * m:2 * m + 2], act_g[:, m],
                                    PS[0:ECHUNK, BU + m, 0:2 * CAP].rearrange("p (j s) -> p j s", j=2), ALU.mult
                                    ).then_inc(inter_sb, 1)

                gate(0)
                if not first:
                    result(e - 1, half if par else half - 1, 1 - par)
                if not last:
                    rows_out(e + 1, 1 - par)
                gate(1)

            rows_out(0, 0)
            steps(dve, step)
            result(EXPERTS - 1, EXPERTS // 2 - 1, 1)

        @block.gpsimd
        def _(pool):
            def step(e, half, par, first=False, last=False):
                pool.wait_ge(y_sb, e + 1)
                pool.sem_inc(carrier, 1)
                if not first:
                    pool.wait_ge(added, 32 * e)
                    pool.sem_inc(carrier, 1)
                for tile in range(2):
                    nc.gpsimd.indirect_dma_start(
                        out[:, :], bass.IndirectOffsetOnAxis(tokn[:, par, tile:tile + 1], 0), yb[:, par, tile, :],
                        None, bounds_check=NTOK + CAP - 1, oob_is_err=True, compute_op=ALU.add).then_inc(added, 16)

            steps(pool, step)
            pool.wait_ge(added, 32 * EXPERTS)

    ctx.close()


def program(nc, x, cls_tok, z, pos_enc, w_qkv, w_g0, w_g1, w_proj, b_proj, Wg, e_bias, Wgu, Wd, Wsg, Wsu, Wsd, out):
    with ExitStack() as ctx:
        hseq = nc.dram_tensor("hseq", [IMAGES * PATCHES, DIM], fp32, kind="Internal").ap()
        xdisp = nc.dram_tensor("xdisp", [SLOTS, XCOLS], fp32, kind="Internal").ap()
        PS = ctx.enter_context(nc.psum_tensor("PS", [128, 8, 512], fp32))
        shapes = {
            "ident": [128, 128], "rbase": [ROWS, EXPERTS], "tid": [ROWS, 2], "mhalf": [ROWS, 2],
            "wq": [HALF, 2, 2, 4, HEAD_PAD], "wk": [HALF, 2, 2, 4, HEAD_PAD], "wv": [HALF, 2, DIM],
            "wg": [HALF, 2, 3, HALF], "wp": [HALF, 2, DIM], "wgate": [HALF, 2, EXPERTS],
            "wsg": [HALF, 2, SHID], "wsu": [HALF, 2, SHID], "wsd": [ECHUNK, SCHUNKS, DIM],
            "bproj": [ROWS, DIM], "ebias": [ROWS, EXPERTS],
        }
        t = {k: ctx.enter_context(nc.sbuf_tensor(f"k_{k}", v, fp32)) for k, v in shapes.items()}
        t["tri"] = ctx.enter_context(nc.sbuf_tensor("k_tri", [ROWS, ROWS], bf16))
        t["ones"] = ctx.enter_context(nc.sbuf_tensor("k_ones", [ROWS, ROWS], bf16))
        embed(nc, PS, t, x, cls_tok, z, pos_enc, w_qkv, w_g0, w_g1, w_proj, b_proj, Wg, e_bias, Wsg, Wsu, Wsd,
              hseq, xdisp, out)
        layer(nc, PS, t, cls_tok, hseq, xdisp, out)
        experts(nc, PS, t, Wgu, Wd, xdisp, out)


_INS = ["x", "cls_tok", "L0_tok_z", "L0_tok_pos_enc", "L0_attn_w_qkv", "L0_attn_w_g0", "L0_attn_w_g1",
        "L0_attn_w_proj", "L0_attn_b_proj", "L0_ffn_Wg", "L0_ffn_e_bias", "L0_ffn_W_gate_up", "L0_ffn_W_down",
        "L0_ffn_Wsg", "L0_ffn_Wsu", "L0_ffn_Wsd"]


def kernel(**inputs):
    import numpy as _np
    import concourse.bacc as _bacc
    from concourse import mybir as _mybir
    from concourse.bass_utils import run_bass_kernel_spmd as _run

    nc = _bacc.Bacc("TRN2", target_bir_lowering=False, num_devices=1)
    arrays, args = {}, []
    for name in _INS:
        a = _np.ascontiguousarray(inputs[name])
        if name == "cls_tok":
            a = a.reshape(1, DIM)
        arrays[f"in_{name}"] = a
        args.append(nc.dram_tensor(f"in_{name}", a.shape, _mybir.dt.from_np(a.dtype), kind="ExternalInput").ap())
    args.append(nc.dram_tensor("out_h", (NTOK + CAP, DIM), _mybir.dt.float32, kind="ExternalOutput").ap())
    program(nc, *args)
    r = _run(nc, [arrays], core_ids=[0])
    return r.results[0]["out_h"][:NTOK].reshape(IMAGES, TOKENS, DIM)
```

```python
import concourse.bass as bass
from concourse import mybir
from contextlib import ExitStack

IMAGES, CHANNELS, SIDE, PATCH = 64, 3, 224, 16
GRID = SIDE // PATCH
PATCHES = GRID * GRID
TOKENS = PATCHES + 1
DIM = 192
HALF = DIM // 2
HEADS, HEAD_DIM, HEAD_PAD = 8, 24, 32
SCALE = float(HEAD_DIM) ** -0.5
ROWS = 99
PADDED = 2 * ROWS
FEATURES = CHANNELS * PATCH * PATCH
FCHUNKS = FEATURES // 128
TILE_IMAGES = 8
TILES = IMAGES // TILE_IMAGES
TROWS = TILE_IMAGES * GRID
EXPERTS, TOP, CAP, EHID = 128, 6, 192, 464
ECHUNK, ECHUNKS = 116, 4
SHID, SCHUNKS = 928, 8
ROUTE_SCALE = 2.5
SLOTS = EXPERTS * CAP
XCOLS = DIM + EXPERTS + 1
NTOK = IMAGES * TOKENS
SINK = NTOK
SLOT_TOP = 32768.0
UNITS = HEADS + 2
G0, G1 = 0, 5
UNIT_HEAD = {n: h for h, n in enumerate(n for n in range(UNITS) if n not in (G0, G1))}
FF_SLOT = 3

fp32 = mybir.dt.float32
bf16 = mybir.dt.bfloat16
u32 = mybir.dt.uint32
ALU = mybir.AluOpType
ACT = mybir.ActivationFunctionType
AX = mybir.AxisListType


class Steps:

    def __init__(self, engine, sem, base=0):
        self.engine, self.sem, self.base, self.n = engine, sem, base, 0

    def link(self, ins, carrier=None):
        self.wait(self.mark(ins))
        if carrier is not None:
            self.engine.sem_inc(carrier, 1)

    def mark(self, ins):
        self.n += 1
        ins.then_inc(self.sem, 1)
        return self.n

    def wait(self, n):
        self.engine.wait_ge(self.sem, self.base + n)


def need(engine, sem, value):
    if isinstance(value, int) and value <= 0:
        return
    engine.wait_ge(sem, value)


def embed(nc, PS, t, x, cls_tok, z, pos_enc, w_qkv, w_g0, w_g1, w_proj, b_proj, Wg, e_bias,
          Wsg, Wsu, Wsd, hseq, xdisp, out):
    ctx = ExitStack()

    def sb(name, shape, dt=fp32):
        return ctx.enter_context(nc.sbuf_tensor(name, shape, dt))

    def sem(name):
        return ctx.enter_context(nc.semaphore(name))

    ximg = sb("ximg", [TROWS, 2, CHANNELS, PATCH * SIDE])
    prow = sb("prow", [TROWS, 2, FEATURES])
    patchT = sb("patchT", [128, 2, FCHUNKS, TROWS])
    zw = sb("zw", [128, FCHUNKS, DIM])
    vbuf = sb("vbuf", [TROWS, 2, GRID, DIM])
    hbuf = sb("hbuf", [TROWS, GRID, DIM])
    pos = sb("pos", [TROWS, GRID, DIM])
    prods = sb("prods", [TROWS, 2, 2, 2, DIM])
    y2 = sb("y2", [TROWS, GRID])
    sums = sb("sums", [TROWS, 2, 2, GRID])
    norm = sb("norm", [TROWS, GRID])
    th = sb("th", [TROWS, GRID])
    s = sb("s", [TROWS, GRID])
    x2 = sb("x2", [TROWS, GRID])
    xy = sb("xy", [TROWS, GRID])
    num = sb("num", [TROWS, GRID])
    den = sb("den", [TROWS, GRID])
    alpha = sb("alpha", [TROWS, GRID])
    beta = sb("beta", [TROWS, GRID])
    halfp = sb("halfp", [TROWS, GRID])
    minus1 = sb("minus1", [TROWS, GRID])
    empty = sb("empty", [HALF, 2, XCOLS])
    n_qkv = sb("n_qkv", [HALF, 6, 2, 4, HEAD_PAD])
    n_g = sb("n_g", [HALF, 2, 3, 4, HEAD_PAD])
    n_p = sb("n_p", [HALF, 2, 2, 4, HEAD_PAD])
    n_gate = sb("n_gate", [EXPERTS, DIM])

    zero_set = sem("zero_set")
    spread_set = sem("spread_set")
    ident_set = sem("ident_set")
    empty_set = sem("empty_set")
    w_loaded = sem("w_loaded")
    z_loaded = sem("z_loaded")
    w_kept = sem("w_kept")
    pos_loaded = sem("pos_loaded")
    w_turned = sem("w_turned")
    w_copied = sem("w_copied")
    x_loaded = [sem(f"x_loaded{p}") for p in range(2)]
    rows_sb = sem("rows_sb")
    left_ps = sem("left_ps")
    right_ps = sem("right_ps")
    left_sb = sem("left_sb")
    right_sb = sem("right_sb")
    v_ps = sem("v_ps")
    v_sb = sem("v_sb")
    v_prod = sem("v_prod")
    v_dot = sem("v_dot")
    tanh_in = sem("tanh_in")
    tanh_out = sem("tanh_out")
    h_sb = sem("h_sb")
    h_stored = sem("h_stored")
    filled = sem("filled")
    pchain = sem("a_pchain")
    carrier = sem("a_carrier")
    pos_ready = sem("pos_ready")

    xsrc = x.rearrange("b c (g p) w -> b g c (p w)", p=PATCH)
    hdst = hseq.rearrange("(i r g) d -> i r (g d)", g=GRID, r=TROWS)
    UNIT = GRID
    turn = []
    def spread(ap):
        return ap.rearrange("p h d -> p (h d)")

    for k in range(6):
        src = [spread(n_qkv[:, k, c]) for c in range(2)]
        if k < 4:
            w = t["wq"] if k < 2 else t["wk"]
            dst = [w[:, c, k % 2, :, 0:HEAD_DIM] for c in range(2)]
        else:
            dst = [t["wv"][:, c, (k - 4) * HALF:(k - 3) * HALF] for c in range(2)]
        turn.append((src, dst, SCALE if k < 2 else 1.0, HALF))
    for g in range(2):
        for part in range(3):
            turn.append(([spread(n_g[:, g, part])], [t["wg"][:, g, part, :]], SCALE if part == 0 else 1.0, HALF))
    for k in range(2):
        turn.append(([spread(n_p[:, k, c]) for c in range(2)],
                     [t["wp"][:, c, k * HALF:(k + 1) * HALF] for c in range(2)], 1.0, HALF))
    turn.append(([n_gate[:, c * HALF:(c + 1) * HALF] for c in range(2)],
                 [t["wgate"][:, c, :] for c in range(2)], 1.0, EXPERTS))
    W_LOADS, W_KEPT = 15, 5

    with nc.Block() as block:

        @block.sync
        def _(sp):
            sp.wait_ge(spread_set, 3)
            for k in range(6):
                sp.dma_start(n_qkv[:, k].rearrange("p c h d -> p (c h) d")[:, :, 0:HEAD_DIM],
                             w_qkv[k * HALF:(k + 1) * HALF].rearrange("p (h d) -> p h d", d=HEAD_DIM)
                             ).then_inc(w_loaded, 16)
            for g, w in enumerate((w_g0, w_g1)):
                for k in range(3):
                    sp.dma_start(n_g[:, g, k, :, 0:HEAD_DIM],
                                 w[k * HALF:(k + 1) * HALF].rearrange("p (h d) -> p h d", d=HEAD_DIM)
                                 ).then_inc(w_loaded, 16)
            for k in range(2):
                sp.dma_start(n_p[:, k].rearrange("p c h d -> p (c h) d")[:, :, 0:HEAD_DIM],
                             w_proj[k * HALF:(k + 1) * HALF].rearrange("p (h d) -> p h d", d=HEAD_DIM)
                             ).then_inc(w_loaded, 16)
            sp.dma_start(n_gate[:], Wg).then_inc(w_loaded, 16)
            sp.dma_start(zw[:], z.rearrange("(k p) d -> p k d", p=128)).then_inc(z_loaded, 16)
            for b in range(TILE_IMAGES):
                sp.dma_start(pos[b * GRID:(b + 1) * GRID].rearrange("g w d -> g (w d)"),
                             pos_enc.rearrange("(g w) d -> g (w d)", w=GRID)).then_inc(pos_loaded, 16)

            def load(tile, par):
                for b in range(TILE_IMAGES):
                    sp.dma_start(ximg[b * GRID:(b + 1) * GRID, par],
                                 xsrc[bass.ds(tile * TILE_IMAGES + b, 1)].rearrange("b g c f -> (b g) c f")
                                 ).then_inc(x_loaded[par], 16)

            load(0, 0)
            load(1, 1)
            sp.dma_start(t["wsg"][:], Wsg.rearrange("(c p) f -> p c f", p=HALF)).then_inc(w_kept, 16)
            sp.dma_start(t["wsu"][:], Wsu.rearrange("(c p) f -> p c f", p=HALF)).then_inc(w_kept, 16)
            sp.dma_start(t["wsd"][:], Wsd.rearrange("(j p) d -> p j d", p=ECHUNK)).then_inc(w_kept, 16)
            sp.dma_start(t["bproj"][:], b_proj.rearrange("(a d) -> a d", a=1).broadcast_to([ROWS, DIM])
                         ).then_inc(w_kept, 16)
            sp.dma_start(t["ebias"][:], e_bias.rearrange("(a d) -> a d", a=1).broadcast_to([ROWS, EXPERTS])
                         ).then_inc(w_kept, 16)
            sp.wait_ge(empty_set, 1)
            for half in range(2):
                dst = xdisp.rearrange("(e t p) c -> t p e c", t=2, p=HALF)[half]
                sp.dma_start(dst, empty[:, half:half + 1, :].broadcast_to([HALF, EXPERTS, XCOLS])
                             ).then_inc(filled, 16)
            sp.dma_start(out[SINK:SINK + CAP].rearrange("(t p) d -> p t d", t=2),
                         empty[:, :, 0:DIM]).then_inc(filled, 16)
            with sp.Fori(0, TILES // 2 - 1) as k:
                for par in range(2):
                    sp.wait_ge(rows_sb, UNIT * (2 * k + par + 1))
                    load(2 * k + 2 + par, par)
            sp.wait_ge(w_kept, 16 * W_KEPT)
            sp.wait_ge(filled, 48)

        @block.gpsimd
        def _(pool):
            chain = Steps(pool, pchain)
            for w in (n_qkv, n_g, n_p):
                nc.gpsimd.memset(w[:], 0.0).then_inc(spread_set, 1)
            nc.gpsimd.memset(t["ident"][:], 0.0).then_inc(zero_set, 1)
            nc.gpsimd.memset(halfp[:], 0.5).then_inc(zero_set, 1)
            nc.gpsimd.memset(minus1[:], -1.0).then_inc(zero_set, 1)
            nc.gpsimd.memset(t["tri"][:], 1.0).then_inc(zero_set, 1)
            nc.gpsimd.memset(t["ones"][:], 1.0).then_inc(zero_set, 1)
            nc.gpsimd.memset(empty[:], 0.0).then_inc(zero_set, 1)
            nc.gpsimd.memset(t["mhalf"][:], -0.5).then_inc(zero_set, 1)
            nc.gpsimd.memset(t["wq"][:], 0.0).then_inc(zero_set, 1)
            nc.gpsimd.memset(t["wk"][:], 0.0).then_inc(zero_set, 1)
            pool.wait_ge(zero_set, 9)
            nc.gpsimd.affine_select(out=t["ident"][:], in_=t["ident"][:], compare_op=ALU.not_equal, fill=1.0,
                                    base=0, pattern=[[-1, 128]], channel_multiplier=1).then_inc(ident_set, 1)
            nc.gpsimd.affine_select(out=t["tri"][:], in_=t["tri"][:], compare_op=ALU.is_gt, fill=0.0,
                                    base=0, pattern=[[1, ROWS]], channel_multiplier=-1)
            nc.gpsimd.iota(empty[:, :, XCOLS - 1:XCOLS].rearrange("p t c -> p (t c)"), [[HALF, 2]], base=SINK,
                           channel_multiplier=1, allow_small_or_imprecise_dtypes=True).then_inc(empty_set, 1)
            nc.gpsimd.iota(t["rbase"][:], [[-CAP, EXPERTS]], base=int(SLOT_TOP), channel_multiplier=0,
                           allow_small_or_imprecise_dtypes=True)
            chain.link(nc.gpsimd.iota(t["tid"][:], [[ROWS, 2]], base=0, channel_multiplier=1,
                                      allow_small_or_imprecise_dtypes=True))

            pool.wait_ge(v_dot, 1)
            chain.link(nc.gpsimd.tensor_tensor(norm[:], y2[:], halfp[:], ALU.pow))
            nc.gpsimd.tensor_scalar(norm[:], norm[:], 1e-15, None, ALU.max).then_inc(tanh_in, 1)
            pool.wait_ge(tanh_in, 1)
            chain.link(nc.gpsimd.tensor_tensor(x2[:], norm[:], minus1[:], ALU.pow))
            pool.wait_ge(tanh_out, 1)
            chain.link(nc.gpsimd.tensor_tensor(s[:], th[:], x2[:], ALU.mult))
            for w in range(GRID):
                last = nc.gpsimd.tensor_scalar(pos[:, w], pos[:, w], s[:, w:w + 1], None, ALU.mult)
            last.then_inc(pos_ready, 1)
            first = chain.n

            def tile(tl, par, base):
                step = Steps(pool, pchain, base)
                link = step.link
                a, v = sums[:, par, 0], sums[:, par, 1]
                pool.wait_ge(v_dot, 2 + UNIT // 2 * (tl + 1))
                link(nc.gpsimd.tensor_tensor(norm[:], a, halfp[:], ALU.pow), carrier)
                nc.gpsimd.tensor_scalar(norm[:], norm[:], 1e-15, None, ALU.max).then_inc(tanh_in, 1)
                pool.wait_ge(tanh_in, tl + 2)
                link(nc.gpsimd.tensor_tensor(s[:], norm[:], minus1[:], ALU.pow))
                pool.wait_ge(tanh_out, tl + 2)
                link(nc.gpsimd.tensor_tensor(s[:], th[:], s[:], ALU.mult))
                link(nc.gpsimd.tensor_tensor(x2[:], s[:], s[:], ALU.mult))
                link(nc.gpsimd.tensor_tensor(x2[:], x2[:], a, ALU.mult))
                link(nc.gpsimd.tensor_tensor(xy[:], s[:], v, ALU.mult), carrier)
                link(nc.gpsimd.tensor_scalar(xy[:], xy[:], 2.0, 1.0, ALU.mult, ALU.add))
                link(nc.gpsimd.tensor_tensor(num[:], xy[:], y2[:], ALU.add))
                link(nc.gpsimd.tensor_tensor(den[:], x2[:], y2[:], ALU.mult))
                link(nc.gpsimd.tensor_tensor(den[:], den[:], xy[:], ALU.add), carrier)
                link(nc.gpsimd.tensor_scalar(den[:], den[:], 1e-15, None, ALU.max))
                link(nc.gpsimd.tensor_tensor(den[:], den[:], minus1[:], ALU.pow))
                link(nc.gpsimd.tensor_tensor(alpha[:], num[:], s[:], ALU.mult))
                link(nc.gpsimd.tensor_tensor(alpha[:], alpha[:], den[:], ALU.mult), carrier)
                link(nc.gpsimd.tensor_scalar(beta[:], x2[:], -1.0, 1.0, ALU.mult, ALU.add))
                link(nc.gpsimd.tensor_tensor(beta[:], beta[:], den[:], ALU.mult))
                need(pool, h_stored, 16 * tl)
                wide = [TROWS, GRID, DIM]
                nc.gpsimd.tensor_tensor(vbuf[:, par], vbuf[:, par], alpha[:].unsqueeze(2).broadcast_to(wide), ALU.mult)
                link(nc.gpsimd.tensor_tensor(hbuf[:], pos[:], beta[:].unsqueeze(2).broadcast_to(wide), ALU.mult))
                nc.gpsimd.tensor_tensor(hbuf[:], hbuf[:], vbuf[:, par], ALU.add).then_inc(h_sb, 1)
                pool.wait_ge(h_sb, tl + 1)
                pool.sem_inc(carrier, 1)
                nc.gpsimd.dma_start(hdst[bass.ds(tl, 1)].rearrange("i r f -> (i r) f"),
                                    hbuf[:].rearrange("p g d -> p (g d)")).then_inc(h_stored, 16)
                return step.n

            per = tile(0, 0, first)
            assert tile(1, 1, first + per) == per
            with pool.Fori(1, TILES // 2) as k:
                for par in range(2):
                    assert tile(2 * k + par, par, first + per * (2 * k + par)) == per
            pool.wait_ge(h_stored, 16 * TILES)

        @block.tensor
        def _(pe):
            pe.wait_ge(ident_set, 1)
            pe.wait_ge(w_loaded, 16 * W_LOADS)
            for n, (srcs, _, _, k) in enumerate(turn):
                need(pe, w_copied, n - 1)
                for m, src in enumerate(srcs):
                    last = nc.tensor.transpose(PS[0:src.shape[1], 6 + n % 2, m * 128:m * 128 + k], src,
                                               t["ident"][0:k, 0:k])
                last.then_inc(w_turned, 1)
            pe.wait_ge(z_loaded, 16)

            def turns(u, par):
                if isinstance(u, int):
                    need(pe, left_sb, u - 1)
                    need(pe, right_sb, u - 1)
                else:
                    pe.wait_ge(left_sb, u - 1)
                    pe.wait_ge(right_sb, u - 1)
                pe.wait_ge(rows_sb, u + 1)
                w = wloc
                for k in range(FCHUNKS):
                    src = prow[:, w % 2, k * 128:(k + 1) * 128]
                    ins = nc.tensor.transpose(PS[:, 2 * (w % 2) + k // 3, (k % 3) * 128:(k % 3) * 128 + TROWS],
                                              src, t["ident"][0:TROWS, 0:TROWS])
                    if k == 2:
                        ins.then_inc(left_ps, 1)
                ins.then_inc(right_ps, 1)

            def product(u, w):
                pe.wait_ge(left_sb, u + 1)
                pe.wait_ge(right_sb, u + 1)
                if w % 2 == 0:
                    pair = (u - w) // 2 + w // 2 if isinstance(u, int) else u_pair + w // 2
                    need(pe, v_sb, pair - 1)
                bank = 4 + (par_pairs + w // 2) % 2
                for k in range(FCHUNKS):
                    ins = nc.tensor.matmul(PS[0:TROWS, bank, (w % 2) * DIM:(w % 2 + 1) * DIM],
                                           patchT[:, w % 2, k, :], zw[:, k, :], start=(k == 0), stop=(k == FCHUNKS - 1))
                ins.then_inc(v_ps, 1)

            def tile(tl, par):
                nonlocal wloc, u_pair, par_pairs
                u_pair = UNIT // 2 * tl
                par_pairs = par * (UNIT // 2)
                for w in range(GRID):
                    wloc = w
                    turns(UNIT * tl + w, par)
                    if w:
                        product(UNIT * tl + w - 1, w - 1)
                product(UNIT * tl + GRID - 1, GRID - 1)

            wloc = u_pair = par_pairs = 0
            for tl in range(2):
                tile(tl, tl)
            with pe.Fori(1, TILES // 2) as k:
                for par in range(2):
                    tile(2 * k + par, par)

        @block.scalar
        def _(act):
            act.wait_ge(tanh_in, 1)
            nc.scalar.activation(th[:], norm[:], ACT.Tanh).then_inc(tanh_out, 1)

            def pair(tl, par, m):
                act.wait_ge(v_ps, UNIT * tl + 2 * m + 2)
                if m == 0:
                    need(act, h_sb, tl - 1)
                nc.scalar.activation(
                    vbuf[:, par, 2 * m:2 * m + 2].rearrange("p w d -> p (w d)"),
                    PS[0:TROWS, 4 + (par * (UNIT // 2) + m) % 2, 0:2 * DIM], ACT.Copy).then_inc(v_sb, 1)

            def rows(tl, par, w):
                need(act, right_ps, UNIT * tl + w - 1)
                nc.scalar.activation(
                    prow[:, w % 2].rearrange("r (f q) -> r f q", q=PATCH),
                    ximg[:, par].rearrange("r c (p w q) -> r (c p) w q", p=PATCH, w=GRID)[:, :, w, :],
                    ACT.Copy).then_inc(rows_sb, 1)

            def tile(tl, par, half_of):
                act.wait_ge(x_loaded[par], 16 * TILE_IMAGES * (half_of + 1))
                rows(tl, par, 0)
                for w in range(GRID):
                    if w + 1 < GRID:
                        rows(tl, par, w + 1)
                    act.wait_ge(left_ps, UNIT * tl + w + 1)
                    nc.scalar.activation(
                        patchT[:, w % 2, 0:3, :],
                        PS[:, 2 * (w % 2), 0:384].rearrange("p (k r) -> p k r", k=3)[:, :, 0:TROWS],
                        ACT.Copy).then_inc(left_sb, 1)
                    if w and w % 2 == 0:
                        pair(tl, par, w // 2 - 1)
                pair(tl, par, GRID // 2 - 1)
                act.wait_ge(tanh_in, tl + 2)
                nc.scalar.activation(th[:], norm[:], ACT.Tanh).then_inc(tanh_out, 1)

            for tl in range(2):
                tile(tl, tl, 0)
            with act.Fori(1, TILES // 2) as k:
                for par in range(2):
                    tile(2 * k + par, par, k)

        @block.vector
        def _(dve):
            dve.wait_ge(zero_set, 9)
            for n, (_, dsts, scale, k) in enumerate(turn):
                dve.wait_ge(w_turned, n + 1)
                for m, dst in enumerate(dsts):
                    src = PS[0:dst.shape[0], 6 + n % 2, m * 128:m * 128 + k]
                    if len(dst.shape) == 3:
                        src = src.rearrange("p (h d) -> p h d", d=HEAD_DIM)
                    last = nc.vector.tensor_scalar(dst, src, scale, None, ALU.mult)
                last.then_inc(w_copied, 1)
            dve.wait_ge(pos_loaded, 16 * TILE_IMAGES)
            for turn_of in range(2):
                if turn_of:
                    dve.wait_ge(pos_ready, 1)
                nc.vector.tensor_tensor(hbuf[:], pos[:], pos[:], ALU.mult).then_inc(v_prod, 1)
                dve.wait_ge(v_prod, turn_of + 1)
                nc.vector.tensor_reduce(y2[:], hbuf[:], AX.X, ALU.add).then_inc(v_dot, 1)

            def dots(tl, par, m):
                dve.wait_ge(v_sb, UNIT // 2 * tl + m + 1)
                v = vbuf[:, par, 2 * m:2 * m + 2]
                nc.vector.tensor_tensor(prods[:, m % 2, 0], v, v, ALU.mult)
                nc.vector.tensor_tensor(prods[:, m % 2, 1], v, pos[:, 2 * m:2 * m + 2], ALU.mult).then_inc(v_prod, 1)

            def sum_up(tl, par, m):
                dve.wait_ge(v_prod, 2 + UNIT // 2 * tl + m + 1)
                nc.vector.tensor_reduce(sums[:, par, :, 2 * m:2 * m + 2], prods[:, m % 2], AX.X, ALU.add).then_inc(v_dot, 1)

            def tile(tl, par):
                for w in range(GRID):
                    dve.wait_ge(right_ps, UNIT * tl + w + 1)
                    nc.vector.tensor_copy(
                        patchT[:, w % 2, 3:6, :],
                        PS[:, 2 * (w % 2) + 1, 0:384].rearrange("p (k r) -> p k r", k=3)[:, :, 0:TROWS]
                    ).then_inc(right_sb, 1)
                    if w > 2 and w % 2 == 1:
                        dots(tl, par, w // 2 - 1)
                    if w > 2 and w % 2 == 0:
                        sum_up(tl, par, w // 2 - 2)
                sum_up(tl, par, GRID // 2 - 2)
                dots(tl, par, GRID // 2 - 1)
                sum_up(tl, par, GRID // 2 - 1)

            for tl in range(2):
                tile(tl, tl)
            with dve.Fori(1, TILES // 2) as k:
                for par in range(2):
                    tile(2 * k + par, par)

    ctx.close()


def layer(nc, PS, t, cls_tok, hseq, xdisp, out):
    ctx = ExitStack()

    def sb(name, shape, dt=fp32):
        return ctx.enter_context(nc.sbuf_tensor(name, shape, dt))

    def sem(name):
        return ctx.enter_context(nc.semaphore(name))

    hin = sb("hin", [ROWS, 2, 2, DIM])
    hb = sb("hb", [ROWS, 2, 2, DIM])
    stats1 = sb("stats1", [ROWS, 2, 6])
    mv1 = sb("mv1", [ROWS, 2, 2])
    ve1 = sb("ve1", [ROWS, 2])
    rstd1 = sb("rstd1", [ROWS, 2])
    xn = sb("xn", [ROWS, 2, 2, 4, HEAD_PAD])
    xT = sb("xT", [128, 2, PADDED])
    qT = sb("qT", [128, 2, 4, PADDED])
    kT = sb("kT", [128, 2, PADDED])
    vn = sb("vn", [ROWS, 2, HEADS, HEAD_PAD])
    gqk = sb("gqk", [HALF, 2, PADDED])
    gv = sb("gv", [ROWS, 2, 4, HEAD_PAD])
    cur = sb("cur", [128, PADDED])
    nmax = sb("nmax", [ROWS, 2, 2])
    prob = sb("prob", [ROWS, 2, 2, PADDED])
    probT = sb("probT", [ROWS, 2, 2, PADDED])
    sums = sb("psums", [ROWS, 2, 2])
    invs = sb("invs", [ROWS, 2, 2])
    hxT = sb("hxT", [128, 2, PADDED])
    yT = sb("yT", [128, 2, PADDED])
    h2 = sb("h2", [ROWS, 2, 2, DIM])
    stats2 = sb("stats2", [ROWS, 2, 6])
    mv2 = sb("mv2", [ROWS, 2, 2])
    ve2 = sb("ve2", [ROWS, 2])
    rstd2 = sb("rstd2", [ROWS, 2])
    xrow = sb("xrow", [ROWS, 2, 2, XCOLS])
    x2T = sb("x2T", [HALF, 2, PADDED])
    tanh = sb("tanh", [ECHUNK, 2, PADDED])
    gated = sb("gated", [ECHUNK, 2, PADDED])
    inter = sb("inter", [ECHUNK, SCHUNKS, PADDED])
    obuf = sb("obuf", [ROWS, 2, 2, DIM])
    elog = sb("elog", [ROWS, 2, EXPERTS])
    sig = sb("sig", [ROWS, 2, EXPERTS])
    choice = sb("choice", [ROWS, 2, EXPERTS + 2])
    struck = sb("struck", [ROWS, 2, EXPERTS + 2])
    top = sb("top", [ROWS, 2, 8])
    mask = sb("mask", [ROWS, 2, EXPERTS], bf16)
    wraw = sb("wraw", [ROWS, 2, EXPERTS])
    wsum = sb("wsum", [ROWS, 2])
    winv = sb("winv", [ROWS, 2])
    place = sb("place", [ROWS, 2, EXPERTS])
    fits = sb("fits", [ROWS, 2, EXPERTS])
    code = sb("code", [ROWS, 2, EXPERTS])
    best = sb("best", [ROWS, 2, 8])
    slot = sb("slot", [ROWS, 2, 2, 8], u32)
    taken = sb("taken", [ROWS, EXPERTS])

    ready = sem("b_ready")
    h_loaded = [sem(f"h_loaded{p}") for p in range(2)]
    cls_in = sem("cls_in")
    ve1_ready = sem("ve1_ready")
    rstd1_ready, hb_ready = sem("rstd1_ready"), sem("hb_ready")
    xn_ready = sem("xn_ready")
    xt_ps, xt_ready = sem("xt_ps"), sem("xt_ready")
    q_ps, q_ready = sem("q_ps"), sem("q_ready")
    k_ps, k_ready = sem("k_ps"), sem("k_ready")
    vv_ps, vv_ready = sem("vv_ps"), sem("vv_ready")
    gqk_ps, gqk_ready = sem("gqk_ps"), sem("gqk_ready")
    gv_ps, gv_ready = sem("gv_ps"), sem("gv_ready")
    s_ps = sem("s_ps")
    max_ready = sem("max_ready")
    p_ready = sem("p_ready")
    pn_ready = sem("pn_ready")
    t_ps = sem("t_ps")
    t_ready = sem("t_ready")
    hx_ps, hx_ready = sem("hx_ps"), sem("hx_ready")
    heads_ps, yt_ready = sem("heads_ps"), sem("yt_ready")
    proj_ps, h2_ready = sem("proj_ps"), sem("h2_ready")
    ve2_ready, rstd2_ready = sem("ve2_ready"), sem("rstd2_ready")
    xn2_ready = sem("xn2_ready")
    x2t_ps, x2t_ready = sem("x2t_ps"), sem("x2t_ready")
    logit_ps, elog_ready = sem("logit_ps"), sem("elog_ready")
    sig_ready = sem("sig_ready")
    top_ready, mask_ready, winv_ready = sem("top_ready"), sem("mask_ready"), sem("winv_ready")
    count_ps, count_used = sem("count_ps"), sem("count_used")
    slot_ready = sem("slot_ready")
    ff_ps, tanh_ready, inter_ready = sem("ff_ps"), sem("tanh_ready"), sem("inter_ready")
    down_ps, out_ready = sem("down_ps"), sem("out_ready")
    sent = [sem(f"sent{p}") for p in range(2)]
    stored = [sem(f"stored{p}") for p in range(2)]
    c_norm, c_att, c_ffn, c_slot = sem("c_norm"), sem("c_att"), sem("c_ffn"), sem("c_slot")
    carrier = sem("b_carrier")
    READY = 10
    N_NORM, N_ATT, N_FFN, N_SLOT = 2, UNITS, 19, 3

    def tiles(bank, rows, width, used=None):
        return PS[0:rows, bank, 0:2 * width].rearrange("p (t k) -> p t k", t=2)[:, :, 0:used or width]

    def both(ap):
        return ap.unsqueeze(1).broadcast_to([ap.shape[0], 2, ap.shape[1]])

    def steps(engine, step):
        step(0, 0, 0, True, False, down=False)
        step(1, 0, 1, True, True, down=False)
        for s in range(2, 4):
            step(s, s // 2, s % 2, True, True)
        with engine.Fori(2, IMAGES // 2 - 1) as k:
            for par in range(2):
                step(2 * k + par, k, par, True, True)
        step(IMAGES - 2, IMAGES // 2 - 1, 0, True, True)
        step(IMAGES - 1, IMAGES // 2 - 1, 1, True, True, last=True)
        step(IMAGES, IMAGES // 2, 0, False, True)
        step(IMAGES + 1, IMAGES // 2, 1, False, False)

    with nc.Block() as block:

        @block.sync
        def _(sp):
            sp.wait_ge(ready, READY)
            for p in range(2):
                sp.dma_start(hin[0:1, p, 0, :], cls_tok).then_inc(cls_in, 16)

            def load(image, p):
                src = image * PATCHES
                sp.dma_start(hin[1:ROWS, p, 0, :], hseq[bass.ds(src, ROWS - 1), :]).then_inc(h_loaded[p], 16)
                sp.dma_start(hin[0:ROWS - 1, p, 1, :], hseq[bass.ds(src + ROWS - 1, ROWS - 1), :]
                             ).then_inc(h_loaded[p], 16)

            def store(f, p):
                sp.wait_ge(out_ready, f + 1)
                sp.dma_start(out[bass.ds(f * TOKENS, ROWS), :], obuf[:, p, 0, :]).then_inc(stored[p], 16)
                sp.dma_start(out[bass.ds(f * TOKENS + ROWS, ROWS - 1), :], obuf[0:ROWS - 1, p, 1, :]
                             ).then_inc(stored[p], 16)

            load(0, 0)
            load(1, 1)

            def step(s, half, par, att, ffn, last=False, down=True):
                if att and not (isinstance(s, int) and s >= IMAGES - 2):
                    sp.wait_ge(xn_ready, s + 1)
                    sp.wait_ge(hb_ready, s + 1)
                    load(s + 2, par)
                if down:
                    store(s - 2, par)

            steps(sp, step)
            for p in range(2):
                sp.wait_ge(stored[p], 32 * (IMAGES // 2))

        @block.gpsimd
        def _(pool):
            nc.gpsimd.memset(hin[:], 0.0).then_inc(ready, 1)
            nc.gpsimd.memset(prob[:], 0.0).then_inc(ready, 1)
            nc.gpsimd.memset(choice[:], 1e30).then_inc(ready, 1)
            nc.gpsimd.memset(taken[:], 0.0).then_inc(ready, 1)
            nc.gpsimd.memset(xrow[:], 0.0).then_inc(ready, 1)
            nc.gpsimd.memset(obuf[:], 0.0).then_inc(ready, 1)
            for spread in (xn, qT, vn, gv):
                nc.gpsimd.memset(spread[:], 0.0).then_inc(ready, 1)

            def norm1(a, half, p):
                pool.wait_ge(ve1_ready, a + 1)
                nc.gpsimd.tensor_tensor(rstd1[:], ve1[:], t["mhalf"][:], ALU.pow).then_inc(rstd1_ready, 1)
                pool.wait_ge(h_loaded[p], 32 * (half + 1))
                need(pool, h2_ready, a - 1)
                nc.gpsimd.tensor_tensor(hb[:, p], hin[:, p], both(t["bproj"][:]), ALU.add).then_inc(hb_ready, 1)

            def dispatch(f, p):
                pool.wait_ge(slot_ready, f + 1)
                pool.sem_inc(carrier, 1)
                for tile in range(2):
                    rows = ROWS - tile
                    for k in range(TOP):
                        nc.gpsimd.indirect_dma_start(
                            xdisp[:, :], bass.IndirectOffsetOnAxis(slot[0:rows, p, tile, k:k + 1], 0),
                            xrow[0:rows, p, tile, :], None, bounds_check=SLOTS - 1, oob_is_err=False
                        ).then_inc(sent[p], 16)

            norm1(0, 0, 0)

            def step(s, half, par, att, ffn, last=False, down=True):
                if ffn:
                    pool.wait_ge(ve2_ready, s)
                    nc.gpsimd.tensor_tensor(rstd2[:], ve2[:], t["mhalf"][:], ALU.pow).then_inc(rstd2_ready, 1)
                if att and not last:
                    norm1(s + 1, half + par, 1 - par)
                if ffn and down:
                    dispatch(s - 2, par)

            steps(pool, step)
            dispatch(IMAGES - 1, 1)
            for p in range(2):
                pool.wait_ge(sent[p], 16 * 2 * TOP * (IMAGES // 2))

        @block.tensor
        def _(pe):
            mm, turn, ident = nc.tensor.matmul, nc.tensor.transpose, t["ident"]

            def product(dst, pairs):
                for n, (l, r) in enumerate(pairs):
                    ins = mm(dst, l, r, start=(n == 0), stop=(n == len(pairs) - 1))
                return ins

            def cols(src, tile):
                return src[:, tile * ROWS:(tile + 1) * ROWS]

            def turn_rows(bank, src, width):
                for c in range(2):
                    for tile in range(2):
                        ins = turn(PS[0:width, bank, c * PADDED + tile * ROWS:c * PADDED + (tile + 1) * ROWS],
                                   src[:, tile, c * width:(c + 1) * width], ident[0:ROWS, 0:ROWS])
                return ins

            def group_qk(bank, g, src):
                for part in range(2):
                    ins = product(PS[0:HALF, bank, part * PADDED:(part + 1) * PADDED],
                                  [(t["wg"][:, g, part, :], src)])
                ins.then_inc(gqk_ps, 1)

            def group_v(bank, g, src):
                for tile in range(2):
                    ins = product(PS[0:ROWS, bank, tile * HALF:(tile + 1) * HALF],
                                  [(cols(src, tile), t["wg"][:, g, 2, :])])
                ins.then_inc(gv_ps, 1)

            def scores(s, n):
                if n >= 2:
                    pe.wait_ge(p_ready, UNITS * s + n - 1)
                elif n == 1:
                    pe.wait_ge(k_ready, s + 1)
                if n in (G0, G1):
                    pe.wait_ge(gqk_ready, 2 * s + 1 + (n == G1))
                    if n == G0:
                        pe.wait_ge(q_ready, s + 1)
                    q, k = gqk[:, 0, :], gqk[:, 1, :]
                else:
                    h = UNIT_HEAD[n]
                    q, k = qT[:, h // 4, h % 4, :], kT[:, h // 4, :]
                for tile in range(2):
                    ins = mm(PS[0:ROWS, n % 2, tile * PADDED:(tile + 1) * PADDED], cols(q, tile), k,
                             start=True, stop=True)
                ins.then_inc(s_ps, 1)

            def turn_probs(s, n):
                pe.wait_ge(pn_ready, UNITS * s + n + 1)
                if n == 0:
                    pe.wait_ge(vv_ready, s + 1)
                for kt in range(2):
                    for tile in range(2):
                        ins = turn(PS[0:ROWS, 2 + n % 2, kt * PADDED + tile * ROWS:kt * PADDED + (tile + 1) * ROWS],
                                   cols(prob[:, n % 2, tile, :], kt), ident[0:ROWS, 0:ROWS])
                ins.then_inc(t_ps, 1)

            def values(s, n):
                pe.wait_ge(t_ready, UNITS * s + n + 1)
                if n in (G0, G1):
                    g = int(n == G1)
                    pe.wait_ge(gv_ready, 2 * s + 1 + g)
                    product(PS[:, 7, 0:PADDED], [(gv[:, kt].rearrange("p h d -> p (h d)"), probT[:, n % 2, kt, :]) for kt in range(2)]
                            ).then_inc(hx_ps, 1)
                    return
                h = UNIT_HEAD[n]
                if h == 0:
                    need(pe, h2_ready, s)
                at, blk = (h % 4) * HEAD_PAD, h // 4
                ins = product(PS[at:at + HEAD_PAD, 4, blk * PADDED:(blk + 1) * PADDED],
                              [(vn[:, kt, h, :], probT[:, n % 2, kt, :]) for kt in range(2)])
                if h == HEADS - 1:
                    ins.then_inc(heads_ps, 1)

            def ffn_chunk(s, j):
                if j >= 2:
                    pe.wait_ge(inter_ready, SCHUNKS * (s - 1) + j - 1)
                elif j == 1:
                    pe.wait_ge(elog_ready, s)
                for half, w in enumerate((t["wsg"], t["wsu"])):
                    ins = product(PS[0:ECHUNK, 5 + j % 2, half * PADDED:(half + 1) * PADDED],
                                  [(w[:, c, j * ECHUNK:(j + 1) * ECHUNK], x2T[:, c, :]) for c in range(2)])
                ins.then_inc(ff_ps, 1)

            DOWN_PARTS = (3, 7, 11, 2 * SCHUNKS)

            def down_part(s, first, end):
                if first == 0:
                    pe.wait_ge(inter_ready, SCHUNKS * (s - 1))
                for m in range(first, end):
                    tile, j = m // SCHUNKS, m % SCHUNKS
                    ins = mm(PS[0:ROWS, 6, tile * DIM:(tile + 1) * DIM], cols(inter[:, j, :], tile), t["wsd"][:, j, :],
                             start=(j == 0), stop=(j == SCHUNKS - 1))
                if end == 2 * SCHUNKS:
                    ins.then_inc(down_ps, 1)

            def turn_tokens(a):
                pe.wait_ge(xn_ready, a + 1)
                need(pe, hx_ready, 2 * a)
                turn_rows(7, xn[:].rearrange("p t c h d -> p t (c h d)"), 128).then_inc(xt_ps, 1)

            turn_tokens(0)

            def step(s, half, par, att, ffn, last=False, down=True):
                if down:
                    down_part(s, 0, DOWN_PARTS[0])
                if att:
                    pe.wait_ge(xt_ready, s + 1)
                    need(pe, p_ready, UNITS * s)
                    for blk in range(2):
                        ins = product(PS[:, 0, blk * PADDED:(blk + 1) * PADDED],
                                      [(t["wq"][:, c, blk].rearrange("p h d -> p (h d)"), xT[:, c, :]) for c in range(2)])
                    ins.then_inc(q_ps, 1)
                    need(pe, t_ready, UNITS * s)
                    group_qk(3, 0, xT[:, 0, :])
                    for blk in range(2):
                        ins = product(PS[:, 1, blk * PADDED:(blk + 1) * PADDED],
                                      [(t["wk"][:, c, blk].rearrange("p h d -> p (h d)"), xT[:, c, :]) for c in range(2)])
                    ins.then_inc(k_ps, 1)
                if ffn:
                    pe.wait_ge(yt_ready, s)
                    for tile in range(2):
                        ins = product(PS[0:ROWS, 4, tile * DIM:(tile + 1) * DIM],
                                      [(cols(yT[:, c, :], tile), t["wp"][:, c, :]) for c in range(2)])
                    ins.then_inc(proj_ps, 1)
                if att:
                    for tile in range(2):
                        ins = product(PS[0:ROWS, 2, tile * DIM:(tile + 1) * DIM],
                                      [(cols(xT[:, c, :], tile), t["wv"][:, c, :]) for c in range(2)])
                    ins.then_inc(vv_ps, 1)
                    group_v(7, 0, xT[:, 0, :])
                for n in range(UNITS + 2):
                    if att and n < UNITS:
                        scores(s, n)
                    if att and n == 4:
                        pe.wait_ge(hx_ready, 2 * s + 1)
                        group_qk(7, 1, cur[:])
                    if down and n < FF_SLOT:
                        down_part(s, DOWN_PARTS[n], DOWN_PARTS[n + 1])
                    if ffn:
                        if n == 1:
                            pe.wait_ge(xn2_ready, s)
                            need(pe, count_used, s - 1)
                            turn_rows(5, xrow[:, 1 - par], HALF).then_inc(x2t_ps, 1)
                        if n == FF_SLOT:
                            pe.wait_ge(x2t_ready, s)
                            ffn_chunk(s, 0)
                            need(pe, out_ready, s - 1)
                            for tile in range(2):
                                ins = product(PS[0:ROWS, 6, tile * EXPERTS:(tile + 1) * EXPERTS],
                                              [(cols(x2T[:, c, :], tile), t["wgate"][:, c, :]) for c in range(2)])
                            ins.then_inc(logit_ps, 1)
                        if FF_SLOT < n < FF_SLOT + SCHUNKS:
                            ffn_chunk(s, n - FF_SLOT)
                    if att and 2 <= n <= UNITS:
                        values(s, n - 2)
                    if att and 1 <= n <= UNITS:
                        turn_probs(s, n - 1)
                    if att and n == 4:
                        pe.wait_ge(gqk_ready, 2 * s + 2)
                        group_v(7, 1, cur[:])
                    if ffn and n == UNITS + 1:
                        pe.wait_ge(mask_ready, s)
                        pe.wait_ge(inter_ready, SCHUNKS * s - 1)
                        tri, ones = t["tri"], t["ones"]
                        first, second = mask[:, 0, :], mask[0:ROWS - 1, 1, :]
                        product(PS[0:ROWS, 5, 0:EXPERTS], [(tri[:], first)])
                        product(PS[0:ROWS, 5, EXPERTS:2 * EXPERTS], [(ones[:], first), (tri[0:ROWS - 1, :], second)])
                        product(PS[0:ROWS, 5, 2 * EXPERTS:3 * EXPERTS],
                                [(ones[:], first), (ones[0:ROWS - 1, :], second)]).then_inc(count_ps, 1)
                    if att and n == UNITS + 1:
                        if not last:
                            turn_tokens(s + 1)
                        values(s, UNITS - 1)

            steps(pe, step)

        @block.scalar
        def _(act):
            act.wait_ge(ready, READY)

            def copy(dst, src):
                return nc.scalar.activation(dst, src, ACT.Copy)

            def group_values():
                return copy(gv[:, :, :, 0:HEAD_DIM],
                            tiles(7, ROWS, HALF).rearrange("p t (h d) -> p t h d", d=HEAD_DIM))

            def turned_tokens(a):
                act.wait_ge(xt_ps, a + 1)
                copy(xT[:], tiles(7, 128, PADDED)).then_inc(xt_ready, 1)

            turned_tokens(0)

            def step(s, half, par, att, ffn, last=False, down=True):
                if att:
                    act.wait_ge(q_ps, s + 1)
                    for h in range(4):
                        at = slice(h * HEAD_PAD, (h + 1) * HEAD_PAD)
                        ins = copy(qT[at, :, h, :], tiles(0, 128, PADDED)[at])
                    ins.then_inc(q_ready, 1)
                    act.wait_ge(vv_ps, s + 1)
                    copy(vn[:, :, :, 0:HEAD_DIM], tiles(2, ROWS, DIM).rearrange("p t (h d) -> p t h d", d=HEAD_DIM)
                         ).then_inc(vv_ready, 1)
                    act.wait_ge(gv_ps, 2 * s + 1)
                    group_values().then_inc(gv_ready, 1)
                for n in range(UNITS + 2):
                    if att and n < UNITS:
                        act.wait_ge(max_ready, UNITS * s + n + 1)
                        for tile in range(2):
                            ins = nc.scalar.activation(prob[:, n % 2, tile, 0:TOKENS],
                                                       tiles(n % 2, ROWS, PADDED, TOKENS)[:, tile, :], ACT.Exp,
                                                       bias=nmax[:, n % 2, tile:tile + 1], accum_out=sums[:, n % 2, tile:tile + 1])
                        ins.then_inc(p_ready, 1)
                    if ffn and n == FF_SLOT:
                        act.wait_ge(logit_ps, s)
                        nc.scalar.activation(elog[:], tiles(6, ROWS, EXPERTS), ACT.Exp, scale=-1.0
                                             ).then_inc(elog_ready, 1)
                    if ffn and FF_SLOT <= n < FF_SLOT + SCHUNKS:
                        j = n - FF_SLOT
                        act.wait_ge(ff_ps, SCHUNKS * (s - 1) + j + 1)
                        nc.scalar.activation(tanh[:, j % 2, :], PS[0:ECHUNK, 5 + j % 2, 0:PADDED], ACT.Tanh,
                                             scale=0.5).then_inc(tanh_ready, 1)
                    if att and 1 <= n <= UNITS:
                        act.wait_ge(t_ps, UNITS * s + n)
                        copy(probT[:, (n - 1) % 2], tiles(2 + (n - 1) % 2, ROWS, PADDED)).then_inc(t_ready, 1)
                    if att and n == 5:
                        act.wait_ge(gv_ps, 2 * s + 2)
                        group_values().then_inc(gv_ready, 1)
                if att and not last:
                    turned_tokens(s + 1)

            steps(act, step)

        @block.vector
        def _(dve):
            V = nc.vector
            dve.wait_ge(ready, READY)
            dve.wait_ge(cls_in, 32)

            def stats(chain, src, st, mv, ve, done):
                for tile in range(2):
                    last = V.bn_stats(st[:, tile], src[:, tile])
                chain.link(last, carrier)
                for tile in range(2):
                    last = V.bn_aggr(mv[:, tile], st[:, tile])
                chain.link(last)
                V.tensor_scalar(ve[:], mv[:, :, 1], 1e-5, None, ALU.add).then_inc(done, 1)

            def norm1_stats(a, half, p):
                chain = Steps(dve, c_norm, N_NORM * a)
                dve.wait_ge(h_loaded[p], 32 * (half + 1))
                stats(chain, hin[:, p], stats1, mv1, ve1, ve1_ready)
                return chain

            def norm1_apply(a, p, chain):
                dve.wait_ge(rstd1_ready, a + 1)
                need(dve, xt_ps, a)
                for tile in range(2):
                    last = V.tensor_scalar(xn[:, tile].rearrange("p c h d -> p (c h) d")[:, :, 0:HEAD_DIM],
                                           hin[:, p, tile].rearrange("p (h d) -> p h d", d=HEAD_DIM), mv1[:, tile, 0:1], rstd1[:, tile:tile + 1],
                                           ALU.subtract, ALU.mult)
                last.then_inc(xn_ready, 1)
                assert chain.n == N_NORM

            def normalise_and_gate(s, n, j):
                if n is not None:
                    dve.wait_ge(p_ready, UNITS * s + n + 1)
                    inverted = chain_att.mark(V.reciprocal(invs[:, n % 2], sums[:, n % 2]))
                if j is not None:
                    bank = 5 + j % 2
                    g, u = PS[0:ECHUNK, bank, 0:PADDED], PS[0:ECHUNK, bank, PADDED:2 * PADDED]
                    dve.wait_ge(tanh_ready, SCHUNKS * (s - 1) + j + 1)
                    gated_ready = ffn_chain.mark(
                        V.scalar_tensor_tensor(gated[:, j % 2, :], tanh[:, j % 2, :], 1.0, g, ALU.add, ALU.mult))
                if n is not None:
                    chain_att.wait(inverted)
                    p = prob[:, n % 2, :, 0:TOKENS]
                    V.tensor_tensor(p, p, invs[:, n % 2].unsqueeze(2).broadcast_to([ROWS, 2, TOKENS]), ALU.mult
                                    ).then_inc(pn_ready, 1)
                if j is not None:
                    ffn_chain.wait(gated_ready)
                    V.tensor_tensor(inter[:, j, :], gated[:, j % 2, :], u, ALU.mult).then_inc(inter_ready, 1)

            def sigmoid(s, tile):
                if tile == 0:
                    dve.wait_ge(elog_ready, s)
                    ffn_chain.link(V.tensor_scalar(elog[:], elog[:], 1.0, None, ALU.add))
                V.reciprocal(sig[:, tile], elog[:, tile]).then_inc(sig_ready, 1)

            def choose(s):
                dve.wait_ge(sig_ready, 2 * s)
                ffn_chain.link(V.tensor_tensor(choice[:, :, 0:EXPERTS], sig[:], both(t["ebias"][:]), ALU.add), carrier)
                V.max(top[:, 0], choice[:, 0])
                V.max(top[:, 1], choice[:, 1]).then_inc(top_ready, 1)

            def strike(s):
                dve.wait_ge(top_ready, s)
                dve.sem_inc(carrier, 1)
                V.match_replace(struck[:, 0], top[:, 0], choice[:, 0], -1e30)
                ffn_chain.link(V.match_replace(struck[:, 1], top[:, 1], choice[:, 1], -1e30))
                V.tensor_scalar(mask[:], struck[:, :, 0:EXPERTS], -1e29, None, ALU.is_lt).then_inc(mask_ready, 1)

            def weigh(s):
                link = ffn_chain.link
                dve.wait_ge(mask_ready, s)
                link(V.tensor_tensor(wraw[:], sig[:], mask[:], ALU.mult))
                link(V.tensor_reduce(wsum[:], wraw[:], AX.X, ALU.add))
                link(V.tensor_scalar(wsum[:], wsum[:], 1e-20, None, ALU.add))
                V.reciprocal(winv[:], wsum[:]).then_inc(winv_ready, 1)

            def fill_rows(s, p):
                dve.wait_ge(winv_ready, s)
                for tile in range(2):
                    V.tensor_scalar(xrow[:, p, tile, DIM:DIM + EXPERTS], wraw[:, tile], winv[:, tile:tile + 1],
                                    ROUTE_SCALE, ALU.mult, ALU.mult)
                ffn_chain.link(V.tensor_copy(xrow[:, p, :, XCOLS - 1], t["tid"][:]))
                ffn_chain.link(V.tensor_scalar(t["tid"][:], t["tid"][:], float(TOKENS), None, ALU.add))

            def place_tokens(s):
                link = ffn_chain.link
                dve.wait_ge(count_ps, s)
                link(V.tensor_tensor(place[:], tiles(5, ROWS, EXPERTS), both(taken[:]), ALU.add))
                V.tensor_tensor(taken[:], taken[:], PS[0:ROWS, 5, 2 * EXPERTS:3 * EXPERTS], ALU.add
                                ).then_inc(count_used, 1)

            def choose_slots(f, p, piece):
                chain = Steps(dve, c_slot, N_SLOT * f + piece)
                if piece == 0:
                    dve.wait_ge(count_used, f + 1)
                    V.scalar_tensor_tensor(fits[:], place[:], float(CAP), mask[:], ALU.is_lt, ALU.mult)
                    chain.mark(V.tensor_tensor(code[:], both(t["rbase"][:]), place[:], ALU.subtract))
                    return
                chain.wait(0)
                if piece == 1:
                    chain.mark(V.tensor_tensor(code[:], code[:], fits[:], ALU.mult))
                if piece == 2:
                    dve.sem_inc(carrier, 1)
                    V.max(best[:, 0], code[:, 0])
                    chain.mark(V.max(best[:, 1], code[:, 1]))
                if piece == 3:
                    V.tensor_scalar(slot[:, p], best[:], -1.0, SLOT_TOP, ALU.mult, ALU.add).then_inc(slot_ready, 1)

            ffn_chain = chain_att = parf = None

            def step(s, half, par, att, ffn, last=False, down=True):
                nonlocal ffn_chain, chain_att, parf
                parf = 1 - par
                half_f = half if par else half - 1
                ffn_chain = Steps(dve, c_ffn, N_FFN * (s - 1))
                chain_att = Steps(dve, c_att, N_ATT * s)
                if att:
                    dve.wait_ge(gqk_ps, 2 * s + 1)
                    V.tensor_copy(gqk[:], tiles(3, HALF, PADDED)).then_inc(gqk_ready, 1)
                    dve.wait_ge(k_ps, s + 1)
                    V.tensor_copy(kT[:], tiles(1, 128, PADDED)).then_inc(k_ready, 1)
                if ffn:
                    dve.wait_ge(proj_ps, s)
                    dve.wait_ge(hb_ready, s)
                    V.tensor_tensor(h2[:, parf], tiles(4, ROWS, DIM), hb[:, parf], ALU.add).then_inc(h2_ready, 1)
                    dve.wait_ge(h2_ready, s)
                    stats(ffn_chain, h2[:, parf], stats2, mv2, ve2, ve2_ready)
                for n in range(UNITS + 2):
                    if att and n < UNITS:
                        dve.wait_ge(s_ps, UNITS * s + n + 1)
                        V.tensor_reduce(nmax[:, n % 2, :], tiles(n % 2, ROWS, PADDED, TOKENS), AX.X, ALU.max,
                                        negate=True).then_inc(max_ready, 1)
                    if att and n == 4:
                        dve.wait_ge(gqk_ps, 2 * s + 2)
                        V.tensor_copy(gqk[:], tiles(7, HALF, PADDED)).then_inc(gqk_ready, 1)
                    normalise_and_gate(s, n - 1 if att and 1 <= n <= UNITS else None,
                                       n - 1 - FF_SLOT if ffn and FF_SLOT < n <= FF_SLOT + SCHUNKS else None)
                    if ffn and n == 0:
                        dve.wait_ge(rstd2_ready, s)
                        need(dve, sent[parf], 32 * TOP * half_f)
                        for tile in range(2):
                            ins = V.tensor_scalar(xrow[:, parf, tile, 0:DIM], h2[:, parf, tile], mv2[:, tile, 0:1],
                                                  rstd2[:, tile:tile + 1], ALU.subtract, ALU.mult)
                        ins.then_inc(xn2_ready, 1)
                    if down and 2 <= n < 6:
                        choose_slots(s - 2, par, n - 2)
                    if down and n == 2:
                        dve.wait_ge(down_ps, s - 1)
                        need(dve, stored[par], 32 * (half - 1))
                        V.scalar_tensor_tensor(obuf[:, par], tiles(6, ROWS, DIM), 0.5, h2[:, par], ALU.mult, ALU.add
                                               ).then_inc(out_ready, 1)
                    if ffn and n == 1:
                        dve.wait_ge(x2t_ps, s)
                        V.tensor_copy(x2T[:], tiles(5, HALF, PADDED)).then_inc(x2t_ready, 1)
                    if att and n == 3:
                        dve.wait_ge(hx_ps, 2 * s + 1)
                        V.tensor_copy(hxT[:, 0], PS[:, 7, 0:PADDED])
                        V.tensor_tensor(cur[:], xT[:, 1], PS[:, 7, 0:PADDED], ALU.add).then_inc(hx_ready, 1)
                    if att and n == 8:
                        dve.wait_ge(hx_ps, 2 * s + 2)
                        V.tensor_copy(hxT[:, 1], PS[:, 7, 0:PADDED]).then_inc(hx_ready, 1)
                    if ffn:
                        if n in (5, 6):
                            sigmoid(s, n - 5)
                        if n == 7:
                            choose(s)
                        if n == 8:
                            strike(s)
                        if n == 9:
                            weigh(s)
                        if n == 10:
                            fill_rows(s, parf)
                    if att and not last and n == 1:
                        next_norm = norm1_stats(s + 1, half + par, 1 - par)
                    if att and not last and n == 4:
                        norm1_apply(s + 1, 1 - par, next_norm)
                if att:
                    dve.wait_ge(heads_ps, s + 1)
                    V.tensor_tensor(yT[:], tiles(4, 128, PADDED), hxT[:], ALU.add).then_inc(yt_ready, 1)
                    assert chain_att.n == N_ATT
                if ffn:
                    place_tokens(s)
                    assert ffn_chain.n == N_FFN, ffn_chain.n

            norm1_apply(0, 0, norm1_stats(0, 0, 0))
            steps(dve, step)

    ctx.close()


def experts(nc, PS, t, Wgu, Wd, xdisp, out):
    ctx = ExitStack()

    def sb(name, shape, dt=fp32):
        return ctx.enter_context(nc.sbuf_tensor(name, shape, dt))

    def sem(name):
        return ctx.enter_context(nc.semaphore(name))

    wgu = sb("e_wgu", [HALF, 2, 2, 2 * EHID])
    wd = sb("e_wd", [ECHUNK, 2, ECHUNKS, DIM])
    xb = sb("e_xb", [HALF, 2, 2, DIM])
    wt = sb("e_wt", [HALF, 2, 2])
    tok = sb("e_tok", [HALF, 2, 2])
    tokn = sb("e_tokn", [HALF, 2, 2], u32)
    xT = sb("e_xT", [HALF, 2, 2, CAP])
    act_g = sb("e_act", [ECHUNK, 2, 2, CAP])
    inter = sb("e_inter", [ECHUNK, 2, ECHUNKS, CAP])
    yb = sb("e_yb", [HALF, 2, 2, DIM])

    w_in = [sem(f"w_in{p}") for p in range(2)]
    d_in = [sem(f"d_in{p}") for p in range(2)]
    x_in = [sem(f"x_in{p}") for p in range(2)]
    r_in = [sem(f"r_in{p}") for p in range(2)]
    xt_ps, xt_sb = sem("e_xt_ps"), sem("e_xt_sb")
    up_ps = sem("e_up_ps")
    silu_sb, inter_sb = sem("silu_sb"), sem("e_inter_sb")
    y_ps, y_sb = sem("y_ps"), sem("y_sb")
    tok_sb = sem("tok_sb")
    added = sem("added")
    carrier = sem("e_carrier")
    HALVES = 2
    BX, BG, BU, BY = 0, 1, 3, 5

    def steps(engine, step):
        step(0, 0, 0, first=True)
        for e in range(1, 4):
            step(e, e // 2, e % 2)
        with engine.Fori(2, EXPERTS // 2 - 1) as k:
            for par in range(2):
                step(2 * k + par, k, par)
        step(EXPERTS - 2, EXPERTS // 2 - 1, 0)
        step(EXPERTS - 1, EXPERTS // 2 - 1, 1, last=True)

    with nc.Block() as block:

        @block.sync
        def _(sp):
            rows = xdisp.rearrange("(e t p) c -> e p t c", t=2, p=HALF)
            up = Wgu.rearrange("e (c p) f -> e p c f", p=HALF)
            dn = Wd.rearrange("e (j p) d -> e p j d", p=ECHUNK)

            def load_up(e, p):
                sp.dma_start(xb[:, p], rows[bass.ds(e, 1)][:, :, :, 0:DIM].rearrange("e p t c -> (e p) t c")
                             ).then_inc(x_in[p], 16)
                sp.dma_start(wgu[:, p], up[bass.ds(e, 1)].rearrange("e p c f -> (e p) c f")).then_inc(w_in[p], 16)

            def load_down(e, p):
                sp.dma_start(wd[:, p], dn[bass.ds(e, 1)].rearrange("e p j d -> (e p) j d")).then_inc(d_in[p], 16)
                sp.dma_start(wt[:, p], weight_column(e), allow_slow_non_contiguous=True).then_inc(r_in[p], 16)
                sp.dma_start(tok[:, p], rows[bass.ds(e, 1)][:, :, :, XCOLS - 1].rearrange("e p t -> (e p) t"),
                             allow_slow_non_contiguous=True).then_inc(r_in[p], 16)

            def weight_column(e):
                src = xdisp[bass.ds(e * CAP, CAP), :].rearrange("(t p) c -> p t c", p=HALF)
                return src[:, :, bass.ds(DIM + e, 1)].rearrange("p t o -> p (t o)")

            for e in range(2):
                load_up(e, e)
                load_down(e, e)

            def step(e, half, par, first=False, last=False):
                if isinstance(e, int) and e >= EXPERTS - 2:
                    return
                sp.wait_ge(up_ps, 2 * (e + 1))
                load_up(e + 2, par)
                sp.wait_ge(y_sb, e + 1)
                sp.wait_ge(tok_sb, e + 1)
                load_down(e + 2, par)

            steps(sp, step)

        @block.tensor
        def _(pe):
            mm, turn, ident = nc.tensor.matmul, nc.tensor.transpose, t["ident"]

            def turn_slots(e, half, p):
                pe.wait_ge(x_in[p], 16 * (half + 1))
                need(pe, xt_sb, e)
                for c in range(2):
                    for tile in range(2):
                        ins = turn(PS[0:HALF, BX, c * CAP + tile * HALF:c * CAP + (tile + 1) * HALF],
                                   xb[:, p, tile, c * HALF:(c + 1) * HALF], ident[0:HALF, 0:HALF])
                ins.then_inc(xt_ps, 1)

            def up(e, half, p, m):
                if m == 0:
                    pe.wait_ge(w_in[p], 16 * (half + 1))
                    pe.wait_ge(xt_sb, e + 1)
                need(pe, inter_sb, 2 * (e - 1) + m + 1)
                for kind, bank in enumerate((BG + m, BU + m)):
                    for j in range(2):
                        at = kind * EHID + (2 * m + j) * ECHUNK
                        for c in range(2):
                            ins = mm(PS[0:ECHUNK, bank, j * CAP:(j + 1) * CAP], wgu[:, p, c, at:at + ECHUNK],
                                     xT[:, p, c, :], start=(c == 0), stop=(c == 1))
                ins.then_inc(up_ps, 1)

            def down(e, half, p):
                pe.wait_ge(d_in[p], 16 * (half + 1))
                pe.wait_ge(inter_sb, 2 * (e + 1))
                need(pe, y_sb, e)
                for tile in range(2):
                    for j in range(ECHUNKS):
                        ins = mm(PS[0:HALF, BY, tile * DIM:(tile + 1) * DIM],
                                 inter[:, p, j, tile * HALF:(tile + 1) * HALF], wd[:, p, j, :],
                                 start=(j == 0), stop=(j == ECHUNKS - 1))
                ins.then_inc(y_ps, 1)

            def step(e, half, par, first=False, last=False):
                up(e, half, par, 0)
                if not first:
                    down(e - 1, half if par else half - 1, 1 - par)
                if not last:
                    turn_slots(e + 1, half + par, 1 - par)
                up(e, half, par, 1)

            turn_slots(0, 0, 0)
            steps(pe, step)
            down(EXPERTS - 1, EXPERTS // 2 - 1, 1)

        @block.scalar
        def _(act):
            def step(e, half, par, first=False, last=False):
                for m in range(2):
                    act.wait_ge(up_ps, 2 * e + m + 1)
                    nc.scalar.activation(act_g[:, m], PS[0:ECHUNK, BG + m, 0:2 * CAP].rearrange("p (j s) -> p j s", j=2),
                                         ACT.Silu).then_inc(silu_sb, 1)

            steps(act, step)

        @block.vector
        def _(dve):
            V = nc.vector

            def rows_out(e, p):
                dve.wait_ge(xt_ps, e + 1)
                V.tensor_copy(xT[:, p], PS[0:HALF, BX, 0:2 * CAP].rearrange("p (c s) -> p c s", c=2)).then_inc(xt_sb, 1)

            def result(e, half, p):
                dve.wait_ge(y_ps, e + 1)
                dve.wait_ge(r_in[p], 32 * (half + 1))
                need(dve, added, 32 * (e - 1))
                V.tensor_copy(tokn[:, p], tok[:, p]).then_inc(tok_sb, 1)
                V.tensor_tensor(yb[:, p], PS[0:HALF, BY, 0:2 * DIM].rearrange("p (t d) -> p t d", t=2),
                                wt[:, p].unsqueeze(2).broadcast_to([HALF, 2, DIM]), ALU.mult).then_inc(y_sb, 1)

            def step(e, half, par, first=False, last=False):
                def gate(m):
                    dve.wait_ge(silu_sb, 2 * e + m + 1)
                    V.tensor_tensor(inter[:, par, 2 * m:2 * m + 2], act_g[:, m],
                                    PS[0:ECHUNK, BU + m, 0:2 * CAP].rearrange("p (j s) -> p j s", j=2), ALU.mult
                                    ).then_inc(inter_sb, 1)

                gate(0)
                if not first:
                    result(e - 1, half if par else half - 1, 1 - par)
                if not last:
                    rows_out(e + 1, 1 - par)
                gate(1)

            rows_out(0, 0)
            steps(dve, step)
            result(EXPERTS - 1, EXPERTS // 2 - 1, 1)

        @block.gpsimd
        def _(pool):
            def step(e, half, par, first=False, last=False):
                pool.wait_ge(y_sb, e + 1)
                pool.sem_inc(carrier, 1)
                if not first:
                    pool.wait_ge(added, 32 * e)
                    pool.sem_inc(carrier, 1)
                for tile in range(2):
                    nc.gpsimd.indirect_dma_start(
                        out[:, :], bass.IndirectOffsetOnAxis(tokn[:, par, tile:tile + 1], 0), yb[:, par, tile, :],
                        None, bounds_check=NTOK + CAP - 1, oob_is_err=True, compute_op=ALU.add).then_inc(added, 16)

            steps(pool, step)
            pool.wait_ge(added, 32 * EXPERTS)

    ctx.close()


def program(nc, x, cls_tok, z, pos_enc, w_qkv, w_g0, w_g1, w_proj, b_proj, Wg, e_bias, Wgu, Wd, Wsg, Wsu, Wsd, out):
    with ExitStack() as ctx:
        hseq = nc.dram_tensor("hseq", [IMAGES * PATCHES, DIM], fp32, kind="Internal").ap()
        xdisp = nc.dram_tensor("xdisp", [SLOTS, XCOLS], fp32, kind="Internal").ap()
        PS = ctx.enter_context(nc.psum_tensor("PS", [128, 8, 512], fp32))
        shapes = {
            "ident": [128, 128], "rbase": [ROWS, EXPERTS], "tid": [ROWS, 2], "mhalf": [ROWS, 2],
            "wq": [128, 2, 2, 4, HEAD_PAD], "wk": [128, 2, 2, 4, HEAD_PAD], "wv": [128, 2, DIM],
            "wg": [128, 2, 3, HALF], "wp": [128, 2, DIM], "wgate": [HALF, 2, EXPERTS],
            "wsg": [HALF, 2, SHID], "wsu": [HALF, 2, SHID], "wsd": [ECHUNK, SCHUNKS, DIM],
            "bproj": [ROWS, DIM], "ebias": [ROWS, EXPERTS],
        }
        t = {k: ctx.enter_context(nc.sbuf_tensor(f"k_{k}", v, fp32)) for k, v in shapes.items()}
        t["tri"] = ctx.enter_context(nc.sbuf_tensor("k_tri", [ROWS, ROWS], bf16))
        t["ones"] = ctx.enter_context(nc.sbuf_tensor("k_ones", [ROWS, ROWS], bf16))
        embed(nc, PS, t, x, cls_tok, z, pos_enc, w_qkv, w_g0, w_g1, w_proj, b_proj, Wg, e_bias, Wsg, Wsu, Wsd,
              hseq, xdisp, out)
        layer(nc, PS, t, cls_tok, hseq, xdisp, out)
        experts(nc, PS, t, Wgu, Wd, xdisp, out)


_INS = ["x", "cls_tok", "L0_tok_z", "L0_tok_pos_enc", "L0_attn_w_qkv", "L0_attn_w_g0", "L0_attn_w_g1",
        "L0_attn_w_proj", "L0_attn_b_proj", "L0_ffn_Wg", "L0_ffn_e_bias", "L0_ffn_W_gate_up", "L0_ffn_W_down",
        "L0_ffn_Wsg", "L0_ffn_Wsu", "L0_ffn_Wsd"]


def kernel(**inputs):
    import numpy as _np
    import concourse.bacc as _bacc
    from concourse import mybir as _mybir
    from concourse.bass_utils import run_bass_kernel_spmd as _run

    nc = _bacc.Bacc("TRN2", target_bir_lowering=False, num_devices=1)
    arrays, args = {}, []
    for name in _INS:
        a = _np.ascontiguousarray(inputs[name])
        if name == "cls_tok":
            a = a.reshape(1, DIM)
        arrays[f"in_{name}"] = a
        args.append(nc.dram_tensor(f"in_{name}", a.shape, _mybir.dt.from_np(a.dtype), kind="ExternalInput").ap())
    args.append(nc.dram_tensor("out_h", (NTOK + CAP, DIM), _mybir.dt.float32, kind="ExternalOutput").ap())
    program(nc, *args)
    r = _run(nc, [arrays], core_ids=[0])
    return r.results[0]["out_h"][:NTOK].reshape(IMAGES, TOKENS, DIM)
```

```python
import concourse.bass as bass
from concourse import mybir
from contextlib import ExitStack

IMAGES, CHANNELS, SIDE, PATCH = 64, 3, 224, 16
GRID = SIDE // PATCH
PATCHES = GRID * GRID
TOKENS = PATCHES + 1
DIM = 192
HALF = DIM // 2
HEADS, HEAD_DIM, HEAD_PAD = 8, 24, 32
SCALE = float(HEAD_DIM) ** -0.5
ROWS = 99
PADDED = 2 * ROWS
FEATURES = CHANNELS * PATCH * PATCH
FCHUNKS = FEATURES // 128
TILE_IMAGES = 8
TILES = IMAGES // TILE_IMAGES
TROWS = TILE_IMAGES * GRID
EXPERTS, TOP, CAP, EHID = 128, 6, 192, 464
ECHUNK, ECHUNKS = 116, 4
SHID, SCHUNKS = 928, 8
ROUTE_SCALE = 2.5
FIRST, REST = 128, 64
SPLIT = 16.0
SLOTS = EXPERTS * CAP
XCOLS = DIM + EXPERTS + 1
NTOK = IMAGES * TOKENS
SINK = NTOK
SLOT_TOP = 32768.0
UNITS = HEADS + 2
G0, G1 = 0, 5
UNIT_HEAD = {n: h for h, n in enumerate(n for n in range(UNITS) if n not in (G0, G1))}
FF_SLOT = 3

fp32 = mybir.dt.float32
bf16 = mybir.dt.bfloat16
fp16 = mybir.dt.float16
u32 = mybir.dt.uint32
ALU = mybir.AluOpType
ACT = mybir.ActivationFunctionType
AX = mybir.AxisListType


class Steps:

    def __init__(self, engine, sem, base=0):
        self.engine, self.sem, self.base, self.n = engine, sem, base, 0

    def link(self, ins, carrier=None):
        self.wait(self.mark(ins))
        if carrier is not None:
            self.engine.sem_inc(carrier, 1)

    def mark(self, ins):
        self.n += 1
        ins.then_inc(self.sem, 1)
        return self.n

    def wait(self, n):
        self.engine.wait_ge(self.sem, self.base + n)


def need(engine, sem, value):
    if isinstance(value, int) and value <= 0:
        return
    engine.wait_ge(sem, value)


def embed(nc, PS, t, x, cls_tok, z, pos_enc, w_qkv, w_g0, w_g1, w_proj, b_proj, Wg, e_bias,
          Wsg, Wsu, Wsd, hseq, xdisp, out):
    ctx = ExitStack()

    def sb(name, shape, dt=fp32):
        return ctx.enter_context(nc.sbuf_tensor(name, shape, dt))

    def sem(name):
        return ctx.enter_context(nc.semaphore(name))

    ximg = sb("ximg", [TROWS, 2, CHANNELS, PATCH * SIDE])
    prow = sb("prow", [TROWS, 2, FEATURES])
    patchT = sb("patchT", [128, 2, FCHUNKS, TROWS])
    zw = sb("zw", [128, FCHUNKS, DIM])
    vbuf = sb("vbuf", [TROWS, 2, GRID, DIM])
    hbuf = sb("hbuf", [TROWS, GRID, DIM])
    pos = sb("pos", [TROWS, GRID, DIM])
    prods = sb("prods", [TROWS, 2, 2, 2, DIM])
    y2 = sb("y2", [TROWS, GRID])
    sums = sb("sums", [TROWS, 2, 2, GRID])
    norm = sb("norm", [TROWS, GRID])
    th = sb("th", [TROWS, GRID])
    s = sb("s", [TROWS, GRID])
    x2 = sb("x2", [TROWS, GRID])
    xy = sb("xy", [TROWS, GRID])
    num = sb("num", [TROWS, GRID])
    den = sb("den", [TROWS, GRID])
    alpha = sb("alpha", [TROWS, GRID])
    beta = sb("beta", [TROWS, GRID])
    halfp = sb("halfp", [TROWS, GRID])
    minus1 = sb("minus1", [TROWS, GRID])
    empty = sb("empty", [HALF, 2, XCOLS])
    n_qkv = sb("n_qkv", [HALF, 6, 2, 4, HEAD_PAD])
    n_g = sb("n_g", [HALF, 2, 3, 4, HEAD_PAD])
    n_p = sb("n_p", [HALF, 2, 2, 4, HEAD_PAD])
    n_gate = sb("n_gate", [EXPERTS, DIM])

    ws1 = sb("ws1", [FIRST, 2, SHID])
    ws2 = sb("ws2", [REST, 2, SHID])

    s_loaded = sem("s_loaded")
    s_high, s_low = sem("s_high"), sem("s_low")
    zero_set = sem("zero_set")
    spread_set = sem("spread_set")
    ident_set = sem("ident_set")
    empty_set = sem("empty_set")
    w_loaded = sem("w_loaded")
    z_loaded = sem("z_loaded")
    w_kept = sem("w_kept")
    pos_loaded = sem("pos_loaded")
    w_turned = sem("w_turned")
    w_copied = sem("w_copied")
    x_loaded = [sem(f"x_loaded{p}") for p in range(2)]
    rows_sb = sem("rows_sb")
    left_ps = sem("left_ps")
    right_ps = sem("right_ps")
    left_sb = sem("left_sb")
    right_sb = sem("right_sb")
    v_ps = sem("v_ps")
    v_sb = sem("v_sb")
    v_prod = sem("v_prod")
    v_dot = sem("v_dot")
    tanh_in = sem("tanh_in")
    tanh_out = sem("tanh_out")
    h_sb = sem("h_sb")
    h_stored = sem("h_stored")
    filled = sem("filled")
    pchain = sem("a_pchain")
    carrier = sem("a_carrier")
    pos_ready = sem("pos_ready")

    xsrc = x.rearrange("b c (g p) w -> b g c (p w)", p=PATCH)
    hdst = hseq.rearrange("(i r g) d -> i r (g d)", g=GRID, r=TROWS)
    UNIT = GRID
    turn = []
    def spread(ap):
        return ap.rearrange("p h d -> p (h d)")

    for k in range(6):
        src = [spread(n_qkv[:, k, c]) for c in range(2)]
        if k < 4:
            w = t["wq"] if k < 2 else t["wk"]
            dst = [w[:, c, k % 2, :, 0:HEAD_DIM] for c in range(2)]
        else:
            dst = [t["wv"][:, c, (k - 4) * HALF:(k - 3) * HALF] for c in range(2)]
        turn.append((src, dst, SCALE if k < 2 else 1.0, HALF))
    for g in range(2):
        for part in range(3):
            turn.append(([spread(n_g[:, g, part])], [t["wg"][:, g, part, :]], SCALE if part == 0 else 1.0, HALF))
    for k in range(2):
        turn.append(([spread(n_p[:, k, c]) for c in range(2)],
                     [t["wp"][:, c, k * HALF:(k + 1) * HALF] for c in range(2)], 1.0, HALF))
    turn.append(([n_gate[:, 0:FIRST], n_gate[:, FIRST:DIM]], [t["wgate1"][:], t["wgate2"][:]], 1.0, EXPERTS))
    W_LOADS, W_KEPT = 15, 3

    with nc.Block() as block:

        @block.sync
        def _(sp):
            sp.wait_ge(spread_set, 3)
            for k in range(6):
                sp.dma_start(n_qkv[:, k].rearrange("p c h d -> p (c h) d")[:, :, 0:HEAD_DIM],
                             w_qkv[k * HALF:(k + 1) * HALF].rearrange("p (h d) -> p h d", d=HEAD_DIM)
                             ).then_inc(w_loaded, 16)
            for g, w in enumerate((w_g0, w_g1)):
                for k in range(3):
                    sp.dma_start(n_g[:, g, k, :, 0:HEAD_DIM],
                                 w[k * HALF:(k + 1) * HALF].rearrange("p (h d) -> p h d", d=HEAD_DIM)
                                 ).then_inc(w_loaded, 16)
            for k in range(2):
                sp.dma_start(n_p[:, k].rearrange("p c h d -> p (c h) d")[:, :, 0:HEAD_DIM],
                             w_proj[k * HALF:(k + 1) * HALF].rearrange("p (h d) -> p h d", d=HEAD_DIM)
                             ).then_inc(w_loaded, 16)
            sp.dma_start(n_gate[:], Wg).then_inc(w_loaded, 16)
            sp.dma_start(zw[:], z.rearrange("(k p) d -> p k d", p=128)).then_inc(z_loaded, 16)
            for b in range(TILE_IMAGES):
                sp.dma_start(pos[b * GRID:(b + 1) * GRID].rearrange("g w d -> g (w d)"),
                             pos_enc.rearrange("(g w) d -> g (w d)", w=GRID)).then_inc(pos_loaded, 16)

            def load(tile, par):
                for b in range(TILE_IMAGES):
                    sp.dma_start(ximg[b * GRID:(b + 1) * GRID, par],
                                 xsrc[bass.ds(tile * TILE_IMAGES + b, 1)].rearrange("b g c f -> (b g) c f")
                                 ).then_inc(x_loaded[par], 16)

            load(0, 0)
            load(1, 1)
            for kind, w in enumerate((Wsg, Wsu)):
                sp.dma_start(ws1[:, kind], w[0:FIRST]).then_inc(s_loaded, 16)
                sp.dma_start(ws2[:, kind], w[FIRST:DIM]).then_inc(s_loaded, 16)
            sp.dma_start(t["wsd"][:], Wsd.rearrange("(j p) d -> p j d", p=ECHUNK)).then_inc(w_kept, 16)
            sp.dma_start(t["bproj"][:], b_proj.rearrange("(a d) -> a d", a=1).broadcast_to([ROWS, DIM])
                         ).then_inc(w_kept, 16)
            sp.dma_start(t["ebias"][:], e_bias.rearrange("(a d) -> a d", a=1).broadcast_to([ROWS, EXPERTS])
                         ).then_inc(w_kept, 16)
            sp.wait_ge(empty_set, 1)
            def fill(half):
                dst = xdisp.rearrange("(e t p) c -> t p e c", t=2, p=HALF)[half]
                sp.dma_start(dst, empty[:, half:half + 1, :].broadcast_to([HALF, EXPERTS, XCOLS])
                             ).then_inc(filled, 16)

            fill(0)
            sp.dma_start(out[SINK:SINK + CAP].rearrange("(t p) d -> p t d", t=2),
                         empty[:, :, 0:DIM]).then_inc(filled, 16)
            with sp.Fori(0, TILES // 2 - 1) as k:
                for par in range(2):
                    sp.wait_ge(rows_sb, UNIT * (2 * k + par + 1))
                    load(2 * k + 2 + par, par)
            fill(1)
            sp.wait_ge(w_kept, 16 * W_KEPT)
            sp.wait_ge(filled, 48)

        @block.gpsimd
        def _(pool):
            chain = Steps(pool, pchain)
            for w in (n_qkv, n_g, n_p):
                nc.gpsimd.memset(w[:], 0.0).then_inc(spread_set, 1)
            nc.gpsimd.memset(t["ident"][:], 0.0).then_inc(zero_set, 1)
            nc.gpsimd.memset(halfp[:], 0.5).then_inc(zero_set, 1)
            nc.gpsimd.memset(minus1[:], -1.0).then_inc(zero_set, 1)
            nc.gpsimd.memset(t["tri"][:], 1.0).then_inc(zero_set, 1)
            nc.gpsimd.memset(t["ones"][:], 1.0).then_inc(zero_set, 1)
            nc.gpsimd.memset(empty[:], 0.0).then_inc(zero_set, 1)
            nc.gpsimd.memset(t["mhalf"][:], -0.5).then_inc(zero_set, 1)
            nc.gpsimd.memset(t["wq"][:], 0.0).then_inc(zero_set, 1)
            nc.gpsimd.memset(t["wk"][:], 0.0).then_inc(zero_set, 1)
            pool.wait_ge(zero_set, 9)
            nc.gpsimd.affine_select(out=t["ident"][:], in_=t["ident"][:], compare_op=ALU.not_equal, fill=1.0,
                                    base=0, pattern=[[-1, 128]], channel_multiplier=1).then_inc(ident_set, 1)
            nc.gpsimd.affine_select(out=t["tri"][:], in_=t["tri"][:], compare_op=ALU.is_gt, fill=0.0,
                                    base=0, pattern=[[1, ROWS]], channel_multiplier=-1)
            nc.gpsimd.iota(empty[:, :, XCOLS - 1:XCOLS].rearrange("p t c -> p (t c)"), [[HALF, 2]], base=SINK,
                           channel_multiplier=1, allow_small_or_imprecise_dtypes=True).then_inc(empty_set, 1)
            nc.gpsimd.iota(t["rbase"][:], [[-CAP, EXPERTS]], base=int(SLOT_TOP), channel_multiplier=0,
                           allow_small_or_imprecise_dtypes=True)
            chain.link(nc.gpsimd.iota(t["tid"][:], [[ROWS, 2]], base=0, channel_multiplier=1,
                                      allow_small_or_imprecise_dtypes=True))

            pool.wait_ge(v_dot, 1)
            chain.link(nc.gpsimd.tensor_tensor(norm[:], y2[:], halfp[:], ALU.pow))
            nc.gpsimd.tensor_scalar(norm[:], norm[:], 1e-15, None, ALU.max).then_inc(tanh_in, 1)
            pool.wait_ge(tanh_in, 1)
            chain.link(nc.gpsimd.tensor_tensor(x2[:], norm[:], minus1[:], ALU.pow))
            pool.wait_ge(tanh_out, 1)
            chain.link(nc.gpsimd.tensor_tensor(s[:], th[:], x2[:], ALU.mult))
            for w in range(GRID):
                last = nc.gpsimd.tensor_scalar(pos[:, w], pos[:, w], s[:, w:w + 1], None, ALU.mult)
            last.then_inc(pos_ready, 1)
            first = chain.n

            def tile(tl, par, base):
                step = Steps(pool, pchain, base)
                link = step.link
                a, v = sums[:, par, 0], sums[:, par, 1]
                pool.wait_ge(v_dot, 2 + UNIT // 2 * (tl + 1))
                link(nc.gpsimd.tensor_tensor(norm[:], a, halfp[:], ALU.pow), carrier)
                nc.gpsimd.tensor_scalar(norm[:], norm[:], 1e-15, None, ALU.max).then_inc(tanh_in, 1)
                pool.wait_ge(tanh_in, tl + 2)
                link(nc.gpsimd.tensor_tensor(s[:], norm[:], minus1[:], ALU.pow))
                pool.wait_ge(tanh_out, tl + 2)
                link(nc.gpsimd.tensor_tensor(s[:], th[:], s[:], ALU.mult))
                link(nc.gpsimd.tensor_tensor(x2[:], s[:], s[:], ALU.mult))
                link(nc.gpsimd.tensor_tensor(x2[:], x2[:], a, ALU.mult))
                link(nc.gpsimd.tensor_tensor(xy[:], s[:], v, ALU.mult), carrier)
                link(nc.gpsimd.tensor_scalar(xy[:], xy[:], 2.0, 1.0, ALU.mult, ALU.add))
                link(nc.gpsimd.tensor_tensor(num[:], xy[:], y2[:], ALU.add))
                link(nc.gpsimd.tensor_tensor(den[:], x2[:], y2[:], ALU.mult))
                link(nc.gpsimd.tensor_tensor(den[:], den[:], xy[:], ALU.add), carrier)
                link(nc.gpsimd.tensor_scalar(den[:], den[:], 1e-15, None, ALU.max))
                link(nc.gpsimd.tensor_tensor(den[:], den[:], minus1[:], ALU.pow))
                link(nc.gpsimd.tensor_tensor(alpha[:], num[:], s[:], ALU.mult))
                link(nc.gpsimd.tensor_tensor(alpha[:], alpha[:], den[:], ALU.mult), carrier)
                link(nc.gpsimd.tensor_scalar(beta[:], x2[:], -1.0, 1.0, ALU.mult, ALU.add))
                link(nc.gpsimd.tensor_tensor(beta[:], beta[:], den[:], ALU.mult))
                need(pool, h_stored, 16 * tl)
                wide = [TROWS, GRID, DIM]
                nc.gpsimd.tensor_tensor(vbuf[:, par], vbuf[:, par], alpha[:].unsqueeze(2).broadcast_to(wide), ALU.mult)
                link(nc.gpsimd.tensor_tensor(hbuf[:], pos[:], beta[:].unsqueeze(2).broadcast_to(wide), ALU.mult))
                nc.gpsimd.tensor_tensor(hbuf[:], hbuf[:], vbuf[:, par], ALU.add).then_inc(h_sb, 1)
                pool.wait_ge(h_sb, tl + 1)
                pool.sem_inc(carrier, 1)
                nc.gpsimd.dma_start(hdst[bass.ds(tl, 1)].rearrange("i r f -> (i r) f"),
                                    hbuf[:].rearrange("p g d -> p (g d)")).then_inc(h_stored, 16)
                return step.n

            per = tile(0, 0, first)
            assert tile(1, 1, first + per) == per
            with pool.Fori(1, TILES // 2) as k:
                for par in range(2):
                    assert tile(2 * k + par, par, first + per * (2 * k + par)) == per
            pool.wait_ge(h_stored, 16 * TILES)

        @block.tensor
        def _(pe):
            pe.wait_ge(ident_set, 1)
            pe.wait_ge(w_loaded, 16 * W_LOADS)
            for n, (srcs, _, _, k) in enumerate(turn):
                need(pe, w_copied, n - 1)
                for m, src in enumerate(srcs):
                    last = nc.tensor.transpose(PS[0:src.shape[1], 6 + n % 2, m * 128:m * 128 + k], src,
                                               t["ident"][0:k, 0:k])
                last.then_inc(w_turned, 1)
            pe.wait_ge(z_loaded, 16)

            def turns(u, par):
                if isinstance(u, int):
                    need(pe, left_sb, u - 1)
                    need(pe, right_sb, u - 1)
                else:
                    pe.wait_ge(left_sb, u - 1)
                    pe.wait_ge(right_sb, u - 1)
                pe.wait_ge(rows_sb, u + 1)
                w = wloc
                for k in range(FCHUNKS):
                    src = prow[:, w % 2, k * 128:(k + 1) * 128]
                    ins = nc.tensor.transpose(PS[:, 2 * (w % 2) + k // 3, (k % 3) * 128:(k % 3) * 128 + TROWS],
                                              src, t["ident"][0:TROWS, 0:TROWS])
                    if k == 2:
                        ins.then_inc(left_ps, 1)
                ins.then_inc(right_ps, 1)

            def product(u, w):
                pe.wait_ge(left_sb, u + 1)
                pe.wait_ge(right_sb, u + 1)
                if w % 2 == 0:
                    pair = (u - w) // 2 + w // 2 if isinstance(u, int) else u_pair + w // 2
                    need(pe, v_sb, pair - 1)
                bank = 4 + (par_pairs + w // 2) % 2
                for k in range(FCHUNKS):
                    ins = nc.tensor.matmul(PS[0:TROWS, bank, (w % 2) * DIM:(w % 2 + 1) * DIM],
                                           patchT[:, w % 2, k, :], zw[:, k, :], start=(k == 0), stop=(k == FCHUNKS - 1))
                ins.then_inc(v_ps, 1)

            def tile(tl, par):
                nonlocal wloc, u_pair, par_pairs
                u_pair = UNIT // 2 * tl
                par_pairs = par * (UNIT // 2)
                for w in range(GRID):
                    wloc = w
                    turns(UNIT * tl + w, par)
                    if w:
                        product(UNIT * tl + w - 1, w - 1)
                product(UNIT * tl + GRID - 1, GRID - 1)

            wloc = u_pair = par_pairs = 0
            for tl in range(2):
                tile(tl, tl)
            with pe.Fori(1, TILES // 2) as k:
                for par in range(2):
                    tile(2 * k + par, par)

        @block.scalar
        def _(act):
            act.wait_ge(tanh_in, 1)
            nc.scalar.activation(th[:], norm[:], ACT.Tanh).then_inc(tanh_out, 1)

            def pair(tl, par, m):
                act.wait_ge(v_ps, UNIT * tl + 2 * m + 2)
                if m == 0:
                    need(act, h_sb, tl - 1)
                nc.scalar.activation(
                    vbuf[:, par, 2 * m:2 * m + 2].rearrange("p w d -> p (w d)"),
                    PS[0:TROWS, 4 + (par * (UNIT // 2) + m) % 2, 0:2 * DIM], ACT.Copy).then_inc(v_sb, 1)

            def rows(tl, par, w):
                need(act, right_ps, UNIT * tl + w - 1)
                nc.scalar.activation(
                    prow[:, w % 2].rearrange("r (f q) -> r f q", q=PATCH),
                    ximg[:, par].rearrange("r c (p w q) -> r (c p) w q", p=PATCH, w=GRID)[:, :, w, :],
                    ACT.Copy).then_inc(rows_sb, 1)

            def tile(tl, par, half_of):
                act.wait_ge(x_loaded[par], 16 * TILE_IMAGES * (half_of + 1))
                rows(tl, par, 0)
                for w in range(GRID):
                    if w + 1 < GRID:
                        rows(tl, par, w + 1)
                    act.wait_ge(left_ps, UNIT * tl + w + 1)
                    nc.scalar.activation(
                        patchT[:, w % 2, 0:3, :],
                        PS[:, 2 * (w % 2), 0:384].rearrange("p (k r) -> p k r", k=3)[:, :, 0:TROWS],
                        ACT.Copy).then_inc(left_sb, 1)
                    if w and w % 2 == 0:
                        pair(tl, par, w // 2 - 1)
                pair(tl, par, GRID // 2 - 1)
                act.wait_ge(tanh_in, tl + 2)
                nc.scalar.activation(th[:], norm[:], ACT.Tanh).then_inc(tanh_out, 1)

            for tl in range(2):
                tile(tl, tl, 0)
            with act.Fori(1, TILES // 2) as k:
                for par in range(2):
                    tile(2 * k + par, par, k)
            act.wait_ge(s_loaded, 64)
            nc.scalar.activation(t["ws1h"][:], ws1[:], ACT.Copy, scale=SPLIT)
            nc.scalar.activation(t["ws2hl"][0:REST], ws2[:], ACT.Copy, scale=SPLIT).then_inc(s_high, 1)

        @block.vector
        def _(dve):
            dve.wait_ge(zero_set, 9)
            for n, (_, dsts, scale, k) in enumerate(turn):
                dve.wait_ge(w_turned, n + 1)
                for m, dst in enumerate(dsts):
                    src = PS[0:dst.shape[0], 6 + n % 2, m * 128:m * 128 + k]
                    if len(dst.shape) == 3:
                        src = src.rearrange("p (h d) -> p h d", d=HEAD_DIM)
                    last = nc.vector.tensor_scalar(dst, src, scale, None, ALU.mult)
                last.then_inc(w_copied, 1)
            dve.wait_ge(pos_loaded, 16 * TILE_IMAGES)
            for turn_of in range(2):
                if turn_of:
                    dve.wait_ge(pos_ready, 1)
                nc.vector.tensor_tensor(hbuf[:], pos[:], pos[:], ALU.mult).then_inc(v_prod, 1)
                dve.wait_ge(v_prod, turn_of + 1)
                nc.vector.tensor_reduce(y2[:], hbuf[:], AX.X, ALU.add).then_inc(v_dot, 1)

            def dots(tl, par, m):
                dve.wait_ge(v_sb, UNIT // 2 * tl + m + 1)
                v = vbuf[:, par, 2 * m:2 * m + 2]
                nc.vector.tensor_tensor(prods[:, m % 2, 0], v, v, ALU.mult)
                nc.vector.tensor_tensor(prods[:, m % 2, 1], v, pos[:, 2 * m:2 * m + 2], ALU.mult).then_inc(v_prod, 1)

            def sum_up(tl, par, m):
                dve.wait_ge(v_prod, 2 + UNIT // 2 * tl + m + 1)
                nc.vector.tensor_reduce(sums[:, par, :, 2 * m:2 * m + 2], prods[:, m % 2], AX.X, ALU.add).then_inc(v_dot, 1)

            def tile(tl, par):
                for w in range(GRID):
                    dve.wait_ge(right_ps, UNIT * tl + w + 1)
                    nc.vector.tensor_copy(
                        patchT[:, w % 2, 3:6, :],
                        PS[:, 2 * (w % 2) + 1, 0:384].rearrange("p (k r) -> p k r", k=3)[:, :, 0:TROWS]
                    ).then_inc(right_sb, 1)
                    if w > 2 and w % 2 == 1:
                        dots(tl, par, w // 2 - 1)
                    if w > 2 and w % 2 == 0:
                        sum_up(tl, par, w // 2 - 2)
                sum_up(tl, par, GRID // 2 - 2)
                dots(tl, par, GRID // 2 - 1)
                sum_up(tl, par, GRID // 2 - 1)

            for tl in range(2):
                tile(tl, tl)
            with dve.Fori(1, TILES // 2) as k:
                for par in range(2):
                    tile(2 * k + par, par)
            dve.wait_ge(s_high, 1)
            nc.vector.scalar_tensor_tensor(t["ws1l"][:], ws1[:], SPLIT, t["ws1h"][:], ALU.mult, ALU.subtract)
            nc.vector.scalar_tensor_tensor(t["ws2hl"][REST:2 * REST], ws2[:], SPLIT, t["ws2hl"][0:REST],
                                           ALU.mult, ALU.subtract).then_inc(s_low, 1)
            dve.wait_ge(s_low, 1)

    ctx.close()


def layer(nc, PS, t, cls_tok, hseq, xdisp, out):
    ctx = ExitStack()

    def sb(name, shape, dt=fp32):
        return ctx.enter_context(nc.sbuf_tensor(name, shape, dt))

    def sem(name):
        return ctx.enter_context(nc.semaphore(name))

    hin = sb("hin", [ROWS, 2, 2, DIM])
    hb = sb("hb", [ROWS, 2, 2, DIM])
    stats1 = sb("stats1", [ROWS, 2, 6])
    mv1 = sb("mv1", [ROWS, 2, 2])
    ve1 = sb("ve1", [ROWS, 2])
    rstd1 = sb("rstd1", [ROWS, 2])
    xn = sb("xn", [ROWS, 2, 2, 4, HEAD_PAD])
    xT = sb("xT", [128, 2, PADDED])
    qT = sb("qT", [128, 2, 4, PADDED])
    kT = sb("kT", [128, 2, PADDED])
    vn = sb("vn", [ROWS, 2, HEADS, HEAD_PAD])
    gqk = sb("gqk", [HALF, 2, PADDED])
    gv = sb("gv", [ROWS, 2, 4, HEAD_PAD])
    cur = sb("cur", [128, PADDED])
    nmax = sb("nmax", [ROWS, 2, 2])
    prob = sb("prob", [ROWS, 2, 2, PADDED])
    probT = sb("probT", [ROWS, 2, 2, PADDED])
    sums = sb("psums", [ROWS, 2, 2])
    invs = sb("invs", [ROWS, 2, 2])
    hxT = sb("hxT", [128, 2, PADDED])
    yT = sb("yT", [128, 2, PADDED])
    h2 = sb("h2", [ROWS, 2, 2, DIM])
    stats2 = sb("stats2", [ROWS, 2, 6])
    mv2 = sb("mv2", [ROWS, 2, 2])
    ve2 = sb("ve2", [ROWS, 2])
    rstd2 = sb("rstd2", [ROWS, 2])
    xrow = sb("xrow", [ROWS, 2, 2, XCOLS])
    x1 = sb("f_x1", [FIRST, PADDED])
    x2 = sb("f_x2", [REST, PADDED])
    x1h = sb("f_x1h", [FIRST, PADDED], fp16)
    x1l = sb("f_x1l", [FIRST, PADDED], fp16)
    x2h = sb("f_x2h", [REST, PADDED], fp16)
    x2lh = sb("f_x2lh", [2 * REST, PADDED], fp16)
    tanh = sb("tanh", [ECHUNK, 2, PADDED])
    gated = sb("gated", [ECHUNK, 2, PADDED])
    inter = sb("inter", [ECHUNK, SCHUNKS, PADDED])
    obuf = sb("obuf", [ROWS, 2, 2, DIM])
    elog = sb("elog", [ROWS, 2, EXPERTS])
    sig = sb("sig", [ROWS, 2, EXPERTS])
    choice = sb("choice", [ROWS, 2, EXPERTS + 2])
    struck = sb("struck", [ROWS, 2, EXPERTS + 2])
    top = sb("top", [ROWS, 2, 8])
    mask = sb("mask", [ROWS, 2, EXPERTS], bf16)
    wraw = sb("wraw", [ROWS, 2, EXPERTS])
    wsum = sb("wsum", [ROWS, 2])
    winv = sb("winv", [ROWS, 2])
    place = sb("place", [ROWS, 2, EXPERTS])
    fits = sb("fits", [ROWS, 2, EXPERTS])
    code = sb("code", [ROWS, 2, EXPERTS])
    best = sb("best", [ROWS, 2, 8])
    slot = sb("slot", [ROWS, 2, 2, 8], u32)
    taken = sb("taken", [ROWS, EXPERTS])

    ready = sem("b_ready")
    h_loaded = [sem(f"h_loaded{p}") for p in range(2)]
    cls_in = sem("cls_in")
    ve1_ready = sem("ve1_ready")
    rstd1_ready, hb_ready = sem("rstd1_ready"), sem("hb_ready")
    xn_ready = sem("xn_ready")
    xt_ps, xt_ready = sem("xt_ps"), sem("xt_ready")
    q_ps, q_ready = sem("q_ps"), sem("q_ready")
    k_ps, k_ready = sem("k_ps"), sem("k_ready")
    vv_ps, vv_ready = sem("vv_ps"), sem("vv_ready")
    gqk_ps, gqk_ready = sem("gqk_ps"), sem("gqk_ready")
    gv_ps, gv_ready = sem("gv_ps"), sem("gv_ready")
    s_ps = sem("s_ps")
    max_ready = sem("max_ready")
    p_ready = sem("p_ready")
    pn_ready = sem("pn_ready")
    t_ps = sem("t_ps")
    t_ready = sem("t_ready")
    hx_ps, hx_ready = sem("hx_ps"), sem("hx_ready")
    heads_ps, yt_ready = sem("heads_ps"), sem("yt_ready")
    proj_ps, h2_ready = sem("proj_ps"), sem("h2_ready")
    ve2_ready, rstd2_ready = sem("ve2_ready"), sem("rstd2_ready")
    xn2_ready = sem("xn2_ready")
    x2t_ps, x2t_ready = sem("x2t_ps"), sem("x2t_ready")
    x2high_ready, x2low_ready = sem("x2high_ready"), sem("x2low_ready")
    logit_ps, elog_ready = sem("logit_ps"), sem("elog_ready")
    sig_ready = sem("sig_ready")
    top_ready, mask_ready, winv_ready = sem("top_ready"), sem("mask_ready"), sem("winv_ready")
    count_ps, count_used = sem("count_ps"), sem("count_used")
    slot_ready = sem("slot_ready")
    ff_ps, tanh_ready, inter_ready = sem("ff_ps"), sem("tanh_ready"), sem("inter_ready")
    down_ps, out_ready = sem("down_ps"), sem("out_ready")
    sent = [sem(f"sent{p}") for p in range(2)]
    stored = [sem(f"stored{p}") for p in range(2)]
    c_norm, c_att, c_ffn, c_slot, c_row = (sem(f"c_{n}") for n in ("norm", "att", "ffn", "slot", "row"))
    carrier = sem("b_carrier")
    READY = 10
    N_NORM, N_ATT, N_FFN, N_SLOT, N_ROW = 2, UNITS, 14, 3, 5

    def tiles(bank, rows, width, used=None):
        return PS[0:rows, bank, 0:2 * width].rearrange("p (t k) -> p t k", t=2)[:, :, 0:used or width]

    def both(ap):
        return ap.unsqueeze(1).broadcast_to([ap.shape[0], 2, ap.shape[1]])

    def steps(engine, step):
        step(0, 0, 0, True, False, down=False)
        step(1, 0, 1, True, True, down=False)
        for s in range(2, 4):
            step(s, s // 2, s % 2, True, True)
        with engine.Fori(2, IMAGES // 2 - 1) as k:
            for par in range(2):
                step(2 * k + par, k, par, True, True)
        step(IMAGES - 2, IMAGES // 2 - 1, 0, True, True)
        step(IMAGES - 1, IMAGES // 2 - 1, 1, True, True, last=True)
        step(IMAGES, IMAGES // 2, 0, False, True)
        step(IMAGES + 1, IMAGES // 2, 1, False, False)

    with nc.Block() as block:

        @block.sync
        def _(sp):
            sp.wait_ge(ready, READY)
            for p in range(2):
                sp.dma_start(hin[0:1, p, 0, :], cls_tok).then_inc(cls_in, 16)

            def load(image, p):
                src = image * PATCHES
                sp.dma_start(hin[1:ROWS, p, 0, :], hseq[bass.ds(src, ROWS - 1), :]).then_inc(h_loaded[p], 16)
                sp.dma_start(hin[0:ROWS - 1, p, 1, :], hseq[bass.ds(src + ROWS - 1, ROWS - 1), :]
                             ).then_inc(h_loaded[p], 16)

            def store(f, p):
                sp.wait_ge(out_ready, f + 1)
                sp.dma_start(out[bass.ds(f * TOKENS, ROWS), :], obuf[:, p, 0, :]).then_inc(stored[p], 16)
                sp.dma_start(out[bass.ds(f * TOKENS + ROWS, ROWS - 1), :], obuf[0:ROWS - 1, p, 1, :]
                             ).then_inc(stored[p], 16)

            load(0, 0)
            load(1, 1)

            def step(s, half, par, att, ffn, last=False, down=True):
                if att and not (isinstance(s, int) and s >= IMAGES - 2):
                    sp.wait_ge(xn_ready, s + 1)
                    sp.wait_ge(hb_ready, s + 1)
                    load(s + 2, par)
                if down:
                    store(s - 2, par)

            steps(sp, step)
            for p in range(2):
                sp.wait_ge(stored[p], 32 * (IMAGES // 2))

        @block.gpsimd
        def _(pool):
            nc.gpsimd.memset(hin[:], 0.0).then_inc(ready, 1)
            nc.gpsimd.memset(prob[:], 0.0).then_inc(ready, 1)
            nc.gpsimd.memset(choice[:], 1e30).then_inc(ready, 1)
            nc.gpsimd.memset(taken[:], 0.0).then_inc(ready, 1)
            nc.gpsimd.memset(xrow[:], 0.0).then_inc(ready, 1)
            nc.gpsimd.memset(obuf[:], 0.0).then_inc(ready, 1)

            def norm1(a, half, p):
                pool.wait_ge(ve1_ready, a + 1)
                nc.gpsimd.tensor_tensor(rstd1[:], ve1[:], t["mhalf"][:], ALU.pow).then_inc(rstd1_ready, 1)
                pool.wait_ge(h_loaded[p], 32 * (half + 1))
                need(pool, h2_ready, a - 1)
                nc.gpsimd.tensor_tensor(hb[:, p], hin[:, p], both(t["bproj"][:]), ALU.add).then_inc(hb_ready, 1)

            def dispatch(f, p):
                pool.wait_ge(slot_ready, f + 1)
                pool.sem_inc(carrier, 1)
                for tile in range(2):
                    rows = ROWS - tile
                    for k in range(TOP):
                        nc.gpsimd.indirect_dma_start(
                            xdisp[:, :], bass.IndirectOffsetOnAxis(slot[0:rows, p, tile, k:k + 1], 0),
                            xrow[0:rows, p, tile, :], None, bounds_check=SLOTS - 1, oob_is_err=False
                        ).then_inc(sent[p], 16)

            norm1(0, 0, 0)

            def step(s, half, par, att, ffn, last=False, down=True):
                if ffn:
                    pool.wait_ge(ve2_ready, s)
                    nc.gpsimd.tensor_tensor(rstd2[:], ve2[:], t["mhalf"][:], ALU.pow).then_inc(rstd2_ready, 1)
                if att and not last:
                    norm1(s + 1, half + par, 1 - par)
                if ffn and down:
                    dispatch(s - 2, par)

            steps(pool, step)
            dispatch(IMAGES - 1, 1)
            for p in range(2):
                pool.wait_ge(sent[p], 16 * 2 * TOP * (IMAGES // 2))

        @block.tensor
        def _(pe):
            mm, turn, ident = nc.tensor.matmul, nc.tensor.transpose, t["ident"]

            def product(dst, pairs):
                for n, (l, r) in enumerate(pairs):
                    ins = mm(dst, l, r, start=(n == 0), stop=(n == len(pairs) - 1))
                return ins

            def cols(src, tile):
                return src[:, tile * ROWS:(tile + 1) * ROWS]

            def turn_rows(bank, src, width):
                for c in range(2):
                    for tile in range(2):
                        ins = turn(PS[0:width, bank, c * PADDED + tile * ROWS:c * PADDED + (tile + 1) * ROWS],
                                   src[:, tile, c * width:(c + 1) * width], ident[0:ROWS, 0:ROWS])
                return ins

            def group_qk(bank, g, src):
                for part in range(2):
                    ins = product(PS[0:HALF, bank, part * PADDED:(part + 1) * PADDED],
                                  [(t["wg"][:, g, part, :], src)])
                ins.then_inc(gqk_ps, 1)

            def group_v(bank, g, src):
                for tile in range(2):
                    ins = product(PS[0:ROWS, bank, tile * HALF:(tile + 1) * HALF],
                                  [(cols(src, tile), t["wg"][:, g, 2, :])])
                ins.then_inc(gv_ps, 1)

            def scores(s, n):
                if n >= 2:
                    pe.wait_ge(p_ready, UNITS * s + n - 1)
                elif n == 1:
                    pe.wait_ge(k_ready, s + 1)
                if n in (G0, G1):
                    pe.wait_ge(gqk_ready, 2 * s + 1 + (n == G1))
                    if n == G0:
                        pe.wait_ge(q_ready, s + 1)
                    q, k = gqk[:, 0, :], gqk[:, 1, :]
                else:
                    h = UNIT_HEAD[n]
                    q, k = qT[:, h // 4, h % 4, :], kT[:, h // 4, :]
                for tile in range(2):
                    ins = mm(PS[0:ROWS, n % 2, tile * PADDED:(tile + 1) * PADDED], cols(q, tile), k,
                             start=True, stop=True)
                ins.then_inc(s_ps, 1)

            def turn_probs(s, n):
                pe.wait_ge(pn_ready, UNITS * s + n + 1)
                if n == 0:
                    pe.wait_ge(vv_ready, s + 1)
                for kt in range(2):
                    for tile in range(2):
                        ins = turn(PS[0:ROWS, 2 + n % 2, kt * PADDED + tile * ROWS:kt * PADDED + (tile + 1) * ROWS],
                                   cols(prob[:, n % 2, tile, :], kt), ident[0:ROWS, 0:ROWS])
                ins.then_inc(t_ps, 1)

            def values(s, n):
                pe.wait_ge(t_ready, UNITS * s + n + 1)
                if n in (G0, G1):
                    g = int(n == G1)
                    pe.wait_ge(gv_ready, 2 * s + 1 + g)
                    product(PS[:, 7, 0:PADDED], [(gv[:, kt].rearrange("p h d -> p (h d)"), probT[:, n % 2, kt, :]) for kt in range(2)]
                            ).then_inc(hx_ps, 1)
                    return
                h = UNIT_HEAD[n]
                if h == 0:
                    need(pe, h2_ready, s)
                at, blk = (h % 4) * HEAD_PAD, h // 4
                ins = product(PS[at:at + HEAD_PAD, 4, blk * PADDED:(blk + 1) * PADDED],
                              [(vn[:, kt, h, :], probT[:, n % 2, kt, :]) for kt in range(2)])
                if h == HEADS - 1:
                    ins.then_inc(heads_ps, 1)

            def ffn_chunk(s, j):
                if j >= 2:
                    pe.wait_ge(inter_ready, SCHUNKS * (s - 1) + j - 1)
                elif j == 1:
                    pe.wait_ge(elog_ready, s)
                c = slice(j * ECHUNK, (j + 1) * ECHUNK)
                w1h, w1l, w2hl = t["ws1h"], t["ws1l"], t["ws2hl"]
                for kind in range(2):
                    ins = product(PS[0:ECHUNK, 5 + j % 2, kind * PADDED:(kind + 1) * PADDED],
                                  [(w1h[:, kind, c], x1h[:]), (w1h[:, kind, c], x1l[:]), (w1l[:, kind, c], x1h[:]),
                                   (w2hl[0:REST, kind, c], x2h[:]), (w2hl[:, kind, c], x2lh[:])])
                ins.then_inc(ff_ps, 1)

            DOWN_PARTS = (3, 7, 11, 2 * SCHUNKS)

            def down_part(s, first, end):
                if first == 0:
                    pe.wait_ge(inter_ready, SCHUNKS * (s - 1))
                for m in range(first, end):
                    tile, j = m // SCHUNKS, m % SCHUNKS
                    ins = mm(PS[0:ROWS, 6, tile * DIM:(tile + 1) * DIM], cols(inter[:, j, :], tile), t["wsd"][:, j, :],
                             start=(j == 0), stop=(j == SCHUNKS - 1))
                if end == 2 * SCHUNKS:
                    ins.then_inc(down_ps, 1)

            def turn_tokens(a):
                pe.wait_ge(xn_ready, a + 1)
                need(pe, hx_ready, 2 * a)
                turn_rows(7, xn[:].rearrange("p t c h d -> p t (c h d)"), 128).then_inc(xt_ps, 1)

            turn_tokens(0)

            def step(s, half, par, att, ffn, last=False, down=True):
                if down:
                    down_part(s, 0, DOWN_PARTS[0])
                if att:
                    pe.wait_ge(xt_ready, s + 1)
                    need(pe, p_ready, UNITS * s)
                    for blk in range(2):
                        ins = product(PS[:, 0, blk * PADDED:(blk + 1) * PADDED],
                                      [(t["wq"][:, c, blk].rearrange("p h d -> p (h d)"), xT[:, c, :]) for c in range(2)])
                    ins.then_inc(q_ps, 1)
                if att:
                    need(pe, t_ready, UNITS * s)
                    group_qk(3, 0, xT[:, 0, :])
                    for blk in range(2):
                        ins = product(PS[:, 1, blk * PADDED:(blk + 1) * PADDED],
                                      [(t["wk"][:, c, blk].rearrange("p h d -> p (h d)"), xT[:, c, :]) for c in range(2)])
                    ins.then_inc(k_ps, 1)
                if ffn:
                    pe.wait_ge(yt_ready, s)
                    for tile in range(2):
                        ins = product(PS[0:ROWS, 4, tile * DIM:(tile + 1) * DIM],
                                      [(cols(yT[:, c, :], tile), t["wp"][:, c, :]) for c in range(2)])
                    ins.then_inc(proj_ps, 1)
                if att:
                    for tile in range(2):
                        ins = product(PS[0:ROWS, 2, tile * DIM:(tile + 1) * DIM],
                                      [(cols(xT[:, c, :], tile), t["wv"][:, c, :]) for c in range(2)])
                    ins.then_inc(vv_ps, 1)
                    group_v(7, 0, xT[:, 0, :])
                if att:
                    scores(s, 0)
                for n in range(UNITS + 2):
                    if att and n == 4:
                        pe.wait_ge(hx_ready, 2 * s + 1)
                        group_qk(7, 1, cur[:])
                    if down and n < FF_SLOT:
                        down_part(s, DOWN_PARTS[n], DOWN_PARTS[n + 1])
                    if ffn:
                        if n == 1:
                            pe.wait_ge(xn2_ready, s)
                            need(pe, count_used, s - 1)
                            for at, width, col in ((0, FIRST, 0), (FIRST, REST, PADDED)):
                                for tile in range(2):
                                    ins = turn(PS[0:width, 5, col + tile * ROWS:col + (tile + 1) * ROWS],
                                               xrow[:, 1 - par, tile, at:at + width], ident[0:ROWS, 0:ROWS])
                            ins.then_inc(x2t_ps, 1)
                        if n == FF_SLOT:
                            pe.wait_ge(x2t_ready, s)
                            need(pe, out_ready, s - 1)
                            for tile in range(2):
                                ins = product(PS[0:ROWS, 6, tile * EXPERTS:(tile + 1) * EXPERTS],
                                              [(cols(x1, tile), t["wgate1"][:]), (cols(x2, tile), t["wgate2"][:])])
                            ins.then_inc(logit_ps, 1)
                            pe.wait_ge(x2low_ready, s)
                            ffn_chunk(s, 0)
                        if FF_SLOT < n < FF_SLOT + SCHUNKS:
                            ffn_chunk(s, n - FF_SLOT)
                    if att and 2 <= n <= UNITS:
                        values(s, n - 2)
                    if att and n < UNITS - 1:
                        scores(s, n + 1)
                    if att and 1 <= n <= UNITS:
                        turn_probs(s, n - 1)
                    if att and n == 4:
                        pe.wait_ge(gqk_ready, 2 * s + 2)
                        group_v(7, 1, cur[:])
                    if ffn and n == UNITS + 1:
                        pe.wait_ge(mask_ready, s)
                        pe.wait_ge(inter_ready, SCHUNKS * s - 1)
                        tri, ones = t["tri"], t["ones"]
                        first, second = mask[:, 0, :], mask[0:ROWS - 1, 1, :]
                        product(PS[0:ROWS, 5, 0:EXPERTS], [(tri[:], first)])
                        product(PS[0:ROWS, 5, EXPERTS:2 * EXPERTS], [(ones[:], first), (tri[0:ROWS - 1, :], second)])
                        product(PS[0:ROWS, 5, 2 * EXPERTS:3 * EXPERTS],
                                [(ones[:], first), (ones[0:ROWS - 1, :], second)]).then_inc(count_ps, 1)
                    if att and n == UNITS + 1:
                        if not last:
                            turn_tokens(s + 1)
                        values(s, UNITS - 1)

            steps(pe, step)

        @block.scalar
        def _(act):
            act.wait_ge(ready, READY)

            def copy(dst, src):
                return nc.scalar.activation(dst, src, ACT.Copy)

            def group_values():
                return copy(gv[:, :, :, 0:HEAD_DIM],
                            tiles(7, ROWS, HALF).rearrange("p t (h d) -> p t h d", d=HEAD_DIM))

            def turned_tokens(a):
                act.wait_ge(xt_ps, a + 1)
                copy(xT[:], tiles(7, 128, PADDED)).then_inc(xt_ready, 1)

            turned_tokens(0)

            def step(s, half, par, att, ffn, last=False, down=True):
                if att:
                    act.wait_ge(q_ps, s + 1)
                    for h in range(4):
                        at = slice(h * HEAD_PAD, (h + 1) * HEAD_PAD)
                        ins = copy(qT[at, :, h, :], tiles(0, 128, PADDED)[at])
                    ins.then_inc(q_ready, 1)
                    act.wait_ge(vv_ps, s + 1)
                    copy(vn[:, :, :, 0:HEAD_DIM], tiles(2, ROWS, DIM).rearrange("p t (h d) -> p t h d", d=HEAD_DIM)
                         ).then_inc(vv_ready, 1)
                    act.wait_ge(gv_ps, 2 * s + 1)
                    group_values().then_inc(gv_ready, 1)
                for n in range(UNITS + 2):
                    if att and n < UNITS:
                        act.wait_ge(max_ready, UNITS * s + n + 1)
                        for tile in range(2):
                            ins = nc.scalar.activation(prob[:, n % 2, tile, 0:TOKENS],
                                                       tiles(n % 2, ROWS, PADDED, TOKENS)[:, tile, :], ACT.Exp,
                                                       bias=nmax[:, n % 2, tile:tile + 1], accum_out=sums[:, n % 2, tile:tile + 1])
                        ins.then_inc(p_ready, 1)
                    if ffn and n == FF_SLOT:
                        act.wait_ge(logit_ps, s)
                        nc.scalar.activation(elog[:], tiles(6, ROWS, EXPERTS), ACT.Exp, scale=-1.0
                                             ).then_inc(elog_ready, 1)
                    if ffn and FF_SLOT <= n < FF_SLOT + SCHUNKS:
                        j = n - FF_SLOT
                        act.wait_ge(ff_ps, SCHUNKS * (s - 1) + j + 1)
                        nc.scalar.activation(tanh[:, j % 2, :], PS[0:ECHUNK, 5 + j % 2, 0:PADDED], ACT.Tanh,
                                             scale=0.5 / SPLIT).then_inc(tanh_ready, 1)
                    if att and 1 <= n <= UNITS:
                        act.wait_ge(t_ps, UNITS * s + n)
                        copy(probT[:, (n - 1) % 2], tiles(2 + (n - 1) % 2, ROWS, PADDED)).then_inc(t_ready, 1)
                    if ffn and n == 1:
                        act.wait_ge(x2t_ready, s)
                        copy(x1h[:], x1[:])
                        copy(x2h[:], x2[:])
                        copy(x2lh[REST:2 * REST], x2[:]).then_inc(x2high_ready, 1)
                    if att and n == 5:
                        act.wait_ge(gv_ps, 2 * s + 2)
                        group_values().then_inc(gv_ready, 1)
                if att and not last:
                    turned_tokens(s + 1)

            steps(act, step)

        @block.vector
        def _(dve):
            V = nc.vector
            for spread in (xn, qT, vn, gv):
                V.memset(spread[:], 0.0).then_inc(ready, 1)
            dve.wait_ge(ready, READY)
            dve.wait_ge(cls_in, 32)

            def stats(chain, src, st, mv, ve, done):
                for tile in range(2):
                    last = V.bn_stats(st[:, tile], src[:, tile])
                chain.link(last, carrier)
                for tile in range(2):
                    last = V.bn_aggr(mv[:, tile], st[:, tile])
                chain.link(last)
                V.tensor_scalar(ve[:], mv[:, :, 1], 1e-5, None, ALU.add).then_inc(done, 1)

            def norm1_stats(a, half, p):
                chain = Steps(dve, c_norm, N_NORM * a)
                dve.wait_ge(h_loaded[p], 32 * (half + 1))
                stats(chain, hin[:, p], stats1, mv1, ve1, ve1_ready)
                return chain

            def norm1_apply(a, p, chain):
                dve.wait_ge(rstd1_ready, a + 1)
                need(dve, xt_ps, a)
                for tile in range(2):
                    last = V.tensor_scalar(xn[:, tile].rearrange("p c h d -> p (c h) d")[:, :, 0:HEAD_DIM],
                                           hin[:, p, tile].rearrange("p (h d) -> p h d", d=HEAD_DIM), mv1[:, tile, 0:1], rstd1[:, tile:tile + 1],
                                           ALU.subtract, ALU.mult)
                last.then_inc(xn_ready, 1)
                assert chain.n == N_NORM

            def normalise_and_gate(s, n, j):
                if n is not None:
                    dve.wait_ge(p_ready, UNITS * s + n + 1)
                    inverted = chain_att.mark(V.reciprocal(invs[:, n % 2], sums[:, n % 2]))
                if j is not None:
                    bank = 5 + j % 2
                    g, u = PS[0:ECHUNK, bank, 0:PADDED], PS[0:ECHUNK, bank, PADDED:2 * PADDED]
                    dve.wait_ge(tanh_ready, SCHUNKS * (s - 1) + j + 1)
                    gated_ready = ffn_chain.mark(
                        V.scalar_tensor_tensor(gated[:, j % 2, :], tanh[:, j % 2, :], 1.0, g, ALU.add, ALU.mult))
                if n is not None:
                    chain_att.wait(inverted)
                    p = prob[:, n % 2, :, 0:TOKENS]
                    V.tensor_tensor(p, p, invs[:, n % 2].unsqueeze(2).broadcast_to([ROWS, 2, TOKENS]), ALU.mult
                                    ).then_inc(pn_ready, 1)
                if j is not None:
                    ffn_chain.wait(gated_ready)
                    V.tensor_tensor(inter[:, j, :], gated[:, j % 2, :], u, ALU.mult).then_inc(inter_ready, 1)

            def sigmoid(s, piece):
                if piece == 0:
                    dve.wait_ge(elog_ready, s)
                    ffn_chain.link(V.tensor_scalar(elog[:], elog[:], 1.0, None, ALU.add))
                tile, c = piece // 2, slice(piece % 2 * EXPERTS // 2, (piece % 2 + 1) * EXPERTS // 2)
                V.reciprocal(sig[:, tile, c], elog[:, tile, c]).then_inc(sig_ready, 1)

            def choose(s):
                dve.wait_ge(sig_ready, 4 * s)
                return ffn_chain.mark(V.tensor_tensor(choice[:, :, 0:EXPERTS], sig[:], both(t["ebias"][:]), ALU.add))

            def best_choices(chosen_at):
                ffn_chain.wait(chosen_at)
                dve.sem_inc(carrier, 1)
                V.max(top[:, 0], choice[:, 0])
                V.max(top[:, 1], choice[:, 1]).then_inc(top_ready, 1)

            def strike(s):
                dve.wait_ge(top_ready, s)
                dve.sem_inc(carrier, 1)
                V.match_replace(struck[:, 0], top[:, 0], choice[:, 0], -1e30)
                return ffn_chain.mark(V.match_replace(struck[:, 1], top[:, 1], choice[:, 1], -1e30))

            def fill_mask(struck_at):
                ffn_chain.wait(struck_at)
                V.tensor_scalar(mask[:], struck[:, :, 0:EXPERTS], -1e29, None, ALU.is_lt).then_inc(mask_ready, 1)

            def weigh(f):
                link = row_chain.link
                dve.wait_ge(mask_ready, f + 1)
                link(V.tensor_tensor(wraw[:], sig[:], mask[:], ALU.mult))
                link(V.tensor_reduce(wsum[:], wraw[:], AX.X, ALU.add))
                link(V.tensor_scalar(wsum[:], wsum[:], 1e-20, None, ALU.add))
                V.reciprocal(winv[:], wsum[:]).then_inc(winv_ready, 1)

            def fill_rows(f, p):
                dve.wait_ge(winv_ready, f + 1)
                for tile in range(2):
                    V.tensor_scalar(xrow[:, p, tile, DIM:DIM + EXPERTS], wraw[:, tile], winv[:, tile:tile + 1],
                                    ROUTE_SCALE, ALU.mult, ALU.mult)
                row_chain.link(V.tensor_copy(xrow[:, p, :, XCOLS - 1], t["tid"][:]))
                row_chain.link(V.tensor_scalar(t["tid"][:], t["tid"][:], float(TOKENS), None, ALU.add))
                assert row_chain.n == N_ROW

            def place_tokens(s):
                link = ffn_chain.link
                dve.wait_ge(count_ps, s)
                link(V.tensor_tensor(place[:], tiles(5, ROWS, EXPERTS), both(taken[:]), ALU.add))
                V.tensor_tensor(taken[:], taken[:], PS[0:ROWS, 5, 2 * EXPERTS:3 * EXPERTS], ALU.add
                                ).then_inc(count_used, 1)

            def choose_slots(f, p, piece):
                chain = Steps(dve, c_slot, N_SLOT * f + piece)
                if piece == 0:
                    dve.wait_ge(count_used, f + 1)
                    V.scalar_tensor_tensor(fits[:], place[:], float(CAP), mask[:], ALU.is_lt, ALU.mult)
                    chain.mark(V.tensor_tensor(code[:], both(t["rbase"][:]), place[:], ALU.subtract))
                    return
                chain.wait(0)
                if piece == 1:
                    chain.mark(V.tensor_tensor(code[:], code[:], fits[:], ALU.mult))
                if piece == 2:
                    dve.sem_inc(carrier, 1)
                    V.max(best[:, 0], code[:, 0])
                    chain.mark(V.max(best[:, 1], code[:, 1]))
                if piece == 3:
                    V.tensor_scalar(slot[:, p], best[:], -1.0, SLOT_TOP, ALU.mult, ALU.add).then_inc(slot_ready, 1)

            ffn_chain = chain_att = row_chain = parf = None

            def step(s, half, par, att, ffn, last=False, down=True):
                nonlocal ffn_chain, chain_att, row_chain, parf
                parf = 1 - par
                half_f = half if par else half - 1
                ffn_chain = Steps(dve, c_ffn, N_FFN * (s - 1))
                chain_att = Steps(dve, c_att, N_ATT * s)
                row_chain = Steps(dve, c_row, N_ROW * (s - 2))
                if att:
                    dve.wait_ge(gqk_ps, 2 * s + 1)
                    V.tensor_copy(gqk[:], tiles(3, HALF, PADDED)).then_inc(gqk_ready, 1)
                    dve.wait_ge(k_ps, s + 1)
                    V.tensor_copy(kT[:], tiles(1, 128, PADDED)).then_inc(k_ready, 1)
                    if not last:
                        next_norm = norm1_stats(s + 1, half + par, 1 - par)
                if ffn:
                    dve.wait_ge(proj_ps, s)
                    dve.wait_ge(hb_ready, s)
                    V.tensor_tensor(h2[:, parf], tiles(4, ROWS, DIM), hb[:, parf], ALU.add).then_inc(h2_ready, 1)
                    dve.wait_ge(h2_ready, s)
                    stats(ffn_chain, h2[:, parf], stats2, mv2, ve2, ve2_ready)
                for n in range(UNITS + 2):
                    if att and n < UNITS:
                        dve.wait_ge(s_ps, UNITS * s + n + 1)
                        V.tensor_reduce(nmax[:, n % 2, :], tiles(n % 2, ROWS, PADDED, TOKENS), AX.X, ALU.max,
                                        negate=True).then_inc(max_ready, 1)
                    if att and n == 4:
                        dve.wait_ge(gqk_ps, 2 * s + 2)
                        V.tensor_copy(gqk[:], tiles(7, HALF, PADDED)).then_inc(gqk_ready, 1)
                    normalise_and_gate(s, n - 1 if att and 1 <= n <= UNITS else None,
                                       n - 1 - FF_SLOT if ffn and FF_SLOT < n <= FF_SLOT + SCHUNKS else None)
                    if ffn and n == 0:
                        dve.wait_ge(rstd2_ready, s)
                        need(dve, sent[parf], 32 * TOP * half_f)
                        for tile in range(2):
                            ins = V.tensor_scalar(xrow[:, parf, tile, 0:DIM], h2[:, parf, tile], mv2[:, tile, 0:1],
                                                  rstd2[:, tile:tile + 1], ALU.subtract, ALU.mult)
                        ins.then_inc(xn2_ready, 1)
                    if ffn and n == 2:
                        dve.wait_ge(x2high_ready, s)
                        V.tensor_tensor(x1l[:], x1[:], x1h[:], ALU.subtract)
                        V.tensor_tensor(x2lh[0:REST], x2[:], x2h[:], ALU.subtract).then_inc(x2low_ready, 1)
                    if down and n == 2:
                        dve.wait_ge(down_ps, s - 1)
                        need(dve, stored[par], 32 * (half - 1))
                        V.scalar_tensor_tensor(obuf[:, par], tiles(6, ROWS, DIM), 0.5 / (SPLIT * SPLIT), h2[:, par], ALU.mult, ALU.add
                                               ).then_inc(out_ready, 1)
                    if ffn and n == 1:
                        dve.wait_ge(x2t_ps, s)
                        V.tensor_copy(x1[:], PS[0:FIRST, 5, 0:PADDED])
                        V.tensor_copy(x2[:], PS[0:REST, 5, PADDED:2 * PADDED]).then_inc(x2t_ready, 1)
                    if down and 2 <= n < 6:
                        choose_slots(s - 2, par, n - 2)
                    if down and n == 0:
                        weigh(s - 2)
                    if down and n == 1:
                        fill_rows(s - 2, par)
                    if att and n == 3:
                        dve.wait_ge(hx_ps, 2 * s + 1)
                        V.tensor_copy(hxT[:, 0], PS[:, 7, 0:PADDED])
                        V.tensor_tensor(cur[:], xT[:, 1], PS[:, 7, 0:PADDED], ALU.add).then_inc(hx_ready, 1)
                    if att and n == 9:
                        dve.wait_ge(hx_ps, 2 * s + 2)
                        V.tensor_copy(hxT[:, 1], PS[:, 7, 0:PADDED]).then_inc(hx_ready, 1)
                    if ffn:
                        if 4 <= n < 8:
                            sigmoid(s, n - 4)
                        if n == 7:
                            chosen_at = choose(s)
                        if n == 8:
                            best_choices(chosen_at)
                            struck_at = strike(s)
                        if n == 9:
                            fill_mask(struck_at)
                    if att and not last and n == 10:
                        norm1_apply(s + 1, 1 - par, next_norm)
                if att:
                    dve.wait_ge(heads_ps, s + 1)
                    V.tensor_tensor(yT[:], tiles(4, 128, PADDED), hxT[:], ALU.add).then_inc(yt_ready, 1)
                    assert chain_att.n == N_ATT
                if ffn:
                    place_tokens(s)
                    assert ffn_chain.n == N_FFN, ffn_chain.n

            norm1_apply(0, 0, norm1_stats(0, 0, 0))
            steps(dve, step)

    ctx.close()


def experts(nc, PS, t, Wgu, Wd, xdisp, out):
    ctx = ExitStack()

    def sb(name, shape, dt=fp32):
        return ctx.enter_context(nc.sbuf_tensor(name, shape, dt))

    def sem(name):
        return ctx.enter_context(nc.semaphore(name))

    KIND = EHID
    w1 = sb("e_w1", [FIRST, 2, 2, KIND])
    w2 = sb("e_w2", [REST, 2, 2, KIND])
    wd = sb("e_wd", [ECHUNK, 2, ECHUNKS, DIM])
    w1h = sb("e_w1h", [FIRST, 2, 2, KIND], fp16)
    w1l = sb("e_w1l", [FIRST, 2, 2, KIND], fp16)
    w2hl = sb("e_w2hl", [2 * REST, 2, 2, KIND], fp16)
    wdh = sb("e_wdh", [ECHUNK, 2, ECHUNKS, DIM], fp16)
    wdl = sb("e_wdl", [ECHUNK, 2, ECHUNKS, DIM], fp16)
    xb = sb("e_xb", [HALF, 2, 2, DIM])
    wt = sb("e_wt", [HALF, 2, 2])
    tok = sb("e_tok", [HALF, 2, 2])
    tokn = sb("e_tokn", [HALF, 2, 2], u32)
    x1h = sb("e_x1h", [FIRST, 2, CAP], fp16)
    x1l = sb("e_x1l", [FIRST, 2, CAP], fp16)
    x2h = sb("e_x2h", [REST, 2, CAP], fp16)
    x2lh = sb("e_x2lh", [2 * REST, 2, CAP], fp16)
    act_g = sb("e_act", [ECHUNK, 2, 2, CAP])
    inter = sb("e_inter", [ECHUNK, 2, 2, CAP])
    ih = sb("e_ih", [ECHUNK, 2, ECHUNKS, CAP], fp16)
    il = sb("e_il", [ECHUNK, 2, ECHUNKS, CAP], fp16)
    yb = sb("e_yb", [HALF, 2, 2, DIM])

    w_in = [sem(f"w_in{p}") for p in range(2)]
    d_in = [sem(f"d_in{p}") for p in range(2)]
    x_in = [sem(f"x_in{p}") for p in range(2)]
    r_in = [sem(f"r_in{p}") for p in range(2)]
    high_w = [sem(f"high_w{m}") for m in range(2)]
    low_w = [sem(f"low_w{m}") for m in range(2)]
    high_d, low_d = sem("high_d"), sem("low_d")
    xt_ps, high_x, low_x = sem("e_xt_ps"), sem("high_x"), sem("low_x")
    up_ps = sem("e_up_ps")
    silu_sb, gate_sb = sem("silu_sb"), sem("gate_sb")
    high_i = sem("high_i")
    low_i = [sem(f"low_i{m}") for m in range(2)]
    y_ps, y_sb = sem("y_ps"), sem("y_sb")
    tok_sb = sem("tok_sb")
    added = sem("added")
    carrier = sem("e_carrier")
    BX, BG, BU, BY = 0, 1, 3, 5

    def steps(engine, step):
        step(0, 0, 0, first=True)
        for e in range(1, 4):
            step(e, e // 2, e % 2)
        with engine.Fori(2, EXPERTS // 2 - 1) as k:
            for par in range(2):
                step(2 * k + par, k, par)
        step(EXPERTS - 2, EXPERTS // 2 - 1, 0)
        step(EXPERTS - 1, EXPERTS // 2 - 1, 1, last=True)

    def pair(w, p, m):
        return w[:, p, :, 2 * m * ECHUNK:2 * (m + 1) * ECHUNK]

    with nc.Block() as block:

        @block.sync
        def _(sp):
            rows = xdisp.rearrange("(e t p) c -> e p t c", t=2, p=HALF)
            dn = Wd.rearrange("e (j p) d -> e p j d", p=ECHUNK)

            def load_rows(e, p):
                sp.dma_start(xb[:, p], rows[bass.ds(e, 1)][:, :, :, 0:DIM].rearrange("e p t c -> (e p) t c")
                             ).then_inc(x_in[p], 16)

            def load_up(e, p):
                up = Wgu[bass.ds(e, 1)].rearrange("e p (k f) -> (e p) k f", k=2)
                sp.dma_start(w1[:, p], up[0:FIRST]).then_inc(w_in[p], 16)
                sp.dma_start(w2[:, p], up[FIRST:DIM]).then_inc(w_in[p], 16)

            def load_down(e, p):
                sp.dma_start(wd[:, p], dn[bass.ds(e, 1)].rearrange("e p j d -> (e p) j d")).then_inc(d_in[p], 16)

            def load_columns(e, p):
                src = xdisp[bass.ds(e * CAP, CAP), :].rearrange("(t p) c -> p t c", p=HALF)
                sp.dma_start(wt[:, p], src[:, :, bass.ds(DIM + e, 1)].rearrange("p t o -> p (t o)"),
                             allow_slow_non_contiguous=True).then_inc(r_in[p], 16)
                sp.dma_start(tok[:, p], rows[bass.ds(e, 1)][:, :, :, XCOLS - 1].rearrange("e p t -> (e p) t"),
                             allow_slow_non_contiguous=True).then_inc(r_in[p], 16)

            for e in range(2):
                load_rows(e, e)
                load_up(e, e)
                load_down(e, e)
            load_columns(0, 0)

            def step(e, half, par, first=False, last=False):
                loads = not (isinstance(e, int) and e >= EXPERTS - 2)
                if loads:
                    sp.wait_ge(xt_ps, e + 1)
                    load_rows(e + 2, par)
                    sp.wait_ge(low_w[1], e + 1)
                    load_up(e + 2, par)
                if not last:
                    need(sp, y_sb, e)
                    need(sp, tok_sb, e)
                    load_columns(e + 1, 1 - par)
                if loads:
                    sp.wait_ge(low_d, e + 1)
                    load_down(e + 2, par)

            steps(sp, step)

        @block.tensor
        def _(pe):
            mm, turn, ident = nc.tensor.matmul, nc.tensor.transpose, t["ident"]

            def product(dst, pairs):
                for n, (l, r) in enumerate(pairs):
                    ins = mm(dst, l, r, start=(n == 0), stop=(n == len(pairs) - 1))
                return ins

            def turn_slots(e, half, p):
                pe.wait_ge(x_in[p], 16 * (half + 1))
                need(pe, low_x, e)
                for at, width, col in ((0, FIRST, 0), (FIRST, REST, CAP)):
                    for tile in range(2):
                        ins = turn(PS[0:width, BX, col + tile * HALF:col + (tile + 1) * HALF],
                                   xb[:, p, tile, at:at + width], ident[0:HALF, 0:HALF])
                ins.then_inc(xt_ps, 1)

            def up(e, p, m):
                pe.wait_ge(low_w[m], e + 1)
                if m == 0:
                    pe.wait_ge(low_x, e + 1)
                need(pe, gate_sb, 2 * (e - 1) + m + 1)
                for kind, bank in enumerate((BG + m, BU + m)):
                    for j in range(2):
                        c = slice((2 * m + j) * ECHUNK, (2 * m + j + 1) * ECHUNK)
                        ins = product(PS[0:ECHUNK, bank, j * CAP:(j + 1) * CAP],
                                      [(w1h[:, p, kind, c], x1h[:, p]), (w1h[:, p, kind, c], x1l[:, p]),
                                       (w1l[:, p, kind, c], x1h[:, p]),
                                       (w2hl[0:REST, p, kind, c], x2h[:, p]), (w2hl[:, p, kind, c], x2lh[:, p])])
                ins.then_inc(up_ps, 1)

            def down(e, p):
                pe.wait_ge(low_d, e + 1)
                need(pe, y_sb, e)
                for tile in range(2):
                    s = slice(tile * HALF, (tile + 1) * HALF)
                    for j in range(ECHUNKS):
                        if tile == 0 and j % 2 == 0:
                            pe.wait_ge(low_i[j // 2], e + 1)
                        for part, (l, r) in enumerate(((ih, wdh), (ih, wdl), (il, wdh))):
                            ins = mm(PS[0:HALF, BY, tile * DIM:(tile + 1) * DIM], l[:, p, j, s], r[:, p, j, :],
                                     start=(j == 0 and part == 0), stop=(j == ECHUNKS - 1 and part == 2))
                ins.then_inc(y_ps, 1)

            def step(e, half, par, first=False, last=False):
                if not last:
                    turn_slots(e + 1, half + par, 1 - par)
                up(e, par, 0)
                if not first:
                    down(e - 1, 1 - par)
                up(e, par, 1)

            turn_slots(0, 0, 0)
            steps(pe, step)
            down(EXPERTS - 1, 1)

        @block.scalar
        def _(act):
            def copy(dst, src, scale=1.0):
                return nc.scalar.activation(dst, src, ACT.Copy, scale=scale)

            def high_up(half, p, m):
                if m == 0:
                    act.wait_ge(w_in[p], 32 * (half + 1))
                copy(pair(w1h, p, m), pair(w1, p, m), SPLIT)
                copy(pair(w2hl[0:REST], p, m), pair(w2, p, m), SPLIT).then_inc(high_w[m], 1)

            def high_down(half, p):
                act.wait_ge(d_in[p], 16 * (half + 1))
                copy(wdh[:, p], wd[:, p], SPLIT).then_inc(high_d, 1)

            def high_rows(e, p):
                act.wait_ge(xt_ps, e + 1)
                copy(x1h[:, p], PS[0:FIRST, BX, 0:CAP])
                copy(x2h[:, p], PS[0:REST, BX, CAP:2 * CAP])
                copy(x2lh[REST:2 * REST, p], PS[0:REST, BX, CAP:2 * CAP]).then_inc(high_x, 1)

            def silu(e, m):
                act.wait_ge(up_ps, 2 * e + m + 1)
                nc.scalar.activation(act_g[:, m], PS[0:ECHUNK, BG + m, 0:2 * CAP].rearrange("p (j s) -> p j s", j=2),
                                     ACT.Silu, scale=1.0 / SPLIT).then_inc(silu_sb, 1)

            def high_inter(e, p, m):
                act.wait_ge(gate_sb, 2 * e + m + 1)
                copy(ih[:, p, 2 * m:2 * m + 2], inter[:, m]).then_inc(high_i, 1)

            high_rows(0, 0)
            high_up(0, 0, 0)

            def step(e, half, par, first=False, last=False):
                if not first:
                    silu(e - 1, 1)
                if not last:
                    high_rows(e + 1, 1 - par)
                if not first:
                    high_inter(e - 1, 1 - par, 1)
                high_up(half, par, 1)
                silu(e, 0)
                if not last:
                    high_up(half + par, 1 - par, 0)
                high_inter(e, par, 0)
                need(act, y_ps, e - 1)
                high_down(half, par)

            steps(act, step)
            silu(EXPERTS - 1, 1)
            high_inter(EXPERTS - 1, 1, 1)

        @block.vector
        def _(dve):
            V = nc.vector

            def low_up(e, p, m):
                dve.wait_ge(high_w[m], e + 1)
                V.scalar_tensor_tensor(pair(w1l, p, m), pair(w1, p, m), SPLIT, pair(w1h, p, m), ALU.mult, ALU.subtract)
                V.scalar_tensor_tensor(pair(w2hl[REST:2 * REST], p, m), pair(w2, p, m), SPLIT,
                                       pair(w2hl[0:REST], p, m), ALU.mult, ALU.subtract).then_inc(low_w[m], 1)

            def low_down(e, p):
                dve.wait_ge(high_d, e + 1)
                V.scalar_tensor_tensor(wdl[:, p], wd[:, p], SPLIT, wdh[:, p], ALU.mult, ALU.subtract).then_inc(low_d, 1)

            def low_rows(e, p):
                dve.wait_ge(high_x, e + 1)
                V.tensor_tensor(x1l[:, p], PS[0:FIRST, BX, 0:CAP], x1h[:, p], ALU.subtract)
                V.tensor_tensor(x2lh[0:REST, p], PS[0:REST, BX, CAP:2 * CAP], x2h[:, p], ALU.subtract).then_inc(low_x, 1)

            def gate(e, m):
                if m == 0:
                    need(dve, low_i[0], e)
                dve.wait_ge(silu_sb, 2 * e + m + 1)
                V.tensor_tensor(inter[:, m], act_g[:, m], PS[0:ECHUNK, BU + m, 0:2 * CAP].rearrange(
                    "p (j s) -> p j s", j=2), ALU.mult).then_inc(gate_sb, 1)

            def low_inter(e, p):
                dve.wait_ge(high_i, 2 * e + 2)
                V.tensor_tensor(il[:, p, 2:4], inter[:, 1], ih[:, p, 2:4], ALU.subtract).then_inc(low_i[1], 1)

            def result(e, half, p):
                dve.wait_ge(y_ps, e + 1)
                dve.wait_ge(r_in[p], 32 * (half + 1))
                need(dve, added, 32 * (e - 1))
                V.tensor_copy(tokn[:, p], tok[:, p]).then_inc(tok_sb, 1)
                V.scalar_tensor_tensor(yb[:, p], PS[0:HALF, BY, 0:2 * DIM].rearrange("p (t d) -> p t d", t=2),
                                       1.0 / (SPLIT * SPLIT), wt[:, p].unsqueeze(2).broadcast_to([HALF, 2, DIM]),
                                       ALU.mult, ALU.mult).then_inc(y_sb, 1)

            low_rows(0, 0)
            low_up(0, 0, 0)

            def step(e, half, par, first=False, last=False):
                if not first:
                    gate(e - 1, 1)
                if not last:
                    low_rows(e + 1, 1 - par)
                if not first:
                    low_inter(e - 1, 1 - par)
                low_up(e, par, 1)
                gate(e, 0)
                if not last:
                    low_up(e + 1, 1 - par, 0)
                if not first:
                    result(e - 1, half if par else half - 1, 1 - par)
                low_down(e, par)

            steps(dve, step)
            gate(EXPERTS - 1, 1)
            low_inter(EXPERTS - 1, 1)
            result(EXPERTS - 1, EXPERTS // 2 - 1, 1)

        @block.gpsimd
        def _(pool):
            def low_inter(e, p):
                pool.wait_ge(high_i, 2 * e + 1)
                nc.gpsimd.tensor_tensor(il[:, p, 0:2], inter[:, 0], ih[:, p, 0:2], ALU.subtract).then_inc(low_i[0], 1)

            def add(e, p):
                pool.wait_ge(y_sb, e + 1)
                pool.sem_inc(carrier, 1)
                if not (isinstance(e, int) and e == 0):
                    pool.wait_ge(added, 32 * e)
                    pool.sem_inc(carrier, 1)
                for tile in range(2):
                    nc.gpsimd.indirect_dma_start(
                        out[:, :], bass.IndirectOffsetOnAxis(tokn[:, p, tile:tile + 1], 0), yb[:, p, tile, :],
                        None, bounds_check=NTOK + CAP - 1, oob_is_err=True, compute_op=ALU.add).then_inc(added, 16)

            def step(e, half, par, first=False, last=False):
                low_inter(e, par)
                if not first:
                    add(e - 1, 1 - par)

            steps(pool, step)
            add(EXPERTS - 1, 1)
            pool.wait_ge(added, 32 * EXPERTS)

    ctx.close()


def program(nc, x, cls_tok, z, pos_enc, w_qkv, w_g0, w_g1, w_proj, b_proj, Wg, e_bias, Wgu, Wd, Wsg, Wsu, Wsd, out):
    with ExitStack() as ctx:
        hseq = nc.dram_tensor("hseq", [IMAGES * PATCHES, DIM], fp32, kind="Internal").ap()
        xdisp = nc.dram_tensor("xdisp", [SLOTS, XCOLS], fp32, kind="Internal").ap()
        PS = ctx.enter_context(nc.psum_tensor("PS", [128, 8, 512], fp32))
        shapes = {
            "ident": [128, 128], "rbase": [ROWS, EXPERTS], "tid": [ROWS, 2], "mhalf": [ROWS, 2],
            "wq": [128, 2, 2, 4, HEAD_PAD], "wk": [128, 2, 2, 4, HEAD_PAD], "wv": [128, 2, DIM],
            "wg": [128, 2, 3, HALF], "wp": [128, 2, DIM], "wgate1": [FIRST, EXPERTS], "wgate2": [REST, EXPERTS],
            "wsd": [ECHUNK, SCHUNKS, DIM],
            "bproj": [ROWS, DIM], "ebias": [ROWS, EXPERTS],
        }
        t = {k: ctx.enter_context(nc.sbuf_tensor(f"k_{k}", v, fp32)) for k, v in shapes.items()}
        for k, rows in (("ws1h", FIRST), ("ws1l", FIRST), ("ws2hl", 2 * REST)):
            t[k] = ctx.enter_context(nc.sbuf_tensor(f"k_{k}", [rows, 2, SHID], fp16))
        t["tri"] = ctx.enter_context(nc.sbuf_tensor("k_tri", [ROWS, ROWS], bf16))
        t["ones"] = ctx.enter_context(nc.sbuf_tensor("k_ones", [ROWS, ROWS], bf16))
        embed(nc, PS, t, x, cls_tok, z, pos_enc, w_qkv, w_g0, w_g1, w_proj, b_proj, Wg, e_bias, Wsg, Wsu, Wsd,
              hseq, xdisp, out)
        layer(nc, PS, t, cls_tok, hseq, xdisp, out)
        experts(nc, PS, t, Wgu, Wd, xdisp, out)


_INS = ["x", "cls_tok", "L0_tok_z", "L0_tok_pos_enc", "L0_attn_w_qkv", "L0_attn_w_g0", "L0_attn_w_g1",
        "L0_attn_w_proj", "L0_attn_b_proj", "L0_ffn_Wg", "L0_ffn_e_bias", "L0_ffn_W_gate_up", "L0_ffn_W_down",
        "L0_ffn_Wsg", "L0_ffn_Wsu", "L0_ffn_Wsd"]


def kernel(**inputs):
    import numpy as _np
    import concourse.bacc as _bacc
    from concourse import mybir as _mybir
    from concourse.bass_utils import run_bass_kernel_spmd as _run

    nc = _bacc.Bacc("TRN2", target_bir_lowering=False, num_devices=1)
    arrays, args = {}, []
    for name in _INS:
        a = _np.ascontiguousarray(inputs[name])
        if name == "cls_tok":
            a = a.reshape(1, DIM)
        arrays[f"in_{name}"] = a
        args.append(nc.dram_tensor(f"in_{name}", a.shape, _mybir.dt.from_np(a.dtype), kind="ExternalInput").ap())
    args.append(nc.dram_tensor("out_h", (NTOK + CAP, DIM), _mybir.dt.float32, kind="ExternalOutput").ap())
    program(nc, *args)
    r = _run(nc, [arrays], core_ids=[0])
    return r.results[0]["out_h"][:NTOK].reshape(IMAGES, TOKENS, DIM)
```
